# Optimizing a Trainium2 kernel written in Bass

```python
import numpy as np
import jax
import jax.numpy as jnp

def _softmax(x, axis=-1):
    return jax.nn.softmax(x, axis=axis)

def _gelu(x):
    return jax.nn.gelu(x, approximate=True)

def _silu(x):
    return jax.nn.silu(x)

def _sigmoid(x):
    return jax.nn.sigmoid(x)

def _layernorm(x, axis=-1, eps=1e-05):
    m = jnp.mean(x, axis=axis, keepdims=True)
    v = jnp.var(x, axis=axis, keepdims=True)
    return (x - m) / jnp.sqrt(v + eps)

def _scatter_add(tgt, idx, src, axis=0):
    return tgt.at[idx].add(src)

def _segment_sum(src, seg, n):
    return jax.ops.segment_sum(src, seg, n)
kernel_name = 'mk_seq_postln_d1_jaxref_r8_0f6d5a'

def setup_inputs(seed: int=0):
    np.random.seed(seed)
    _w = jnp.asarray

    def _L0_attn_setup():
        import jax, jax.numpy as jnp
        import numpy as np
        import math
        DIM = 512
        N_HEADS = 32
        N_KV_HEADS = 8
        HEAD_DIM = DIM // N_HEADS
        N_REP = N_HEADS // N_KV_HEADS
        ROPE_BASE = 10000.0

        def apply_rotary_emb(x):
            b, s, h, d = x.shape
            inv_freq = 1.0 / ROPE_BASE ** (jnp.arange(0, d, 2, dtype=jnp.float32) / d)
            pos = jnp.arange(s, dtype=jnp.float32)
            ang = pos[:, None] * inv_freq[None, :]
            cos = jnp.cos(ang)[None, :, None, :]
            sin = jnp.sin(ang)[None, :, None, :]
            xr = x.reshape(b, s, h, d // 2, 2)
            x0, x1 = (xr[..., 0], xr[..., 1])
            out = jnp.stack([x0 * cos - x1 * sin, x0 * sin + x1 * cos], axis=-1)
            return out.reshape(b, s, h, d)
        key = jax.random.key(seed)
        ks = jax.random.split(key, 5)
        sc = 1.0 / math.sqrt(DIM)
        return {'x': jax.random.normal(ks[0], (2, 256, DIM), dtype=jnp.float32), 'Wq': jax.random.normal(ks[1], (DIM, N_HEADS * HEAD_DIM), dtype=jnp.float32) * sc, 'Wk': jax.random.normal(ks[2], (DIM, N_KV_HEADS * HEAD_DIM), dtype=jnp.float32) * sc, 'Wv': jax.random.normal(ks[3], (DIM, N_KV_HEADS * HEAD_DIM), dtype=jnp.float32) * sc, 'Wo': jax.random.normal(ks[4], (N_HEADS * HEAD_DIM, DIM), dtype=jnp.float32) * sc}
    _L0_attn_in = _L0_attn_setup()

    def _L0_ffn_setup():
        import jax, jax.numpy as jnp
        import numpy as np
        HIDDEN = 512
        MOE_INTER = 128
        SHARED_INTER = 512
        NUM_EXPERTS = 16
        TOP_K = 2

        def _moe_forward(x, gate_w, w_gate_up, w_down, shared_w_gate_up, shared_w_down):
            orig_shape = x.shape
            x2 = x.reshape(-1, orig_shape[-1])
            gu_s = x2 @ shared_w_gate_up.T
            g_s, u_s = jnp.split(gu_s, 2, axis=-1)
            shared_out = jax.nn.silu(g_s) * u_s @ shared_w_down.T
            logits = x2 @ gate_w.T
            probs = jax.nn.softmax(logits, axis=-1)
            topk_vals, topk_idx = jax.lax.top_k(probs, TOP_K)
            topk_vals = topk_vals / jnp.sum(topk_vals, axis=-1, keepdims=True)
            combine = jnp.sum(jax.nn.one_hot(topk_idx, NUM_EXPERTS, dtype=x2.dtype) * topk_vals[..., None], axis=1)
            gu = jnp.einsum('th,eih->eti', x2, w_gate_up)
            g, u = jnp.split(gu, 2, axis=-1)
            act = jax.nn.silu(g) * u
            out_e = jnp.einsum('eti,ehi->eth', act, w_down)
            moe_out = jnp.einsum('eth,te->th', out_e, combine)
            return (moe_out + shared_out).reshape(orig_shape)
        key = jax.random.key(seed)
        ks = jax.random.split(key, 6)
        s = 0.02
        hidden_states = jax.random.normal(ks[0], (2, 256, HIDDEN), dtype=jnp.float32)
        gate_w = jax.random.normal(ks[1], (NUM_EXPERTS, HIDDEN), dtype=jnp.float32) * s
        w_gate_up = jax.random.normal(ks[2], (NUM_EXPERTS, 2 * MOE_INTER, HIDDEN), dtype=jnp.float32) * s
        w_down = jax.random.normal(ks[3], (NUM_EXPERTS, HIDDEN, MOE_INTER), dtype=jnp.float32) * s
        shared_w_gate_up = jax.random.normal(ks[4], (2 * SHARED_INTER, HIDDEN), dtype=jnp.float32) * s
        shared_w_down = jax.random.normal(ks[5], (HIDDEN, SHARED_INTER), dtype=jnp.float32) * s
        return {'hidden_states': hidden_states, 'gate_w': gate_w, 'w_gate_up': w_gate_up, 'w_down': w_down, 'shared_w_gate_up': shared_w_gate_up, 'shared_w_down': shared_w_down}
    _L0_ffn_in = _L0_ffn_setup()
    _d = {'L0_attn_x': _L0_attn_in['x'], 'L0_attn_Wq': _L0_attn_in['Wq'], 'L0_attn_Wk': _L0_attn_in['Wk'], 'L0_attn_Wv': _L0_attn_in['Wv'], 'L0_attn_Wo': _L0_attn_in['Wo'], 'L0_ffn_gate_w': _L0_ffn_in['gate_w'], 'L0_ffn_w_gate_up': _L0_ffn_in['w_gate_up'], 'L0_ffn_w_down': _L0_ffn_in['w_down'], 'L0_ffn_shared_w_gate_up': _L0_ffn_in['shared_w_gate_up'], 'L0_ffn_shared_w_down': _L0_ffn_in['shared_w_down']}
    _x0 = _d['L0_attn_x']
    _d['L0_attn_x'] = jax.random.normal(jax.random.fold_in(jax.random.key(seed), 1), (2, 1024, 512), dtype=_x0.dtype)
    del _x0
    return _d

def reference(L0_attn_x, L0_attn_Wq, L0_attn_Wk, L0_attn_Wv, L0_attn_Wo, L0_ffn_gate_w, L0_ffn_w_gate_up, L0_ffn_w_down, L0_ffn_shared_w_gate_up, L0_ffn_shared_w_down):

    def _L0_attn_ref(x, Wq, Wk, Wv, Wo):
        import jax, jax.numpy as jnp
        import numpy as np
        import math
        DIM = 512
        N_HEADS = 32
        N_KV_HEADS = 8
        HEAD_DIM = DIM // N_HEADS
        N_REP = N_HEADS // N_KV_HEADS
        ROPE_BASE = 10000.0

        def apply_rotary_emb(x):
            b, s, h, d = x.shape
            inv_freq = 1.0 / ROPE_BASE ** (jnp.arange(0, d, 2, dtype=jnp.float32) / d)
            pos = jnp.arange(s, dtype=jnp.float32)
            ang = pos[:, None] * inv_freq[None, :]
            cos = jnp.cos(ang)[None, :, None, :]
            sin = jnp.sin(ang)[None, :, None, :]
            xr = x.reshape(b, s, h, d // 2, 2)
            x0, x1 = (xr[..., 0], xr[..., 1])
            out = jnp.stack([x0 * cos - x1 * sin, x0 * sin + x1 * cos], axis=-1)
            return out.reshape(b, s, h, d)
        b, s, _ = x.shape
        xq = (x @ Wq).reshape(b, s, N_HEADS, HEAD_DIM)
        xk = (x @ Wk).reshape(b, s, N_KV_HEADS, HEAD_DIM)
        xv = (x @ Wv).reshape(b, s, N_KV_HEADS, HEAD_DIM)
        xq = apply_rotary_emb(xq)
        xk = apply_rotary_emb(xk)
        xk = jnp.repeat(xk, N_REP, axis=2)
        xv = jnp.repeat(xv, N_REP, axis=2)
        scores = jnp.einsum('bqhd,bkhd->bhqk', xq, xk) / math.sqrt(HEAD_DIM)
        causal = jnp.tril(jnp.ones((s, s), dtype=bool))
        scores = jnp.where(causal[None, None], scores, -jnp.inf)
        probs = jax.nn.softmax(scores.astype(jnp.float32), axis=-1).astype(xq.dtype)
        out = jnp.einsum('bhqk,bkhd->bqhd', probs, xv).reshape(b, s, N_HEADS * HEAD_DIM)
        return out @ Wo

    def _L0_ffn_ref(hidden_states, gate_w, w_gate_up, w_down, shared_w_gate_up, shared_w_down):
        import jax, jax.numpy as jnp
        import numpy as np
        HIDDEN = 512
        MOE_INTER = 128
        SHARED_INTER = 512
        NUM_EXPERTS = 16
        TOP_K = 2

        def _moe_forward(x, gate_w, w_gate_up, w_down, shared_w_gate_up, shared_w_down):
            orig_shape = x.shape
            x2 = x.reshape(-1, orig_shape[-1])
            gu_s = x2 @ shared_w_gate_up.T
            g_s, u_s = jnp.split(gu_s, 2, axis=-1)
            shared_out = jax.nn.silu(g_s) * u_s @ shared_w_down.T
            logits = x2 @ gate_w.T
            probs = jax.nn.softmax(logits, axis=-1)
            topk_vals, topk_idx = jax.lax.top_k(probs, TOP_K)
            topk_vals = topk_vals / jnp.sum(topk_vals, axis=-1, keepdims=True)
            combine = jnp.sum(jax.nn.one_hot(topk_idx, NUM_EXPERTS, dtype=x2.dtype) * topk_vals[..., None], axis=1)
            gu = jnp.einsum('th,eih->eti', x2, w_gate_up)
            g, u = jnp.split(gu, 2, axis=-1)
            act = jax.nn.silu(g) * u
            out_e = jnp.einsum('eti,ehi->eth', act, w_down)
            moe_out = jnp.einsum('eth,te->th', out_e, combine)
            return (moe_out + shared_out).reshape(orig_shape)
        return _moe_forward(hidden_states, gate_w, w_gate_up, w_down, shared_w_gate_up, shared_w_down)
    x = L0_attn_x
    x = _layernorm(x + _L0_attn_ref(x, L0_attn_Wq, L0_attn_Wk, L0_attn_Wv, L0_attn_Wo), axis=-1)
    x = _layernorm(x + _L0_ffn_ref(x, L0_ffn_gate_w, L0_ffn_w_gate_up, L0_ffn_w_down, L0_ffn_shared_w_gate_up, L0_ffn_shared_w_down), axis=-1)
    return x

_drawn_inputs = setup_inputs


def setup_inputs(seed=0):
    import zlib

    import numpy as np

    out = dict(_drawn_inputs(seed))
    spreads = {}
    factors = {'L0_ffn_gate_w': 3.447, 'L0_ffn_w_gate_up': 3.226, 'L0_ffn_w_down': 3.227}
    for name, (base, spread) in spreads.items():
        noise = np.random.default_rng([zlib.crc32(name.encode()), seed]).standard_normal(out[name].shape)
        drawn = base * np.exp(spread * noise) if base else spread * noise
        out[name] = jnp.asarray(drawn.astype(out[name].dtype))
    for name, factor in factors.items():
        out[name] = (out[name] * factor).astype(out[name].dtype)
    return out
```

```python
from contextlib import ExitStack

import concourse.bass as bass
from concourse import mybir

F32 = mybir.dt.float32
F32R = mybir.dt.float32r
BF16 = mybir.dt.bfloat16
ALU = mybir.AluOpType
ACT = mybir.ActivationFunctionType
AX = mybir.AxisListType

P = 128
BATCH, SEQ, DIM = 2, 1024, 512
TOKENS = BATCH * SEQ
HEADS, KV_HEADS, HEAD = 32, 8, 16
REP = HEADS // KV_HEADS
PAIRS = HEAD // 2
KC = DIM // P
CHUNK = 512
CHUNKS = TOKENS // CHUNK
KT = SEQ // P
GROUPS = BATCH * KV_HEADS
SETS = HEADS * PAIRS // P
SET_HEADS = P // PAIRS
COLS = 7
SCALE = HEAD ** -0.5
VW = 32
EXPERTS, INTER = 16, 128
SHARED = 512 // INTER
LARGEST = 3.4028234663852886e38
DMA = 16


def prime(eng, *sems, by=1):
    for s in sems:
        eng.sem_inc(s, by)


def project_qkv(nc, x_t, w_qkv, cos, sin, ident_dram, q_s, k_s, m_s, values, ident, bound):
    with ExitStack() as c:
        sb = lambda n, s, d=F32: c.enter_context(nc.sbuf_tensor(n, s, d))
        sem = lambda n: c.enter_context(nc.semaphore(n))
        w = sb("w", [P, KC, COLS * P])
        w_hi = sb("w_hi", [P, KC, COLS * P], F32R)
        w_lo = sb("w_lo", [P, KC, COLS * P], F32R)
        xs = [sb(f"x{n}", [P, KC, CHUNK]) for n in range(2)]
        x_hi = sb("x_hi", [P, KC, TOKENS], F32R)
        x_lo = sb("x_lo", [P, KC, TOKENS], F32R)
        cos_s = sb("cos_s", [P, SEQ])
        sin_s = sb("sin_s", [P, SEQ])
        prod = sb("prod", [P, 4, CHUNK])
        rot = sb("rot", [P, 2, CHUNK])
        parts = sb("parts", [P, SETS + 1, 2, 2, CHUNK], F32R)
        v_t = sb("v_t", [P, TOKENS])
        sq = sb("sq", [P, 2, CHUNK], BF16)
        sum_heads = sb("sum_heads", [P, 32], BF16)
        norm = sb("norm", [P, CHUNK])
        norm_hi = sb("norm_hi", [P, CHUNK], F32R)
        norm_lo = sb("norm_lo", [P, CHUNK], F32R)
        k_max = sb("k_max", [P, CHUNKS])
        k_top = sb("k_top", [P, 1])
        k_one = sb("k_one", [1, 1])
        ones_row = sb("ones_row", [1, P])
        acc = [c.enter_context(nc.psum_tensor(f"acc{j}", [P, CHUNK], F32)) for j in range(COLS)]
        small = c.enter_context(nc.psum_tensor("small", [P, CHUNK], F32))

        w_in, x_in, table_in, ident_in = [sem(f"w_in{j}") for j in range(SETS + 2)], [sem("x_in0"), sem("x_in1")], sem("table_in"), sem("ident_in")
        w_high, w_split, x_high, x_split = sem("w_high"), sem("w_split"), sem("x_high"), sem("x_split")
        projected = sem("projected")
        products, turned = sem("products"), sem("turned")
        high, low, stored = sem("high"), sem("low"), sem("stored")
        squared, summed, normed = sem("squared"), sem("summed"), sem("normed")
        norm_high, norm_low, norm_stored = sem("norm_high"), sem("norm_low"), sem("norm_stored")
        v_copied, v_turned, v_kept = sem("v_copied"), sem("v_turned"), sem("v_kept")
        made = sem("made")
        top_ready, top_turned, top_one, top_spread, top_done = [sem(f"top{j}") for j in range(5)]
        block = c.enter_context(nc.Block())
        N_SETS = SETS + 1
        W_PARTS = [(2 * P * s, min(2 * P * (s + 1), COLS * P)) for s in range(N_SETS + 1)]

        @block.sync
        def _(sp):
            prime(sp, stored, norm_stored)

            def load_w(i):
                a, b = W_PARTS[i]
                sp.dma_start(w[:, :, a:b], w_qkv.rearrange("(c p) n -> p c n", p=P)[:, :, a:b]).then_inc(w_in[i], DMA)

            load_w(0)
            for n in range(CHUNKS):
                if n >= 2:
                    sp.wait_ge(x_split, n - 1)
                sp.dma_start(xs[n % 2][:], x_t[:, n * CHUNK:(n + 1) * CHUNK].rearrange("(c p) n -> p c n", p=P)
                             ).then_inc(x_in[n % 2], DMA)
                if n == 0:
                    for i in range(1, len(W_PARTS)):
                        load_w(i)
                    sp.dma_start(cos_s[:], cos).then_inc(table_in, DMA)
                    sp.dma_start(sin_s[:], sin).then_inc(table_in, DMA)
                    sp.dma_start(ident[:], ident_dram).then_inc(ident_in, DMA)
            with sp.Fori(0, CHUNKS) as n:
                col = n * CHUNK
                for s in range(N_SETS):
                    rows = P // 2 if s == 0 else P
                    dst = k_s if s == 0 else q_s[(s - 1) * SET_HEADS:s * SET_HEADS]
                    for half in range(2):
                        for part in range(2):
                            if half == 0 and part == 0:
                                sp.wait_ge(low, (n * N_SETS + s + 1) * 2 + 1)
                            sp.dma_start(dst[:, part, half * PAIRS:(half + 1) * PAIRS, bass.ds(col, CHUNK)],
                                         parts[0:rows, s, half, part, :].bitcast(F32)).then_inc(stored, DMA)
                sp.wait_ge(norm_low, n + 2)
                for s in range(SETS):
                    for part, src in enumerate((norm_hi, norm_lo)):
                        at = 32 * (s + 1)
                        sp.dma_start(m_s[s * SET_HEADS:(s + 1) * SET_HEADS, part, bass.ds(col, CHUNK)],
                                     src[at:at + SET_HEADS, :].bitcast(F32)).then_inc(norm_stored, DMA)
            sp.wait_ge(stored, CHUNKS * N_SETS * 4 * DMA + 1)
            sp.wait_ge(norm_stored, CHUNKS * SETS * 2 * DMA + 1)

        @block.scalar
        def _(act):
            prime(act, squared, high, v_copied, normed, norm_high)

            def w_part(i):
                a, b = W_PARTS[i]
                act.wait_ge(w_in[i], DMA)
                nc.scalar.activation(w_hi[:, :, a:b], w[:, :, a:b], ACT.Copy).then_inc(w_high, 1)

            w_part(0)
            for n in range(CHUNKS):
                act.wait_ge(x_in[n % 2], DMA * (n // 2 + 1))
                nc.scalar.activation(x_hi[:, :, n * CHUNK:(n + 1) * CHUNK], xs[n % 2][:], ACT.Copy).then_inc(x_high, 1)
                if n == 0:
                    for i in range(1, len(W_PARTS)):
                        w_part(i)
            with act.Fori(0, CHUNKS) as n:
                for s in range(N_SETS):
                    act.wait_ge(projected, n * COLS + 2 * s + 3)
                    act.wait_ge(summed, n * N_SETS + s + 1)
                    for half in range(2):
                        last = nc.scalar.activation(sq[:, half, :], acc[2 * s + half][:], ACT.Square)
                    last.then_inc(squared, 1)
                    if s == N_SETS - 1:
                        act.wait_ge(projected, n * COLS + COLS + 1)
                        nc.scalar.activation(v_t[:, bass.ds(n * CHUNK, CHUNK)], acc[COLS - 1][:], ACT.Copy).then_inc(v_copied, 1)
                    act.wait_ge(turned, n * N_SETS + s + 2)
                    if s == 0:
                        act.wait_ge(stored, n * (N_SETS * 4 * DMA) + 1)
                    nc.scalar.activation(parts[:, s, :, 0, :], rot[:], ACT.Copy).then_inc(high, 1)
                act.wait_ge(summed, n * N_SETS + N_SETS + 1)
                act.wait_ge(norm_low, n + 1)
                nc.scalar.activation(norm[0:96], small[0:96], ACT.Copy, scale=-0.5).then_inc(normed, 1)
                act.wait_ge(normed, n + 2)
                act.wait_ge(norm_stored, n * (SETS * 2 * DMA) + 1)
                nc.scalar.activation(norm_hi[0:96], norm[0:96], ACT.Copy).then_inc(norm_high, 1)
            for n in range(CHUNKS):
                act.wait_ge(v_turned, n + 1)
                nc.scalar.activation(values[:, n * (CHUNK // P):(n + 1) * (CHUNK // P), :],
                                     acc[n][:].rearrange("p (t d) -> p t d", d=P), ACT.Copy).then_inc(v_kept, 1)
            act.wait_ge(v_kept, CHUNKS)

        @block.vector
        def _(dve):
            nc.vector.memset(ones_row[:], 1.0).then_inc(made, 1)
            for _ in range(N_SETS - 1):
                prime(dve, products)
            prime(dve, products, turned, low, norm_low)

            def w_part(i):
                a, b = W_PARTS[i]
                dve.wait_ge(w_high, i + 1)
                nc.vector.tensor_tensor(w_lo[:, :, a:b], w[:, :, a:b], w_hi[:, :, a:b], ALU.subtract).then_inc(w_split, 1)

            w_part(0)
            dve.wait_ge(x_high, 1)
            nc.vector.tensor_tensor(x_lo[:, :, 0:CHUNK], xs[0][:], x_hi[:, :, 0:CHUNK], ALU.subtract).then_inc(x_split, 1)
            for i in range(1, len(W_PARTS)):
                w_part(i)
            dve.wait_ge(table_in, 2 * DMA)
            with dve.Fori(0, BATCH) as b:
                for half_seq in range(SEQ // CHUNK):
                    n = b * (SEQ // CHUNK) + half_seq
                    co = cos_s[:, half_seq * CHUNK:(half_seq + 1) * CHUNK]
                    si = sin_s[:, half_seq * CHUNK:(half_seq + 1) * CHUNK]
                    for s in range(N_SETS):
                        even, odd = acc[2 * s], acc[2 * s + 1]
                        dve.wait_ge(squared, n * N_SETS + s + 2)
                        dve.wait_ge(turned, n * N_SETS + s + 1)
                        nc.vector.tensor_tensor(prod[:, 0, :], even[:], co, ALU.mult)
                        nc.vector.tensor_tensor(prod[:, 1, :], odd[:], si, ALU.mult)
                        nc.vector.tensor_tensor(prod[:, 2, :], even[:], si, ALU.mult)
                        nc.vector.tensor_tensor(prod[:, 3, :], odd[:], co, ALU.mult).then_inc(products, 1)
                        dve.wait_ge(products, (n + 1) * N_SETS + s + 1)
                        dve.wait_ge(high, n * N_SETS + s + 1)
                        dve.wait_ge(low, (n * N_SETS + s) * 2 + 1)
                        nc.vector.tensor_tensor(rot[:, 0, :], prod[:, 0, :], prod[:, 1, :], ALU.subtract)
                        nc.vector.tensor_tensor(rot[:, 1, :], prod[:, 2, :], prod[:, 3, :], ALU.add).then_inc(turned, 1)
                        dve.wait_ge(high, n * N_SETS + s + 2)
                        for half in range(2):
                            nc.vector.tensor_tensor(parts[:, s, half, 1, :], rot[:, half, :], parts[:, s, half, 0, :],
                                                    ALU.subtract).then_inc(low, 1)
                    dve.wait_ge(norm_high, n + 2)
                    nc.vector.tensor_tensor(norm_lo[0:96], norm[0:96], norm_hi[0:96], ALU.subtract)
                    nc.vector.tensor_reduce(k_max[0:8, bass.ds(n, 1)], norm[0:8, :], AX.X, ALU.min).then_inc(norm_low, 1)
            dve.wait_ge(norm_low, CHUNKS + 1)
            nc.vector.tensor_reduce(k_top[0:8, :], k_max[0:8, :], AX.X, ALU.min).then_inc(top_ready, 1)
            dve.wait_ge(top_turned, 1)
            nc.vector.tensor_reduce(k_one[:], small[0:1, 0:8], AX.X, ALU.min).then_inc(top_one, 1)
            dve.wait_ge(top_spread, 1)
            nc.vector.tensor_copy(bound[:], small[:, 8:9]).then_inc(top_done, 1)
            dve.wait_ge(top_done, 1)

        @block.gpsimd
        def _(pool):
            nc.gpsimd.memset(sum_heads[:], 1.0).then_inc(made, 1)
            pool.wait_ge(made, 2)
            nc.gpsimd.affine_select(out=sum_heads[:], in_=sum_heads[:], compare_op=ALU.is_ge, fill=0.0, base=0,
                                    pattern=[[-PAIRS, 32]], channel_multiplier=1).then_inc(made, 1)
            pool.wait_ge(made, 3)
            nc.gpsimd.affine_select(out=sum_heads[:], in_=sum_heads[:], compare_op=ALU.is_ge, fill=0.0, base=PAIRS - 1,
                                    pattern=[[PAIRS, 32]], channel_multiplier=-1).then_inc(made, 1)
            pool.wait_ge(made, 4)
            for n in range(1, CHUNKS):
                cols = slice(n * CHUNK, (n + 1) * CHUNK)
                pool.wait_ge(x_high, n + 1)
                pool.wait_ge(x_split, n)
                nc.gpsimd.tensor_tensor(x_lo[:, :, cols], xs[n % 2][:], x_hi[:, :, cols], ALU.subtract).then_inc(x_split, 1)

        @block.tensor
        def _(pe):
            prime(pe, projected, summed)
            pe.wait_ge(made, 4)
            pe.wait_ge(ident_in, DMA)

            with pe.Fori(0, CHUNKS) as n:
                pe.wait_ge(x_split, n + 1)
                xh = x_hi[:, :, bass.ds(n * CHUNK, CHUNK)]
                xl = x_lo[:, :, bass.ds(n * CHUNK, CHUNK)]

                def norms(s):
                    pe.wait_ge(squared, n * N_SETS + s + 2)
                    if s == 0:
                        pe.wait_ge(normed, n + 1)
                    for half in range(2):
                        last = nc.tensor.matmul(small[32 * s:32 * s + 32, :], sum_heads[:], sq[:, half, :],
                                                start=half == 0, stop=half == 1)
                    last.then_inc(summed, 1)

                for j in range(COLS):
                    if j < 2 * N_SETS:
                        if j % 2 == 0:
                            pe.wait_ge(products, n * N_SETS + j // 2 + 1)
                            pe.wait_ge(w_split, j // 2 + 1)
                    else:
                        pe.wait_ge(v_copied, n + 1)
                        pe.wait_ge(w_split, len(W_PARTS))
                    terms = [(k, a, b) for k in range(KC) for a, b in ((w_hi, xh), (w_hi, xl), (w_lo, xh))]
                    for i, (k, a, b) in enumerate(terms):
                        last = nc.tensor.matmul(acc[j][:], a[:, k, j * P:(j + 1) * P], b[:, k, :],
                                                start=i == 0, stop=i == len(terms) - 1)
                    last.then_inc(projected, 1)
                    if j in (3, 5):
                        norms((j - 3) // 2)
                norms(N_SETS - 1)
            pe.wait_ge(v_copied, CHUNKS + 1)
            pe.wait_ge(products, (CHUNKS + 1) * N_SETS)
            for n in range(CHUNKS):
                for t in range(CHUNK // P):
                    at = n * CHUNK + t * P
                    last = nc.tensor.transpose(acc[n][:, t * P:(t + 1) * P], v_t[:, at:at + P], ident[:])
                last.then_inc(v_turned, 1)
            pe.wait_ge(top_ready, 1)
            nc.tensor.transpose(small[0:1, 0:8], k_top[0:8, :], ident[0:8, 0:8]).then_inc(top_turned, 1)
            pe.wait_ge(top_one, 1)
            nc.tensor.matmul(small[:, 8:9], ones_row[:], k_one[:], start=True, stop=True).then_inc(top_spread, 1)


def attend(nc, q_s, k_s, m_s, values, bound, o_s, d_s):
    with ExitStack() as c:
        sb = lambda n, s, d=F32: c.enter_context(nc.sbuf_tensor(n, s, d))
        sem = lambda n: c.enter_context(nc.semaphore(n))
        ROWS = 4 * HEAD + 3
        SLOTS = 4
        q_st = [sb(f"q_st{p}", [P, REP, SEQ], F32R) for p in range(2)]
        k_st = [sb(f"k_st{p}", [P, SEQ], F32R) for p in range(2)]
        v_st = [sb(f"v_st{p}", [P, KT, VW]) for p in range(2)]
        prob = [sb(f"prob{j}", [P, REP, SEQ]) for j in range(SLOTS)]
        o_t = [sb(f"o_t{p}", [P, SEQ]) for p in range(2)]
        cap = sb("cap", [P, P])
        ring = [c.enter_context(nc.psum_tensor(f"ring{j}", [P, SEQ], F32)) for j in range(3)]
        out_ps = c.enter_context(nc.psum_tensor("out_ps", [P, SEQ], F32))
        loaded = [sem("loaded0"), sem("loaded1")]
        LOADS, STORES = 7, 2 * REP
        cap_made, blank, zero_made, ones_made, v_blank = sem("cap_made"), sem("blank"), sem("zero_made"), sem("ones_made"), sem("v_blank")
        scored, expd, masked = sem("scored"), sem("expd"), sem("masked")
        weighed = sem("weighed")
        v_staged, out_copied, out_stored = sem("v_staged"), sem("out_copied"), [sem("out_stored0"), sem("out_stored1")]
        UNIT = []
        for kt in range(KT):
            width = SEQ - kt * P
            heads = 1 if width > CHUNK else 2 if width > CHUNK // 2 else REP
            UNIT += [(kt, h, heads) for h in range(0, REP, heads)]
        UNITS = len(UNIT)
        LAST = [max(u for u in range(UNITS) if UNIT[u][0] == kt) for kt in range(KT)]
        AHEAD = 6
        HALF = [(0, CHUNK), (CHUNK, SEQ)]
        LAST_IN_SLOT = [max(v for v in range(-UNITS, u) if v % UNITS % 3 == u % 3) for u in range(UNITS)]

        def halves(kt):
            return [(max(a, kt * P), b, j) for j, (a, b) in enumerate(HALF) if kt * P < b]

        def unit_view(tile, kt, heads):
            width = SEQ - kt * P
            if heads == 1:
                return tile[:, kt * P:SEQ].unsqueeze(1)
            pitch = CHUNK if heads == 2 else width
            return tile[:, 0:heads * pitch].rearrange("p (h w) -> p h w", h=heads)[:, :, 0:width]

        weigh_after = {}
        todo = [(kt, i) for kt in range(KT) for i in range(len(halves(kt)))]
        credit = 0
        for v in range(AHEAD, UNITS + AHEAD):
            kt, _, heads = UNIT[v % UNITS]
            credit = min(credit + heads * (SEQ - kt * P) * (0.83 - 0.42), 1600)
            weigh_after[v] = []
            while todo and LAST[todo[0][0]] <= v - 2:
                a, b, _ = halves(todo[0][0])[todo[0][1]]
                cost = (b - a) * 1.67
                if credit < cost / 2 and v < UNITS + AHEAD - 1:
                    break
                credit -= cost
                weigh_after[v].append(todo.pop(0))
        assert not todo

        block = c.enter_context(nc.Block())

        @block.sync
        def _(sp):
            def load(parity, b, kv):
                q, k, st = q_st[parity], k_st[parity], loaded[parity]
                head = kv * REP
                cols = bass.ds(b * SEQ, SEQ)
                for r in range(2):
                    sp.dma_start(q[32 * r:32 * r + 32, :, :].bitcast(F32),
                                 q_s[bass.ds(head, REP), :, :, cols].rearrange("h a d t -> (a d) h t")).then_inc(st, DMA)
                    for s in range(2):
                        at = 32 * r + HEAD * s
                        sp.dma_start(k[at:at + HEAD, :].bitcast(F32), k_s[bass.ds(kv, 1), r, :, cols].rearrange(
                            "k d t -> (k d) t")).then_inc(st, DMA)
                sp.dma_start(q[4 * HEAD:ROWS - 1, :, :].bitcast(F32),
                             m_s[bass.ds(head, REP), :, cols].rearrange("h a t -> a h t")).then_inc(st, DMA)

            sp.wait_ge(ones_made, 4)
            load(0, 0, 0)
            load(1, 0, 1)
            for b in range(BATCH):
                with sp.Fori(0, KV_HEADS // 2) as i:
                    for parity in range(2):
                        g = b * KV_HEADS + i * 2 + parity
                        sp.wait_ge(scored, (g + 1) * UNITS)
                        nxt = i * 2 + 2 + parity
                        if b + 1 < BATCH:
                            load(parity, b + nxt // KV_HEADS, nxt % KV_HEADS)
                        else:
                            load(parity, b, nxt % KV_HEADS)
                        sp.wait_ge(out_copied, g + 2)
                        for h in range(REP):
                            head = (i * 2 + parity) * REP + h
                            sp.dma_start(o_s[bass.ds(head, 1), :, b * SEQ:(b + 1) * SEQ].rearrange("h d t -> (h d) t"),
                                         o_t[parity][32 * h:32 * h + HEAD, :]).then_inc(out_stored[parity], DMA)
                            sp.dma_start(d_s[bass.ds(head, 1), b * SEQ:(b + 1) * SEQ],
                                         o_t[parity][32 * h + HEAD:32 * h + HEAD + 1, :]).then_inc(out_stored[parity], DMA)
            for parity in range(2):
                sp.wait_ge(loaded[parity], (GROUPS // 2 + 1) * LOADS * DMA)
                sp.wait_ge(out_stored[parity], GROUPS // 2 * STORES * DMA + 1)

        @block.scalar
        def _(act):
            def exp_unit(g, u, first=False):
                kt, h, heads = UNIT[u]
                act.wait_ge(scored, g * UNITS + u + 1)
                if h == 0 and not (first and kt < SLOTS):
                    act.wait_ge(weighed, g * KT + kt - SLOTS + 2)
                nc.scalar.activation(prob[kt % SLOTS][:, h:h + heads, kt * P:SEQ], unit_view(ring[u % 3], kt, heads),
                                     ACT.Exp, scale=SCALE).then_inc(expd, 1)

            act.wait_ge(ones_made, 4)
            for u in range(UNITS):
                exp_unit(0, u, first=True)
            with act.Fori(1, GROUPS) as g:
                for u in range(UNITS):
                    exp_unit(g, u)
            for u in range(AHEAD):
                exp_unit(GROUPS, u)

        @block.gpsimd
        def _(pool):
            def stage_v(parity, b, kv):
                nc.gpsimd.tensor_copy(v_st[parity][:, :, 0:HEAD],
                                      values[:, bass.ds(b * KT, KT), bass.ds(kv * HEAD, HEAD)]).then_inc(v_staged, 1)

            nc.gpsimd.memset(cap[:], LARGEST).then_inc(cap_made, 1)
            pool.wait_ge(cap_made, 1)
            nc.gpsimd.affine_select(out=cap[:], in_=cap[:], compare_op=ALU.is_ge, fill=0.0, base=0,
                                    pattern=[[1, P]], channel_multiplier=-1).then_inc(cap_made, 1)
            pool.wait_ge(cap_made, 2)
            pool.wait_ge(v_blank, 4)
            stage_v(0, 0, 0)
            with pool.Fori(0, GROUPS // 2) as i:
                for parity in range(2):
                    g = i * 2 + parity
                    pool.wait_ge(weighed, g * KT + 1)
                    pool.wait_ge(v_staged, g + 1)
                    nxt = (g + 1) % GROUPS
                    stage_v(1 - parity, nxt // KV_HEADS, nxt % KV_HEADS)

        @block.vector
        def _(dve):
            def mask_unit(g, u):
                kt, h, heads = UNIT[u]
                diag = prob[kt % SLOTS][:, h:h + heads, kt * P:(kt + 1) * P]
                dve.wait_ge(expd, g * UNITS + u + 1)
                nc.vector.tensor_tensor(diag, diag, cap[:].unsqueeze(1).to_broadcast([P, heads, P]),
                                        ALU.min).then_inc(masked, 1)

            prime(dve, out_copied, *out_stored)
            nc.vector.memset(prob[0][4 * HEAD:ROWS, :, :], 0.0).then_inc(zero_made, 1)
            dve.wait_ge(zero_made, 1)
            for p in range(2):
                nc.vector.memset(v_st[p][:], 0.0).then_inc(v_blank, 1)
                nc.vector.memset(k_st[p][4 * HEAD:P, :].bitcast(F32), 0.0).then_inc(blank, 1)
                nc.vector.memset(q_st[p][4 * HEAD:P, :, :].bitcast(F32), 0.0).then_inc(blank, 1)
                dve.wait_ge(blank, 2 * p + 2)
                nc.vector.memset(k_st[p][4 * HEAD:ROWS, :].bitcast(F32), 1.0).then_inc(ones_made, 1)
                nc.vector.tensor_scalar(q_st[p][4 * HEAD:ROWS, :, :], prob[0][4 * HEAD:ROWS, :, :], 0.0,
                                        bound[4 * HEAD:ROWS, 0:1], ALU.mult, ALU.add).then_inc(ones_made, 1)
            dve.wait_ge(v_blank, 2)
            for p in range(2):
                nc.vector.memset(v_st[p][:, :, HEAD:HEAD + 1], 1.0).then_inc(v_blank, 1)
            dve.wait_ge(cap_made, 2)
            for u in range(AHEAD):
                mask_unit(0, u)
            with dve.Fori(0, GROUPS // 2) as i:
                for parity in range(2):
                    g = i * 2 + parity
                    for u in range(AHEAD, UNITS + AHEAD):
                        if u == UNITS + AHEAD - 1:
                            dve.wait_ge(weighed, (g + 1) * KT + 1)
                            dve.wait_ge(out_stored[parity], i * (STORES * DMA) + 1)
                            nc.vector.tensor_copy(o_t[parity][:], out_ps[:]).then_inc(out_copied, 1)
                        mask_unit(g + u // UNITS, u % UNITS)

        @block.tensor
        def _(pe):
            def score(parity, u):
                kt, h0, heads = UNIT[u]
                view = unit_view(ring[u % 3], kt, heads)
                for h in range(heads):
                    for a, b, _ in halves(kt):
                        last = nc.tensor.matmul(view[:, h, a - kt * P:b - kt * P],
                                                k_st[parity][:, kt * P:(kt + 1) * P],
                                                q_st[parity][:, h0 + h, a:b], start=True, stop=True)
                last.then_inc(scored, 1)

            def weigh(parity, g, kt, half):
                a, b, bank = halves(kt)[half]
                if half == 0:
                    pe.wait_ge(masked, g * UNITS + LAST[kt] + 1)
                if kt == 0 and half == 0:
                    pe.wait_ge(v_staged, g + 1)
                    pe.wait_ge(out_copied, g + 1)
                last_of_bank = (kt + 1) * P == HALF[bank][1]
                for h in range(REP):
                    last = nc.tensor.matmul(out_ps[32 * h:32 * h + VW, a:b], v_st[parity][:, kt, :],
                                            prob[kt % SLOTS][:, h, a:b], start=kt == 0, stop=last_of_bank)
                if half == len(halves(kt)) - 1:
                    last.then_inc(weighed, 1)

            prime(pe, weighed)
            pe.wait_ge(ones_made, 4)
            pe.wait_ge(v_blank, 4)
            pe.wait_ge(loaded[0], LOADS * DMA)
            for u in range(AHEAD):
                if u >= 3:
                    pe.wait_ge(expd, u - 2)
                score(0, u)
            with pe.Fori(0, GROUPS // 2) as i:
                for parity in range(2):
                    g = i * 2 + parity
                    for u in range(AHEAD, UNITS + AHEAD):
                        nxt, v = divmod(u, UNITS)
                        pe.wait_ge(expd, (g + nxt) * UNITS + LAST_IN_SLOT[v] + 1)
                        if u == UNITS:
                            pe.wait_ge(loaded[1 - parity], (i + 1 + parity) * (LOADS * DMA))
                        score(parity ^ nxt, v)
                        for kt, half in weigh_after[u]:
                            weigh(parity, g, kt, half)


def project_out(nc, x, w_o, w_gate, ident, o_s, d_s, r_s, c_s, rows, t_hi, t_lo):
    with ExitStack() as c:
        sb = lambda n, s, d=F32: c.enter_context(nc.sbuf_tensor(f"po_{n}", s, d))
        sem = lambda n: c.enter_context(nc.semaphore(f"po_{n}"))
        ps = lambda n: c.enter_context(nc.psum_tensor(f"po_{n}", [P, CHUNK], F32))
        TILES = CHUNK // P
        wo, wo_hi, wo_lo = sb("wo", [P, KC, DIM]), sb("wo_hi", [P, KC, DIM], F32R), sb("wo_lo", [P, KC, DIM], F32R)
        wg, wg_hi, wg_lo = sb("wg", [P, KC, P]), sb("wg_hi", [P, KC, P], F32R), sb("wg_lo", [P, KC, P], F32R)
        den = sb("den", [P, HEADS * TOKENS // P])
        o_c = [sb(f"o_c{p}", [P, KC, CHUNK]) for p in range(2)]
        r_c = [sb(f"r_c{p}", [P, KC, CHUNK]) for p in range(2)]
        a_hi = [sb(f"a_hi{p}", [P, KC, CHUNK], F32R) for p in range(2)]
        a_lo = [sb(f"a_lo{p}", [P, KC, CHUNK], F32R) for p in range(2)]
        fresh = sb("fresh", [P, TILES, DIM])
        eps = sb("eps", [P, 1])
        stats = sb("stats", [P, TILES, 6])
        moments = sb("moments", [P, TILES, 2])
        spread = sb("spread", [P, TILES])
        scale = sb("scale", [P, TILES])
        logit_t = sb("logit_t", [P, CHUNK])
        logits = sb("logits", [P, TOKENS // P, EXPERTS])
        shape = [P, TOKENS // P, EXPERTS]
        rank = sb("rank", shape)
        SIZE = TOKENS // P * EXPERTS
        spare = o_c[0][:].rearrange("p c n -> p (c n)")
        eq, cand, first, second = [spare[:, j * SIZE:(j + 1) * SIZE].rearrange("p (t e) -> p t e", e=EXPERTS) for j in range(4)]
        weight = spare[:, 4 * SIZE:5 * SIZE]
        top, pick, low_top, total, inv_total, w_low = [sb(n, [P, TOKENS // P]) for n in ("top", "pick", "low_top", "total", "inv_total", "w_low")]
        weight_t = sb("weight_t", [P, 2, P])
        ones = sb("ones", [SHARED * TOKENS // P, P])
        wo_ps = [ps(f"wo_ps{t}") for t in range(TILES)]
        turn_ps = [ps(f"turn_ps{j}") for j in range(2)]
        logit_ps, back_ps = ps("logit_ps"), ps("back_ps")

        wo_in, wg_in, den_in, inv_out = sem("wo_in"), sem("wg_in"), sem("den_in"), sem("inv_out")
        o_in = [sem(f"o_in{p}") for p in range(2)]
        r_in = [sem(f"r_in{p}") for p in range(2)]
        x_in = [sem(f"x_in{p}") for p in range(2)]
        inverted, eps_made, ones_made, ranked = sem("inverted"), sem("eps_made"), sem("ones_made"), sem("ranked")
        w_high, w_split = sem("w_high"), sem("w_split")
        divided, a_high, a_split = sem("divided"), sem("a_high"), sem("a_split")
        projected, added, counted, averaged, rooted, scaled, normed = [
            sem(n) for n in ("projected", "added", "counted", "averaged", "rooted", "scaled", "normed")]
        turned, turned_high, turned_low = sem("turned"), sem("turned_high"), sem("turned_low")
        gated, logit_kept, logit_back, logit_done = sem("gated"), sem("logit_kept"), sem("logit_back"), sem("logit_done")
        chosen, lowered, exped = sem("chosen"), sem("lowered"), sem("exped")
        weight_turned, weight_kept, weight_out, ones_out = sem("weight_turned"), sem("weight_kept"), sem("weight_out"), sem("ones_out")
        block = c.enter_context(nc.Block())

        @block.sync
        def _(sp):
            prime(sp, a_split, by=2)
            prime(sp, added, by=TILES + 1)
            sp.dma_start(den[:], d_s.rearrange("h (a b) -> (h a) b", b=den.shape[1])).then_inc(den_in, DMA)
            sp.dma_start(wo[:], w_o.rearrange("(c p) n -> p c n", p=P)).then_inc(wo_in, DMA)
            sp.dma_start(wg[:], w_gate.rearrange("(c p) n -> p c n", p=P)).then_inc(wg_in, DMA)
            sp.wait_ge(inverted, 1)
            sp.dma_start(r_s.rearrange("h (a b) -> (h a) b", b=den.shape[1]), den[:]).then_inc(inv_out, DMA)
            sp.wait_ge(inv_out, DMA)
            sp.wait_ge(ones_made, 1)
            sp.dma_start(c_s[0:SHARED, :].rearrange("e (a b) -> (e a) b", b=P), ones[:]).then_inc(ones_out, DMA)
            with sp.Fori(0, CHUNKS // 2) as i:
                for p in range(2):
                    n = i * 2 + p
                    cols = bass.ds(n * CHUNK, CHUNK)
                    sp.wait_ge(a_split, n + 1)
                    sp.dma_start(o_c[p][:], o_s.rearrange("(c h) d t -> (h d) c t", c=KC)[:, :, cols]).then_inc(o_in[p], DMA)
                    for k in range(KC):
                        heads = P // HEAD
                        sp.dma_start(r_c[p][:, k, :], r_s[k * heads:(k + 1) * heads, cols].unsqueeze(1).to_broadcast(
                            [heads, HEAD, CHUNK])).then_inc(r_in[p], DMA)
                    sp.wait_ge(added, n * TILES + 1)
                    sp.dma_start(rows[:, bass.ds(n * TILES, TILES), :], x[cols, :].rearrange("(t p) d -> p t d", p=P)
                                 ).then_inc(x_in[p], DMA)
            sp.wait_ge(weight_kept, 2)
            for half in range(2):
                for t in range(TOKENS // P // 2):
                    tile = half * (TOKENS // P // 2) + t
                    sp.dma_start(c_s[SHARED:SHARED + EXPERTS, tile * P:(tile + 1) * P],
                                 weight_t[t * EXPERTS:(t + 1) * EXPERTS, half, :]).then_inc(weight_out, DMA)
            sp.wait_ge(weight_out, TOKENS // P * DMA)
            sp.wait_ge(ones_out, DMA)

        @block.gpsimd
        def _(pool):
            nc.gpsimd.memset(ones[:], 1.0).then_inc(ones_made, 1)
            nc.gpsimd.iota(rank[:], pattern=[[0, TOKENS // P], [-1, EXPERTS]], base=EXPERTS, channel_multiplier=0,
                           allow_small_or_imprecise_dtypes=True).then_inc(ranked, 1)
            with pool.Fori(0, CHUNKS // 2) as i:
                for p in range(2):
                    n = i * 2 + p
                    pool.wait_ge(o_in[p], (i + 1) * DMA)
                    pool.wait_ge(r_in[p], (i + 1) * (KC * DMA))
                    nc.gpsimd.tensor_tensor(o_c[p][:], o_c[p][:], r_c[p][:], ALU.mult).then_inc(divided, 1)

        @block.scalar
        def _(act):
            prime(act, logit_kept)
            act.wait_ge(wo_in, DMA)
            nc.scalar.activation(wo_hi[:], wo[:], ACT.Copy).then_inc(w_high, 1)
            act.wait_ge(wg_in, DMA)
            nc.scalar.activation(wg_hi[:], wg[:], ACT.Copy).then_inc(w_high, 1)
            act.wait_ge(eps_made, 1)
            with act.Fori(0, CHUNKS // 2) as i:
                for p in range(2):
                    n = i * 2 + p
                    act.wait_ge(divided, n + 1)
                    act.wait_ge(projected, n * TILES + 1)
                    nc.scalar.activation(a_hi[p][:], o_c[p][:], ACT.Copy).then_inc(a_high, 1)
                    for step in range(TILES + 1):
                        if step < TILES:
                            act.wait_ge(averaged, n * TILES + step + 1)
                            nc.scalar.activation(spread[:, step:step + 1], moments[:, step, 1:2], ACT.Sqrt,
                                                 bias=eps[:, 0:1]).then_inc(rooted, 1)
                        if step >= 1:
                            t = step - 1
                            act.wait_ge(turned, n * TILES + t + 1)
                            nc.scalar.activation(rows[:, bass.ds(n * TILES + t, 1), :], fresh[:, t:t + 1, :], ACT.Copy)
                            nc.scalar.activation(t_hi[:, :, bass.ds(n * CHUNK + t * P, P)],
                                                 turn_ps[t % 2][:].rearrange("p (k t) -> p k t", k=KC),
                                                 ACT.Copy).then_inc(turned_high, 1)
                    act.wait_ge(gated, n + 1)
                    act.wait_ge(logit_back, n + 1)
                    nc.scalar.activation(logit_t[:], logit_ps[:], ACT.Copy).then_inc(logit_kept, 1)
            act.wait_ge(lowered, 1)
            nc.scalar.activation(logits[:], logits[:], ACT.Exp).then_inc(exped, 1)
            act.wait_ge(weight_turned, 2)
            nc.scalar.activation(weight_t[:], back_ps[:, 0:2 * P].rearrange("p (a t) -> p a t", a=2), ACT.Copy
                                 ).then_inc(weight_kept, 2)
            act.wait_ge(weight_kept, 2)

        @block.vector
        def _(dve):
            prime(dve, logit_done)
            prime(dve, turned_low, by=2)
            dve.wait_ge(den_in, DMA)
            nc.vector.reciprocal(den[:], den[:]).then_inc(inverted, 1)
            nc.vector.memset(eps[:], 1e-5).then_inc(eps_made, 1)
            dve.wait_ge(w_high, 1)
            nc.vector.tensor_tensor(wo_lo[:], wo[:], wo_hi[:], ALU.subtract).then_inc(w_split, 1)
            dve.wait_ge(w_high, 2)
            nc.vector.tensor_tensor(wg_lo[:], wg[:], wg_hi[:], ALU.subtract).then_inc(w_split, 1)
            with dve.Fori(0, CHUNKS // 2) as i:
                for p in range(2):
                    n = i * 2 + p
                    dve.wait_ge(a_high, n + 1)
                    nc.vector.tensor_tensor(a_lo[p][:], o_c[p][:], a_hi[p][:], ALU.subtract).then_inc(a_split, 1)
                    for step in range(TILES + 3):
                        if step < TILES:
                            t = step
                            if t == 0:
                                dve.wait_ge(x_in[p], (i + 1) * DMA)
                            dve.wait_ge(projected, n * TILES + t + 2 + TILES)
                            row = rows[:, bass.ds(n * TILES + t, 1), :].rearrange("p a d -> p (a d)")
                            nc.vector.tensor_tensor(fresh[:, t, :], wo_ps[t][:], row, ALU.add).then_inc(added, 1)
                            dve.wait_ge(added, n * TILES + t + 2 + TILES)
                            if t >= 1:
                                dve.wait_ge(counted, n * TILES + t)
                            nc.vector.bn_stats(stats[:, t, :], fresh[:, t, :]).then_inc(counted, 1)
                        if 2 <= step < TILES + 2:
                            t = step - 2
                            dve.wait_ge(rooted, n * TILES + t + 1)
                            if step == TILES:
                                dve.wait_ge(counted, n * TILES + TILES)
                            nc.vector.reciprocal(scale[:, t:t + 1], spread[:, t:t + 1]).then_inc(scaled, 1)
                        if 1 <= step <= TILES:
                            t = step - 1
                            nc.vector.bn_aggr(moments[:, t, :], stats[:, t, :]).then_inc(averaged, 1)
                        if 2 <= step < TILES + 2:
                            t = step - 2
                            dve.wait_ge(scaled, n * TILES + t + 1)
                            nc.vector.tensor_scalar(fresh[:, t, :], fresh[:, t, :], moments[:, t, 0:1], scale[:, t:t + 1],
                                                    ALU.subtract, ALU.mult).then_inc(normed, 1)
                        if step >= 3:
                            t = step - 3
                            cols = bass.ds(n * CHUNK + t * P, P)
                            dve.wait_ge(turned_high, n * TILES + t + 1)
                            nc.vector.tensor_tensor(t_lo[:, :, cols], turn_ps[t % 2][:].rearrange("p (k t) -> p k t", k=KC),
                                                    t_hi[:, :, cols], ALU.subtract).then_inc(turned_low, 1)
                    dve.wait_ge(logit_back, n + 2)
                    nc.vector.tensor_copy(logits[:, bass.ds(n * TILES, TILES), :],
                                          back_ps[:].rearrange("p (t e) -> p t e", e=P)[:, :, 0:EXPERTS]
                                          ).then_inc(logit_done, 1)
            wide = lambda v: v[:].unsqueeze(2).to_broadcast(shape)
            done = 0

            def step(made):
                nonlocal done
                done += 1
                made.then_inc(chosen, 1)
                dve.wait_ge(chosen, done)

            def pick_largest(value, best, hot):
                step(nc.vector.tensor_reduce(best[:], value[:], AX.X, ALU.max))
                step(nc.vector.tensor_tensor(eq[:], value[:], wide(best), ALU.is_equal))
                step(nc.vector.tensor_tensor(cand[:], eq[:], rank[:], ALU.mult))
                step(nc.vector.tensor_reduce(pick[:], cand[:], AX.X, ALU.max))
                step(nc.vector.tensor_tensor(hot[:], cand[:], wide(pick), ALU.is_equal))

            dve.wait_ge(logit_done, CHUNKS + 1)
            dve.wait_ge(ranked, 1)
            step(nc.vector.tensor_reduce(top[:], logits[:], AX.X, ALU.max))
            nc.vector.tensor_tensor(logits[:], logits[:], wide(top), ALU.subtract).then_inc(lowered, 1)
            dve.wait_ge(exped, 1)
            pick_largest(logits, top, first)
            step(nc.vector.tensor_scalar(eq[:], first[:], 2.0, None, ALU.mult))
            step(nc.vector.tensor_tensor(logits[:], logits[:], eq[:], ALU.subtract))
            pick_largest(logits, low_top, second)
            step(nc.vector.tensor_tensor(total[:], top[:], low_top[:], ALU.add))
            step(nc.vector.reciprocal(inv_total[:], total[:]))
            step(nc.vector.tensor_tensor(w_low[:], low_top[:], inv_total[:], ALU.mult))
            step(nc.vector.tensor_tensor(eq[:], first[:], wide(inv_total), ALU.mult))
            step(nc.vector.tensor_tensor(cand[:], second[:], wide(w_low), ALU.mult))
            step(nc.vector.tensor_tensor(weight[:].rearrange("p (t e) -> p t e", e=EXPERTS), eq[:], cand[:], ALU.add))

        STEPS = 1 + 5 + 2 + 5 + 6

        @block.tensor
        def _(pe):
            prime(pe, logit_back)
            prime(pe, projected, by=TILES + 1)
            pe.wait_ge(w_split, 2)
            with pe.Fori(0, CHUNKS // 2) as i:
                for p in range(2):
                    n = i * 2 + p

                    def turn(t):
                        pe.wait_ge(turned_low, n * TILES + t + 1)
                        pe.wait_ge(normed, n * TILES + t + 1)
                        for k in range(KC):
                            last = nc.tensor.transpose(turn_ps[t % 2][:, k * P:(k + 1) * P],
                                                       fresh[:, t, k * P:(k + 1) * P], ident[:])
                        last.then_inc(turned, 1)

                    for t in range(TILES):
                        if t == 0:
                            pe.wait_ge(a_split, n + 3)
                        pe.wait_ge(added, n * TILES + t + 2)
                        terms = [(k, a, b) for k in range(KC) for a, b in
                                 ((a_hi[p], wo_hi), (a_hi[p], wo_lo), (a_lo[p], wo_hi))]
                        for j, (k, a, b) in enumerate(terms):
                            last = nc.tensor.matmul(wo_ps[t][:], a[:, k, t * P:(t + 1) * P], b[:, k, :], start=j == 0,
                                                    stop=j == len(terms) - 1)
                        last.then_inc(projected, 1)
                        if t >= 2:
                            turn(t - 2)
                    turn(TILES - 2)
                    turn(TILES - 1)
                    pe.wait_ge(turned_low, (n + 1) * TILES + 2)
                    pe.wait_ge(logit_kept, n + 1)
                    cols = bass.ds(n * CHUNK, CHUNK)
                    terms = [(k, a, b) for k in range(KC) for a, b in ((wg_hi, t_hi), (wg_hi, t_lo), (wg_lo, t_hi))]
                    for j, (k, a, b) in enumerate(terms):
                        last = nc.tensor.matmul(logit_ps[:], a[:, k, :], b[:, k, cols], start=j == 0,
                                                stop=j == len(terms) - 1)
                    last.then_inc(gated, 1)
                    pe.wait_ge(logit_kept, n + 2)
                    pe.wait_ge(logit_done, n + 1)
                    for t in range(TILES):
                        last = nc.tensor.transpose(back_ps[:, t * P:(t + 1) * P], logit_t[:, t * P:(t + 1) * P],
                                                   ident[:])
                    last.then_inc(logit_back, 1)
            pe.wait_ge(logit_done, CHUNKS + 1)
            pe.wait_ge(chosen, STEPS)
            for half in range(2):
                nc.tensor.transpose(back_ps[:, half * P:(half + 1) * P], weight[:, half * P:(half + 1) * P],
                                    ident[:]).then_inc(weight_turned, 1)


def feed_forward(nc, w_gate_up, w_down, c_s, rows, t_hi, t_lo, out):
    with ExitStack() as c:
        sb = lambda n, s, d=F32: c.enter_context(nc.sbuf_tensor(f"ff_{n}", s, d))
        sem = lambda n: c.enter_context(nc.semaphore(f"ff_{n}"))
        ps = lambda n: c.enter_context(nc.psum_tensor(f"ff_{n}", [P, CHUNK], F32))
        TILES = CHUNK // P
        ALL = SHARED + EXPERTS
        GU = 2 * INTER
        w_gu = [sb(f"w_gu{p}", [P, KC, GU]) for p in range(2)]
        w_dn = [sb(f"w_dn{p}", [P, DIM]) for p in range(2)]
        gu_hi = [sb(f"gu_hi{p}", [P, KC, GU], F32R) for p in range(2)]
        gu_lo = [sb(f"gu_lo{p}", [P, KC, GU], F32R) for p in range(2)]
        dn_hi = [sb(f"dn_hi{p}", [P, DIM], F32R) for p in range(2)]
        dn_lo = [sb(f"dn_lo{p}", [P, DIM], F32R) for p in range(2)]
        coef = [sb(f"coef{p}", [P, TOKENS]) for p in range(2)]
        gate = [sb(f"gate{j}", [P, CHUNK]) for j in range(2)]
        up = [sb(f"up{j}", [P, CHUNK]) for j in range(2)]
        act_f = [sb(f"act_f{j}", [P, CHUNK]) for j in range(2)]
        act_hi = [sb(f"act_hi{j}", [P, CHUNK], F32R) for j in range(2)]
        act_lo = [sb(f"act_lo{j}", [P, CHUNK], F32R) for j in range(2)]
        eps = sb("eps", [P, 1])
        stats = sb("stats", [P, TOKENS // P, 6])
        moments = sb("moments", [P, TOKENS // P, 2])
        spread, scale = sb("spread", [P, TOKENS // P]), sb("scale", [P, TOKENS // P])
        gate_ps = [ps(f"gate_ps{j}") for j in range(2)]
        up_ps = [ps(f"up_ps{j}") for j in range(2)]
        y_ps = [ps(f"y_ps{t}") for t in range(TILES)]

        w_in = [sem(f"w_in{p}") for p in range(2)]
        w_high, w_split = sem("w_high"), sem("w_split")
        gated, upped, silued, weighted = sem("gated"), sem("upped"), sem("silued"), sem("weighted")
        acted, act_high, act_split = sem("acted"), sem("act_high"), sem("act_split")
        downed, added = sem("downed"), sem("added")
        eps_made, counted, averaged, rooted, scaled, normed = [
            sem(n) for n in ("eps_made", "counted", "averaged", "rooted", "scaled", "normed")]
        stored = sem("stored")
        LOADS = 3
        block = c.enter_context(nc.Block())

        @block.sync
        def _(sp):
            prime(sp, w_split, by=2)
            prime(sp, weighted, by=CHUNKS + 1)
            with sp.Fori(0, ALL // 2) as i:
                for p in range(2):
                    e = i * 2 + p
                    sp.wait_ge(w_split, e + 1)
                    sp.dma_start(w_gu[p][:], w_gate_up[bass.ds(e, 1)].rearrange("e (k p) n -> p (e k) n", p=P)
                                 ).then_inc(w_in[p], DMA)
                    sp.dma_start(w_dn[p][:], w_down[bass.ds(e, 1)].rearrange("e p n -> p (e n)")).then_inc(w_in[p], DMA)
                    sp.wait_ge(weighted, e * CHUNKS + 1)
                    sp.dma_start(coef[p][:], c_s[bass.ds(e, 1), :].to_broadcast([P, TOKENS])).then_inc(w_in[p], DMA)
            for t in range(TOKENS // P):
                sp.wait_ge(normed, t + 1)
                sp.dma_start(out[t * P:(t + 1) * P, :], rows[:, t, :]).then_inc(stored, DMA)
            sp.wait_ge(stored, TOKENS // P * DMA)

        @block.scalar
        def _(act):
            prime(act, silued, by=2)

            def high_weights(p, e, pair):
                act.wait_ge(w_in[p], (pair + 1) * (LOADS * DMA))
                act.wait_ge(downed, e * (CHUNKS * TILES) + 1)
                nc.scalar.activation(gu_hi[p][:], w_gu[p][:], ACT.Copy)
                nc.scalar.activation(dn_hi[p][:], w_dn[p][:], ACT.Copy).then_inc(w_high, 1)

            def pair_of_experts(i, final=False):
                for p in range(2):
                    e = i * 2 + p
                    for n in range(CHUNKS):
                        j = n % 2
                        u = e * CHUNKS + n
                        act.wait_ge(gated, u + 1)
                        act.wait_ge(acted, u + 1)
                        nc.scalar.activation(gate[j][:], gate_ps[j][:], ACT.Silu).then_inc(silued, 1)
                        act.wait_ge(acted, u + 3)
                        act.wait_ge(downed, u * TILES + (CHUNKS - 1) * TILES + 1)
                        nc.scalar.activation(act_hi[j][:], act_f[j][:], ACT.Copy).then_inc(act_high, 1)
                        if n == 1 and not (final and p == 1):
                            high_weights(1 - p, e + 1, i + p)

            high_weights(0, 0, 0)
            with act.Fori(0, ALL // 2 - 1) as i:
                pair_of_experts(i)
            pair_of_experts(ALL // 2 - 1, final=True)
            act.wait_ge(eps_made, 1)
            act.wait_ge(averaged, TOKENS // P)
            nc.scalar.activation(spread[:], moments[:, :, 1], ACT.Sqrt, bias=eps[:, 0:1]).then_inc(rooted, 1)

        @block.gpsimd
        def _(pool):
            nc.gpsimd.memset(eps[:], 1e-5).then_inc(eps_made, 1)
            with pool.Fori(0, ALL // 2) as i:
                for p in range(2):
                    pool.wait_ge(w_high, i * 2 + p + 1)
                    nc.gpsimd.tensor_tensor(gu_lo[p][:], w_gu[p][:], gu_hi[p][:], ALU.subtract)
                    nc.gpsimd.tensor_tensor(dn_lo[p][:], w_dn[p][:], dn_hi[p][:], ALU.subtract).then_inc(w_split, 1)

        @block.vector
        def _(dve):
            prime(dve, acted, by=2)
            prime(dve, added, by=TILES)
            with dve.Fori(0, ALL // 2) as i:
                for p in range(2):
                    for n in range(CHUNKS):
                        j = n % 2
                        u = (i * 2 + p) * CHUNKS + n
                        if n == 0:
                            dve.wait_ge(w_in[p], (i + 1) * (LOADS * DMA))
                        dve.wait_ge(upped, u + 1)
                        nc.vector.tensor_tensor(up[j][:], up_ps[j][:], coef[p][:, n * CHUNK:(n + 1) * CHUNK], ALU.mult
                                                ).then_inc(weighted, 1)
                        dve.wait_ge(weighted, u + CHUNKS + 2)
                        dve.wait_ge(silued, u + 3)
                        nc.vector.tensor_tensor(act_f[j][:], up[j][:], gate[j][:], ALU.mult).then_inc(acted, 1)
                        dve.wait_ge(act_high, u + 1)
                        nc.vector.tensor_tensor(act_lo[j][:], act_f[j][:], act_hi[j][:], ALU.subtract).then_inc(act_split, 1)
                        for t in range(TILES):
                            row = rows[:, n * TILES + t, :]
                            dve.wait_ge(downed, u * TILES + t + 2 + CHUNKS * TILES)
                            nc.vector.tensor_tensor(row, row, y_ps[t][:], ALU.add).then_inc(added, 1)
            dve.wait_ge(added, ALL * CHUNKS * TILES + TILES)
            for t in range(TOKENS // P):
                nc.vector.bn_stats(stats[:, t, :], rows[:, t, :]).then_inc(counted, 1)
            for t in range(TOKENS // P):
                dve.wait_ge(counted, t + 1)
                nc.vector.bn_aggr(moments[:, t, :], stats[:, t, :]).then_inc(averaged, 1)
            dve.wait_ge(rooted, 1)
            nc.vector.reciprocal(scale[:], spread[:]).then_inc(scaled, 1)
            dve.wait_ge(scaled, 1)
            for t in range(TOKENS // P):
                nc.vector.tensor_scalar(rows[:, t, :], rows[:, t, :], moments[:, t, 0:1], scale[:, t:t + 1],
                                        ALU.subtract, ALU.mult).then_inc(normed, 1)

        @block.tensor
        def _(pe):
            prime(pe, downed, by=CHUNKS * TILES + 1)

            def gate_and_up(p, e, n):
                j = n % 2
                u = e * CHUNKS + n
                if n == 0:
                    pe.wait_ge(w_split, e + 3)
                cols = slice(n * CHUNK, (n + 1) * CHUNK)
                for bank, first, done in ((gate_ps[j], 0, gated), (up_ps[j], INTER, upped)):
                    if done is gated:
                        pe.wait_ge(silued, u + 1)
                    else:
                        pe.wait_ge(weighted, u + CHUNKS)
                    terms = [(k, a, b) for k in range(KC) for a, b in
                             ((gu_hi[p], t_hi), (gu_hi[p], t_lo), (gu_lo[p], t_hi))]
                    for m, (k, a, b) in enumerate(terms):
                        last = nc.tensor.matmul(bank[:], a[:, k, first:first + INTER], b[:, k, cols], start=m == 0,
                                                stop=m == len(terms) - 1)
                    last.then_inc(done, 1)

            def down(p, e, n):
                j = n % 2
                u = e * CHUNKS + n
                pe.wait_ge(act_split, u + 1)
                for t in range(TILES):
                    pe.wait_ge(added, u * TILES + t + 1)
                    terms = ((act_hi[j], dn_hi[p]), (act_hi[j], dn_lo[p]), (act_lo[j], dn_hi[p]))
                    for m, (a, b) in enumerate(terms):
                        last = nc.tensor.matmul(y_ps[t][:], a[:, t * P:(t + 1) * P], b[:], start=m == 0, stop=m == 2)
                    last.then_inc(downed, 1)

            def pair_of_experts(i, final=False):
                for p in range(2):
                    e = i * 2 + p
                    for n in range(CHUNKS):
                        if n + 1 < CHUNKS:
                            gate_and_up(p, e, n + 1)
                        elif not (final and p == 1):
                            gate_and_up(1 - p, e + 1, 0)
                        down(p, e, n)

            gate_and_up(0, 0, 0)
            with pe.Fori(0, ALL // 2 - 1) as i:
                pair_of_experts(i)
            pair_of_experts(ALL // 2 - 1, final=True)


def layer(nc, ins, out):
    with ExitStack() as c:
        dram = lambda n, *s: nc.dram_tensor(n, s, F32).ap()
        q_s, k_s = dram("q_scratch", HEADS, 2, HEAD, TOKENS), dram("k_scratch", KV_HEADS, 2, HEAD, TOKENS)
        m_s = dram("m_scratch", HEADS, 2, TOKENS)
        o_s, d_s, r_s = dram("o_scratch", HEADS, HEAD, TOKENS), dram("d_scratch", HEADS, TOKENS), dram("r_scratch", HEADS, TOKENS)
        c_s = dram("c_scratch", SHARED + EXPERTS, TOKENS)
        sb = lambda n, s, d=F32: c.enter_context(nc.sbuf_tensor(n, s, d))
        ident = sb("ident", [P, P])
        bound = sb("bound", [P, 1])
        with nc.sbuf_tensor("values", [P, TOKENS // P, P], F32) as values:
            project_qkv(nc, ins["x_t"], ins["w_qkv"], ins["cos"], ins["sin"], ins["ident"], q_s, k_s, m_s, values, ident,
                        bound)
            attend(nc, q_s, k_s, m_s, values, bound, o_s, d_s)
        rows = sb("rows", [P, TOKENS // P, DIM])
        t_hi, t_lo = sb("t_hi", [P, KC, TOKENS], F32R), sb("t_lo", [P, KC, TOKENS], F32R)
        project_out(nc, ins["x"], ins["w_o"], ins["w_gate"], ident, o_s, d_s, r_s, c_s, rows, t_hi, t_lo)
        feed_forward(nc, ins["w_gate_up"], ins["w_down"], c_s, rows, t_hi, t_lo, out)


def arrange(a):
    import numpy as np
    f = lambda n: np.asarray(a[n])
    x = f("L0_attn_x").reshape(TOKENS, DIM)
    w_q = f("L0_attn_Wq").reshape(DIM, SETS, SET_HEADS * PAIRS, 2)
    w_k = f("L0_attn_Wk").reshape(DIM, KV_HEADS * PAIRS, 2)
    cols = [w_k[:, :, 0], w_k[:, :, 0], w_k[:, :, 1], w_k[:, :, 1]]
    for s in range(SETS):
        cols += [w_q[:, s, :, 0], w_q[:, s, :, 1]]
    cols.append(f("L0_attn_Wv"))
    inv_freq = (1.0 / np.float32(10000.0) ** (np.arange(0, HEAD, 2, dtype=np.float32) / np.float32(HEAD))).astype(np.float32)
    ang = np.arange(SEQ, dtype=np.float32)[None, :] * np.tile(inv_freq, SET_HEADS)[:, None]
    gate = np.zeros((DIM, P), np.float32)
    gate[:, :EXPERTS] = f("L0_ffn_gate_w").T
    shared = f("L0_ffn_shared_w_gate_up").reshape(2, SHARED, INTER, DIM).transpose(1, 3, 0, 2).reshape(SHARED, DIM, 2 * INTER)
    shared_down = f("L0_ffn_shared_w_down").reshape(DIM, SHARED, INTER).transpose(1, 2, 0)
    t = np.ascontiguousarray
    return {
        "x": t(x), "x_t": t(x.T), "w_qkv": np.concatenate(cols, axis=1),
        "cos": np.cos(ang).astype(np.float32), "sin": np.sin(ang).astype(np.float32),
        "ident": np.eye(P, dtype=np.float32),
        "w_o": t(f("L0_attn_Wo")), "w_gate": gate,
        "w_gate_up": np.concatenate([shared, f("L0_ffn_w_gate_up").transpose(0, 2, 1)]),
        "w_down": np.concatenate([shared_down, f("L0_ffn_w_down").transpose(0, 2, 1)]),
    }


def kernel(**inputs):
    import concourse.bacc as bacc
    from concourse.bass_utils import run_bass_kernel_spmd as run

    nc = bacc.Bacc("TRN2", target_bir_lowering=False, num_devices=1)
    arrays = arrange(inputs)
    ins = {n: nc.dram_tensor(f"in_{n}", v.shape, mybir.dt.from_np(v.dtype), kind="ExternalInput").ap() for n, v in arrays.items()}
    out = nc.dram_tensor("out", (TOKENS, DIM), F32, kind="ExternalOutput").ap()
    layer(nc, ins, out)
    r = run(nc, [{f"in_{n}": v for n, v in arrays.items()}], core_ids=[0])
    return r.results[0]["out"].reshape(BATCH, SEQ, DIM)
```

```python
from contextlib import ExitStack

import concourse.bass as bass
from concourse import mybir

F32 = mybir.dt.float32
F32R = mybir.dt.float32r
BF16 = mybir.dt.bfloat16
I32 = mybir.dt.int32
ALU = mybir.AluOpType
ACT = mybir.ActivationFunctionType
AX = mybir.AxisListType

P = 128
BATCH, SEQ, DIM = 2, 1024, 512
TOKENS = BATCH * SEQ
HEADS, KV_HEADS, HEAD = 32, 8, 16
REP = HEADS // KV_HEADS
PAIRS = HEAD // 2
KC = DIM // P
CHUNK = 512
CHUNKS = TOKENS // CHUNK
KT = SEQ // P
GROUPS = BATCH * KV_HEADS
SETS = HEADS * PAIRS // P
SET_HEADS = P // PAIRS
COLS = 7
SCALE = HEAD ** -0.5
VW = 32
EXPERTS, INTER = 16, 128
SHARED = 512 // INTER
SLOT_TILES = 2 * TOKENS // P + EXPERTS
LARGEST = 3.4028234663852886e38
DMA = 16


def prime(eng, *sems, by=1):
    for s in sems:
        eng.sem_inc(s, by)


def project_qkv(nc, x_t, w_qkv, cos, sin, ident_dram, q_s, k_s, m_s, values, ident, bound):
    with ExitStack() as c:
        sb = lambda n, s, d=F32: c.enter_context(nc.sbuf_tensor(n, s, d))
        sem = lambda n: c.enter_context(nc.semaphore(n))
        w = sb("w", [P, KC, COLS * P])
        w_hi = sb("w_hi", [P, KC, COLS * P], F32R)
        w_lo = sb("w_lo", [P, KC, COLS * P], F32R)
        xs = [sb(f"x{n}", [P, KC, CHUNK]) for n in range(2)]
        x_hi = sb("x_hi", [P, KC, TOKENS], F32R)
        x_lo = sb("x_lo", [P, KC, TOKENS], F32R)
        cos_s = sb("cos_s", [P, SEQ])
        sin_s = sb("sin_s", [P, SEQ])
        prod = sb("prod", [P, 4, CHUNK])
        rot = sb("rot", [P, 2, CHUNK])
        parts = sb("parts", [P, SETS + 1, 2, 2, CHUNK], F32R)
        v_t = sb("v_t", [P, TOKENS])
        sq = sb("sq", [P, 2, CHUNK], BF16)
        sum_heads = sb("sum_heads", [P, 32], BF16)
        norm = sb("norm", [P, CHUNK])
        norm_hi = sb("norm_hi", [P, CHUNK], F32R)
        norm_lo = sb("norm_lo", [P, CHUNK], F32R)
        k_max = sb("k_max", [P, CHUNKS])
        k_top = sb("k_top", [P, 1])
        k_one = sb("k_one", [1, 1])
        ones_row = sb("ones_row", [1, P])
        acc = [c.enter_context(nc.psum_tensor(f"acc{j}", [P, CHUNK], F32)) for j in range(COLS)]
        small = c.enter_context(nc.psum_tensor("small", [P, CHUNK], F32))

        w_in, x_in, table_in, ident_in = [sem(f"w_in{j}") for j in range(SETS + 2)], [sem("x_in0"), sem("x_in1")], sem("table_in"), sem("ident_in")
        w_high, w_split, x_high, x_split = sem("w_high"), sem("w_split"), sem("x_high"), sem("x_split")
        projected = sem("projected")
        products, turned = sem("products"), sem("turned")
        high, low, stored = sem("high"), sem("low"), sem("stored")
        squared, summed, normed = sem("squared"), sem("summed"), sem("normed")
        norm_high, norm_low, norm_stored = sem("norm_high"), sem("norm_low"), sem("norm_stored")
        v_copied, v_turned, v_kept = sem("v_copied"), sem("v_turned"), sem("v_kept")
        made = sem("made")
        top_ready, top_turned, top_one, top_spread, top_done = [sem(f"top{j}") for j in range(5)]
        block = c.enter_context(nc.Block())
        N_SETS = SETS + 1
        W_PARTS = [(2 * P * s, min(2 * P * (s + 1), COLS * P)) for s in range(N_SETS + 1)]

        @block.sync
        def _(sp):
            prime(sp, stored, norm_stored)

            def load_w(i):
                a, b = W_PARTS[i]
                sp.dma_start(w[:, :, a:b], w_qkv.rearrange("(c p) n -> p c n", p=P)[:, :, a:b]).then_inc(w_in[i], DMA)

            load_w(0)
            for n in range(CHUNKS):
                if n >= 2:
                    sp.wait_ge(x_split, n - 1)
                sp.dma_start(xs[n % 2][:], x_t[:, n * CHUNK:(n + 1) * CHUNK].rearrange("(c p) n -> p c n", p=P)
                             ).then_inc(x_in[n % 2], DMA)
                if n == 0:
                    for i in range(1, len(W_PARTS)):
                        load_w(i)
                    sp.dma_start(cos_s[:], cos).then_inc(table_in, DMA)
                    sp.dma_start(sin_s[:], sin).then_inc(table_in, DMA)
                    sp.dma_start(ident[:], ident_dram).then_inc(ident_in, DMA)
            with sp.Fori(0, CHUNKS) as n:
                col = n * CHUNK
                for s in range(N_SETS):
                    rows = P // 2 if s == 0 else P
                    dst = k_s if s == 0 else q_s[(s - 1) * SET_HEADS:s * SET_HEADS]
                    for half in range(2):
                        for part in range(2):
                            if half == 0 and part == 0:
                                sp.wait_ge(low, (n * N_SETS + s + 1) * 2 + 1)
                            sp.dma_start(dst[:, part, half * PAIRS:(half + 1) * PAIRS, bass.ds(col, CHUNK)],
                                         parts[0:rows, s, half, part, :].bitcast(F32)).then_inc(stored, DMA)
                sp.wait_ge(norm_low, n + 2)
                for s in range(SETS):
                    for part, src in enumerate((norm_hi, norm_lo)):
                        at = 32 * (s + 1)
                        sp.dma_start(m_s[s * SET_HEADS:(s + 1) * SET_HEADS, part, bass.ds(col, CHUNK)],
                                     src[at:at + SET_HEADS, :].bitcast(F32)).then_inc(norm_stored, DMA)
            sp.wait_ge(stored, CHUNKS * N_SETS * 4 * DMA + 1)
            sp.wait_ge(norm_stored, CHUNKS * SETS * 2 * DMA + 1)

        @block.scalar
        def _(act):
            prime(act, squared, high, v_copied, normed, norm_high)

            def w_part(i):
                a, b = W_PARTS[i]
                act.wait_ge(w_in[i], DMA)
                nc.scalar.activation(w_hi[:, :, a:b], w[:, :, a:b], ACT.Copy).then_inc(w_high, 1)

            w_part(0)
            for n in range(CHUNKS):
                act.wait_ge(x_in[n % 2], DMA * (n // 2 + 1))
                nc.scalar.activation(x_hi[:, :, n * CHUNK:(n + 1) * CHUNK], xs[n % 2][:], ACT.Copy).then_inc(x_high, 1)
                if n == 0:
                    for i in range(1, len(W_PARTS)):
                        w_part(i)
            with act.Fori(0, CHUNKS) as n:
                for s in range(N_SETS):
                    act.wait_ge(projected, n * COLS + 2 * s + 3)
                    act.wait_ge(summed, n * N_SETS + s + 1)
                    for half in range(2):
                        last = nc.scalar.activation(sq[:, half, :], acc[2 * s + half][:], ACT.Square)
                    last.then_inc(squared, 1)
                    if s == N_SETS - 1:
                        act.wait_ge(projected, n * COLS + COLS + 1)
                        nc.scalar.activation(v_t[:, bass.ds(n * CHUNK, CHUNK)], acc[COLS - 1][:], ACT.Copy).then_inc(v_copied, 1)
                    act.wait_ge(turned, n * N_SETS + s + 2)
                    if s == 0:
                        act.wait_ge(stored, n * (N_SETS * 4 * DMA) + 1)
                    nc.scalar.activation(parts[:, s, :, 0, :], rot[:], ACT.Copy).then_inc(high, 1)
                act.wait_ge(summed, n * N_SETS + N_SETS + 1)
                act.wait_ge(norm_low, n + 1)
                nc.scalar.activation(norm[0:96], small[0:96], ACT.Copy, scale=-0.5).then_inc(normed, 1)
                act.wait_ge(normed, n + 2)
                act.wait_ge(norm_stored, n * (SETS * 2 * DMA) + 1)
                nc.scalar.activation(norm_hi[0:96], norm[0:96], ACT.Copy).then_inc(norm_high, 1)
            for n in range(CHUNKS):
                act.wait_ge(v_turned, n + 1)
                nc.scalar.activation(values[:, n * (CHUNK // P):(n + 1) * (CHUNK // P), :],
                                     acc[n][:].rearrange("p (t d) -> p t d", d=P), ACT.Copy).then_inc(v_kept, 1)
            act.wait_ge(v_kept, CHUNKS)

        @block.vector
        def _(dve):
            nc.vector.memset(ones_row[:], 1.0).then_inc(made, 1)
            for _ in range(N_SETS - 1):
                prime(dve, products)
            prime(dve, products, turned, low, norm_low)

            def w_part(i):
                a, b = W_PARTS[i]
                dve.wait_ge(w_high, i + 1)
                nc.vector.tensor_tensor(w_lo[:, :, a:b], w[:, :, a:b], w_hi[:, :, a:b], ALU.subtract).then_inc(w_split, 1)

            w_part(0)
            dve.wait_ge(x_high, 1)
            nc.vector.tensor_tensor(x_lo[:, :, 0:CHUNK], xs[0][:], x_hi[:, :, 0:CHUNK], ALU.subtract).then_inc(x_split, 1)
            for i in range(1, len(W_PARTS)):
                w_part(i)
            dve.wait_ge(table_in, 2 * DMA)
            with dve.Fori(0, BATCH) as b:
                for half_seq in range(SEQ // CHUNK):
                    n = b * (SEQ // CHUNK) + half_seq
                    co = cos_s[:, half_seq * CHUNK:(half_seq + 1) * CHUNK]
                    si = sin_s[:, half_seq * CHUNK:(half_seq + 1) * CHUNK]
                    for s in range(N_SETS):
                        even, odd = acc[2 * s], acc[2 * s + 1]
                        dve.wait_ge(squared, n * N_SETS + s + 2)
                        dve.wait_ge(turned, n * N_SETS + s + 1)
                        nc.vector.tensor_tensor(prod[:, 0, :], even[:], co, ALU.mult)
                        nc.vector.tensor_tensor(prod[:, 1, :], odd[:], si, ALU.mult)
                        nc.vector.tensor_tensor(prod[:, 2, :], even[:], si, ALU.mult)
                        nc.vector.tensor_tensor(prod[:, 3, :], odd[:], co, ALU.mult).then_inc(products, 1)
                        dve.wait_ge(products, (n + 1) * N_SETS + s + 1)
                        dve.wait_ge(high, n * N_SETS + s + 1)
                        dve.wait_ge(low, (n * N_SETS + s) * 2 + 1)
                        nc.vector.tensor_tensor(rot[:, 0, :], prod[:, 0, :], prod[:, 1, :], ALU.subtract)
                        nc.vector.tensor_tensor(rot[:, 1, :], prod[:, 2, :], prod[:, 3, :], ALU.add).then_inc(turned, 1)
                        dve.wait_ge(high, n * N_SETS + s + 2)
                        for half in range(2):
                            nc.vector.tensor_tensor(parts[:, s, half, 1, :], rot[:, half, :], parts[:, s, half, 0, :],
                                                    ALU.subtract).then_inc(low, 1)
                    dve.wait_ge(norm_high, n + 2)
                    nc.vector.tensor_tensor(norm_lo[0:96], norm[0:96], norm_hi[0:96], ALU.subtract)
                    nc.vector.tensor_reduce(k_max[0:8, bass.ds(n, 1)], norm[0:8, :], AX.X, ALU.min).then_inc(norm_low, 1)
            dve.wait_ge(norm_low, CHUNKS + 1)
            nc.vector.tensor_reduce(k_top[0:8, :], k_max[0:8, :], AX.X, ALU.min).then_inc(top_ready, 1)
            dve.wait_ge(top_turned, 1)
            nc.vector.tensor_reduce(k_one[:], small[0:1, 0:8], AX.X, ALU.min).then_inc(top_one, 1)
            dve.wait_ge(top_spread, 1)
            nc.vector.tensor_copy(bound[:], small[:, 8:9]).then_inc(top_done, 1)
            dve.wait_ge(top_done, 1)

        @block.gpsimd
        def _(pool):
            nc.gpsimd.memset(sum_heads[:], 1.0).then_inc(made, 1)
            pool.wait_ge(made, 2)
            nc.gpsimd.affine_select(out=sum_heads[:], in_=sum_heads[:], compare_op=ALU.is_ge, fill=0.0, base=0,
                                    pattern=[[-PAIRS, 32]], channel_multiplier=1).then_inc(made, 1)
            pool.wait_ge(made, 3)
            nc.gpsimd.affine_select(out=sum_heads[:], in_=sum_heads[:], compare_op=ALU.is_ge, fill=0.0, base=PAIRS - 1,
                                    pattern=[[PAIRS, 32]], channel_multiplier=-1).then_inc(made, 1)
            pool.wait_ge(made, 4)
            for n in range(1, CHUNKS):
                cols = slice(n * CHUNK, (n + 1) * CHUNK)
                pool.wait_ge(x_high, n + 1)
                pool.wait_ge(x_split, n)
                nc.gpsimd.tensor_tensor(x_lo[:, :, cols], xs[n % 2][:], x_hi[:, :, cols], ALU.subtract).then_inc(x_split, 1)

        @block.tensor
        def _(pe):
            prime(pe, projected, summed)
            pe.wait_ge(made, 4)
            pe.wait_ge(ident_in, DMA)

            with pe.Fori(0, CHUNKS) as n:
                pe.wait_ge(x_split, n + 1)
                xh = x_hi[:, :, bass.ds(n * CHUNK, CHUNK)]
                xl = x_lo[:, :, bass.ds(n * CHUNK, CHUNK)]

                def norms(s):
                    pe.wait_ge(squared, n * N_SETS + s + 2)
                    if s == 0:
                        pe.wait_ge(normed, n + 1)
                    for half in range(2):
                        last = nc.tensor.matmul(small[32 * s:32 * s + 32, :], sum_heads[:], sq[:, half, :],
                                                start=half == 0, stop=half == 1)
                    last.then_inc(summed, 1)

                for j in range(COLS):
                    if j < 2 * N_SETS:
                        if j % 2 == 0:
                            pe.wait_ge(products, n * N_SETS + j // 2 + 1)
                            pe.wait_ge(w_split, j // 2 + 1)
                    else:
                        pe.wait_ge(v_copied, n + 1)
                        pe.wait_ge(w_split, len(W_PARTS))
                    terms = [(k, a, b) for k in range(KC) for a, b in ((w_hi, xh), (w_hi, xl), (w_lo, xh))]
                    for i, (k, a, b) in enumerate(terms):
                        last = nc.tensor.matmul(acc[j][:], a[:, k, j * P:(j + 1) * P], b[:, k, :],
                                                start=i == 0, stop=i == len(terms) - 1)
                    last.then_inc(projected, 1)
                    if j in (3, 5):
                        norms((j - 3) // 2)
                norms(N_SETS - 1)
            pe.wait_ge(v_copied, CHUNKS + 1)
            pe.wait_ge(products, (CHUNKS + 1) * N_SETS)
            for n in range(CHUNKS):
                for t in range(CHUNK // P):
                    at = n * CHUNK + t * P
                    last = nc.tensor.transpose(acc[n][:, t * P:(t + 1) * P], v_t[:, at:at + P], ident[:])
                last.then_inc(v_turned, 1)
            pe.wait_ge(top_ready, 1)
            nc.tensor.transpose(small[0:1, 0:8], k_top[0:8, :], ident[0:8, 0:8]).then_inc(top_turned, 1)
            pe.wait_ge(top_one, 1)
            nc.tensor.matmul(small[:, 8:9], ones_row[:], k_one[:], start=True, stop=True).then_inc(top_spread, 1)


def attend(nc, q_s, k_s, m_s, values, bound, o_s, d_s):
    with ExitStack() as c:
        sb = lambda n, s, d=F32: c.enter_context(nc.sbuf_tensor(n, s, d))
        sem = lambda n: c.enter_context(nc.semaphore(n))
        ROWS = 4 * HEAD + 3
        SLOTS = 4
        q_st = [sb(f"q_st{p}", [P, REP, SEQ], F32R) for p in range(2)]
        k_st = [sb(f"k_st{p}", [P, SEQ], F32R) for p in range(2)]
        v_st = [sb(f"v_st{p}", [P, KT, VW]) for p in range(2)]
        prob = [sb(f"prob{j}", [P, REP, SEQ]) for j in range(SLOTS)]
        o_t = [sb(f"o_t{p}", [P, SEQ]) for p in range(2)]
        cap = sb("cap", [P, P])
        ring = [c.enter_context(nc.psum_tensor(f"ring{j}", [P, SEQ], F32)) for j in range(3)]
        out_ps = c.enter_context(nc.psum_tensor("out_ps", [P, SEQ], F32))
        loaded = [sem("loaded0"), sem("loaded1")]
        LOADS, STORES = 7, 2 * REP
        cap_made, blank, zero_made, ones_made, v_blank = sem("cap_made"), sem("blank"), sem("zero_made"), sem("ones_made"), sem("v_blank")
        scored, expd, masked = sem("scored"), sem("expd"), sem("masked")
        weighed = sem("weighed")
        v_staged, out_copied, out_stored = sem("v_staged"), sem("out_copied"), [sem("out_stored0"), sem("out_stored1")]
        UNIT = []
        for kt in range(KT):
            width = SEQ - kt * P
            heads = 1 if width > CHUNK else 2 if width > CHUNK // 2 else REP
            UNIT += [(kt, h, heads) for h in range(0, REP, heads)]
        UNITS = len(UNIT)
        LAST = [max(u for u in range(UNITS) if UNIT[u][0] == kt) for kt in range(KT)]
        AHEAD = 6
        HALF = [(0, CHUNK), (CHUNK, SEQ)]
        LAST_IN_SLOT = [max(v for v in range(-UNITS, u) if v % UNITS % 3 == u % 3) for u in range(UNITS)]

        def halves(kt):
            return [(max(a, kt * P), b, j) for j, (a, b) in enumerate(HALF) if kt * P < b]

        def unit_view(tile, kt, heads):
            width = SEQ - kt * P
            if heads == 1:
                return tile[:, kt * P:SEQ].unsqueeze(1)
            pitch = CHUNK if heads == 2 else width
            return tile[:, 0:heads * pitch].rearrange("p (h w) -> p h w", h=heads)[:, :, 0:width]

        weigh_after = {}
        todo = [(kt, i) for kt in range(KT) for i in range(len(halves(kt)))]
        credit = 0
        for v in range(AHEAD, UNITS + AHEAD):
            kt, _, heads = UNIT[v % UNITS]
            credit = min(credit + heads * (SEQ - kt * P) * (0.83 - 0.42), 1600)
            weigh_after[v] = []
            while todo and LAST[todo[0][0]] <= v - 2:
                a, b, _ = halves(todo[0][0])[todo[0][1]]
                cost = (b - a) * 1.67
                if credit < cost / 2 and v < UNITS + AHEAD - 1:
                    break
                credit -= cost
                weigh_after[v].append(todo.pop(0))
        assert not todo

        block = c.enter_context(nc.Block())

        @block.sync
        def _(sp):
            def load(parity, b, kv):
                q, k, st = q_st[parity], k_st[parity], loaded[parity]
                head = kv * REP
                cols = bass.ds(b * SEQ, SEQ)
                for r in range(2):
                    sp.dma_start(q[32 * r:32 * r + 32, :, :].bitcast(F32),
                                 q_s[bass.ds(head, REP), :, :, cols].rearrange("h a d t -> (a d) h t")).then_inc(st, DMA)
                    for s in range(2):
                        at = 32 * r + HEAD * s
                        sp.dma_start(k[at:at + HEAD, :].bitcast(F32), k_s[bass.ds(kv, 1), r, :, cols].rearrange(
                            "k d t -> (k d) t")).then_inc(st, DMA)
                sp.dma_start(q[4 * HEAD:ROWS - 1, :, :].bitcast(F32),
                             m_s[bass.ds(head, REP), :, cols].rearrange("h a t -> a h t")).then_inc(st, DMA)

            sp.wait_ge(ones_made, 4)
            load(0, 0, 0)
            load(1, 0, 1)
            for b in range(BATCH):
                with sp.Fori(0, KV_HEADS // 2) as i:
                    for parity in range(2):
                        g = b * KV_HEADS + i * 2 + parity
                        sp.wait_ge(scored, (g + 1) * UNITS)
                        nxt = i * 2 + 2 + parity
                        if b + 1 < BATCH:
                            load(parity, b + nxt // KV_HEADS, nxt % KV_HEADS)
                        else:
                            load(parity, b, nxt % KV_HEADS)
                        sp.wait_ge(out_copied, g + 2)
                        for h in range(REP):
                            head = (i * 2 + parity) * REP + h
                            sp.dma_start(o_s[bass.ds(head, 1), :, b * SEQ:(b + 1) * SEQ].rearrange("h d t -> (h d) t"),
                                         o_t[parity][32 * h:32 * h + HEAD, :]).then_inc(out_stored[parity], DMA)
                            sp.dma_start(d_s[bass.ds(head, 1), b * SEQ:(b + 1) * SEQ],
                                         o_t[parity][32 * h + HEAD:32 * h + HEAD + 1, :]).then_inc(out_stored[parity], DMA)
            for parity in range(2):
                sp.wait_ge(loaded[parity], (GROUPS // 2 + 1) * LOADS * DMA)
                sp.wait_ge(out_stored[parity], GROUPS // 2 * STORES * DMA + 1)

        @block.scalar
        def _(act):
            def exp_unit(g, u, first=False):
                kt, h, heads = UNIT[u]
                act.wait_ge(scored, g * UNITS + u + 1)
                if h == 0 and not (first and kt < SLOTS):
                    act.wait_ge(weighed, g * KT + kt - SLOTS + 2)
                nc.scalar.activation(prob[kt % SLOTS][:, h:h + heads, kt * P:SEQ], unit_view(ring[u % 3], kt, heads),
                                     ACT.Exp, scale=SCALE).then_inc(expd, 1)

            act.wait_ge(ones_made, 4)
            for u in range(UNITS):
                exp_unit(0, u, first=True)
            with act.Fori(1, GROUPS) as g:
                for u in range(UNITS):
                    exp_unit(g, u)
            for u in range(AHEAD):
                exp_unit(GROUPS, u)

        @block.gpsimd
        def _(pool):
            def stage_v(parity, b, kv):
                nc.gpsimd.tensor_copy(v_st[parity][:, :, 0:HEAD],
                                      values[:, bass.ds(b * KT, KT), bass.ds(kv * HEAD, HEAD)]).then_inc(v_staged, 1)

            nc.gpsimd.memset(cap[:], LARGEST).then_inc(cap_made, 1)
            pool.wait_ge(cap_made, 1)
            nc.gpsimd.affine_select(out=cap[:], in_=cap[:], compare_op=ALU.is_ge, fill=0.0, base=0,
                                    pattern=[[1, P]], channel_multiplier=-1).then_inc(cap_made, 1)
            pool.wait_ge(cap_made, 2)
            pool.wait_ge(v_blank, 4)
            stage_v(0, 0, 0)
            with pool.Fori(0, GROUPS // 2) as i:
                for parity in range(2):
                    g = i * 2 + parity
                    pool.wait_ge(weighed, g * KT + 1)
                    pool.wait_ge(v_staged, g + 1)
                    nxt = (g + 1) % GROUPS
                    stage_v(1 - parity, nxt // KV_HEADS, nxt % KV_HEADS)

        @block.vector
        def _(dve):
            def mask_unit(g, u):
                kt, h, heads = UNIT[u]
                diag = prob[kt % SLOTS][:, h:h + heads, kt * P:(kt + 1) * P]
                dve.wait_ge(expd, g * UNITS + u + 1)
                nc.vector.tensor_tensor(diag, diag, cap[:].unsqueeze(1).to_broadcast([P, heads, P]),
                                        ALU.min).then_inc(masked, 1)

            prime(dve, out_copied, *out_stored)
            nc.vector.memset(prob[0][4 * HEAD:ROWS, :, :], 0.0).then_inc(zero_made, 1)
            dve.wait_ge(zero_made, 1)
            for p in range(2):
                nc.vector.memset(v_st[p][:], 0.0).then_inc(v_blank, 1)
                nc.vector.memset(k_st[p][4 * HEAD:P, :].bitcast(F32), 0.0).then_inc(blank, 1)
                nc.vector.memset(q_st[p][4 * HEAD:P, :, :].bitcast(F32), 0.0).then_inc(blank, 1)
                dve.wait_ge(blank, 2 * p + 2)
                nc.vector.memset(k_st[p][4 * HEAD:ROWS, :].bitcast(F32), 1.0).then_inc(ones_made, 1)
                nc.vector.tensor_scalar(q_st[p][4 * HEAD:ROWS, :, :], prob[0][4 * HEAD:ROWS, :, :], 0.0,
                                        bound[4 * HEAD:ROWS, 0:1], ALU.mult, ALU.add).then_inc(ones_made, 1)
            dve.wait_ge(v_blank, 2)
            for p in range(2):
                nc.vector.memset(v_st[p][:, :, HEAD:HEAD + 1], 1.0).then_inc(v_blank, 1)
            dve.wait_ge(cap_made, 2)
            for u in range(AHEAD):
                mask_unit(0, u)
            with dve.Fori(0, GROUPS // 2) as i:
                for parity in range(2):
                    g = i * 2 + parity
                    for u in range(AHEAD, UNITS + AHEAD):
                        if u == UNITS + AHEAD - 1:
                            dve.wait_ge(weighed, (g + 1) * KT + 1)
                            dve.wait_ge(out_stored[parity], i * (STORES * DMA) + 1)
                            nc.vector.tensor_copy(o_t[parity][:], out_ps[:]).then_inc(out_copied, 1)
                        mask_unit(g + u // UNITS, u % UNITS)

        @block.tensor
        def _(pe):
            def score(parity, u):
                kt, h0, heads = UNIT[u]
                view = unit_view(ring[u % 3], kt, heads)
                for h in range(heads):
                    for a, b, _ in halves(kt):
                        last = nc.tensor.matmul(view[:, h, a - kt * P:b - kt * P],
                                                k_st[parity][:, kt * P:(kt + 1) * P],
                                                q_st[parity][:, h0 + h, a:b], start=True, stop=True)
                last.then_inc(scored, 1)

            def weigh(parity, g, kt, half):
                a, b, bank = halves(kt)[half]
                if half == 0:
                    pe.wait_ge(masked, g * UNITS + LAST[kt] + 1)
                if kt == 0 and half == 0:
                    pe.wait_ge(v_staged, g + 1)
                    pe.wait_ge(out_copied, g + 1)
                last_of_bank = (kt + 1) * P == HALF[bank][1]
                for h in range(REP):
                    last = nc.tensor.matmul(out_ps[32 * h:32 * h + VW, a:b], v_st[parity][:, kt, :],
                                            prob[kt % SLOTS][:, h, a:b], start=kt == 0, stop=last_of_bank)
                if half == len(halves(kt)) - 1:
                    last.then_inc(weighed, 1)

            prime(pe, weighed)
            pe.wait_ge(ones_made, 4)
            pe.wait_ge(v_blank, 4)
            pe.wait_ge(loaded[0], LOADS * DMA)
            for u in range(AHEAD):
                if u >= 3:
                    pe.wait_ge(expd, u - 2)
                score(0, u)
            with pe.Fori(0, GROUPS // 2) as i:
                for parity in range(2):
                    g = i * 2 + parity
                    for u in range(AHEAD, UNITS + AHEAD):
                        nxt, v = divmod(u, UNITS)
                        pe.wait_ge(expd, (g + nxt) * UNITS + LAST_IN_SLOT[v] + 1)
                        if u == UNITS:
                            pe.wait_ge(loaded[1 - parity], (i + 1 + parity) * (LOADS * DMA))
                        score(parity ^ nxt, v)
                        for kt, half in weigh_after[u]:
                            weigh(parity, g, kt, half)


def project_out(nc, x, w_o, w_gate, ident, o_s, d_s, r_s, x_s, rows, t_hi, t_lo, logits):
    with ExitStack() as c:
        sb = lambda n, s, d=F32: c.enter_context(nc.sbuf_tensor(f"po_{n}", s, d))
        sem = lambda n: c.enter_context(nc.semaphore(f"po_{n}"))
        ps = lambda n: c.enter_context(nc.psum_tensor(f"po_{n}", [P, CHUNK], F32))
        TILES = CHUNK // P
        wo, wo_hi, wo_lo = sb("wo", [P, KC, DIM]), sb("wo_hi", [P, KC, DIM], F32R), sb("wo_lo", [P, KC, DIM], F32R)
        wg, wg_hi, wg_lo = sb("wg", [P, KC, P]), sb("wg_hi", [P, KC, P], F32R), sb("wg_lo", [P, KC, P], F32R)
        den = sb("den", [P, HEADS * TOKENS // P])
        o_c = [sb(f"o_c{p}", [P, KC, CHUNK]) for p in range(2)]
        r_c = [sb(f"r_c{p}", [P, KC, CHUNK]) for p in range(2)]
        a_hi = [sb(f"a_hi{p}", [P, KC, CHUNK], F32R) for p in range(2)]
        a_lo = [sb(f"a_lo{p}", [P, KC, CHUNK], F32R) for p in range(2)]
        fresh = sb("fresh", [P, TILES, DIM])
        eps = sb("eps", [P, 1])
        stats = sb("stats", [P, TILES, 6])
        moments = sb("moments", [P, TILES, 2])
        spread = sb("spread", [P, TILES])
        scale = sb("scale", [P, TILES])
        logit_t = sb("logit_t", [P, CHUNK])
        wo_ps = [ps(f"wo_ps{t}") for t in range(TILES)]
        turn_ps = [ps(f"turn_ps{j}") for j in range(2)]
        logit_ps, back_ps = ps("logit_ps"), ps("back_ps")

        wo_in, wg_in, den_in, inv_out = sem("wo_in"), sem("wg_in"), sem("den_in"), sem("inv_out")
        o_in = [sem(f"o_in{p}") for p in range(2)]
        r_in = [sem(f"r_in{p}") for p in range(2)]
        x_in = [sem(f"x_in{p}") for p in range(2)]
        inverted, eps_made = sem("inverted"), sem("eps_made")
        w_high, w_split = sem("w_high"), sem("w_split")
        divided, a_high, a_split = sem("divided"), sem("a_high"), sem("a_split")
        projected, added, counted, averaged, rooted, scaled, normed = [
            sem(n) for n in ("projected", "added", "counted", "averaged", "rooted", "scaled", "normed")]
        turned, turned_high, turned_low = sem("turned"), sem("turned_high"), sem("turned_low")
        gated, logit_kept, logit_back, logit_done = sem("gated"), sem("logit_kept"), sem("logit_back"), sem("logit_done")
        rows_out = sem("rows_out")
        block = c.enter_context(nc.Block())

        @block.sync
        def _(sp):
            prime(sp, a_split, by=2)
            prime(sp, added, by=TILES + 1)
            sp.dma_start(den[:], d_s.rearrange("h (a b) -> (h a) b", b=den.shape[1])).then_inc(den_in, DMA)
            sp.dma_start(wo[:], w_o.rearrange("(c p) n -> p c n", p=P)).then_inc(wo_in, DMA)
            sp.dma_start(wg[:], w_gate.rearrange("(c p) n -> p c n", p=P)).then_inc(wg_in, DMA)
            sp.wait_ge(inverted, 1)
            sp.dma_start(r_s.rearrange("h (a b) -> (h a) b", b=den.shape[1]), den[:]).then_inc(inv_out, DMA)
            sp.wait_ge(inv_out, DMA)
            with sp.Fori(0, CHUNKS // 2) as i:
                for p in range(2):
                    n = i * 2 + p
                    cols = bass.ds(n * CHUNK, CHUNK)
                    sp.wait_ge(a_split, n + 1)
                    sp.dma_start(o_c[p][:], o_s.rearrange("(c h) d t -> (h d) c t", c=KC)[:, :, cols]).then_inc(o_in[p], DMA)
                    for k in range(KC):
                        heads = P // HEAD
                        sp.dma_start(r_c[p][:, k, :], r_s[k * heads:(k + 1) * heads, cols].unsqueeze(1).to_broadcast(
                            [heads, HEAD, CHUNK])).then_inc(r_in[p], DMA)
                    sp.wait_ge(added, n * TILES + 1)
                    sp.dma_start(rows[:, bass.ds(n * TILES, TILES), :], x[cols, :].rearrange("(t p) d -> p t d", p=P)
                                 ).then_inc(x_in[p], DMA)
            for n in range(CHUNKS):
                sp.wait_ge(turned_high, (n + 1) * TILES)
                sp.dma_start(x_s[n * CHUNK:(n + 1) * CHUNK, :].rearrange("(t p) d -> p t d", p=P),
                             rows[:, n * TILES:(n + 1) * TILES, :]).then_inc(rows_out, DMA)
            sp.wait_ge(rows_out, CHUNKS * DMA)

        @block.gpsimd
        def _(pool):
            with pool.Fori(0, CHUNKS // 2) as i:
                for p in range(2):
                    n = i * 2 + p
                    pool.wait_ge(o_in[p], (i + 1) * DMA)
                    pool.wait_ge(r_in[p], (i + 1) * (KC * DMA))
                    nc.gpsimd.tensor_tensor(o_c[p][:], o_c[p][:], r_c[p][:], ALU.mult).then_inc(divided, 1)

        @block.scalar
        def _(act):
            prime(act, logit_kept)
            act.wait_ge(wo_in, DMA)
            nc.scalar.activation(wo_hi[:], wo[:], ACT.Copy).then_inc(w_high, 1)
            act.wait_ge(wg_in, DMA)
            nc.scalar.activation(wg_hi[:], wg[:], ACT.Copy).then_inc(w_high, 1)
            act.wait_ge(eps_made, 1)
            with act.Fori(0, CHUNKS // 2) as i:
                for p in range(2):
                    n = i * 2 + p
                    act.wait_ge(divided, n + 1)
                    act.wait_ge(projected, n * TILES + 1)
                    nc.scalar.activation(a_hi[p][:], o_c[p][:], ACT.Copy).then_inc(a_high, 1)
                    for step in range(TILES + 1):
                        if step < TILES:
                            act.wait_ge(averaged, n * TILES + step + 1)
                            nc.scalar.activation(spread[:, step:step + 1], moments[:, step, 1:2], ACT.Sqrt,
                                                 bias=eps[:, 0:1]).then_inc(rooted, 1)
                        if step >= 1:
                            t = step - 1
                            act.wait_ge(turned, n * TILES + t + 1)
                            nc.scalar.activation(rows[:, bass.ds(n * TILES + t, 1), :], fresh[:, t:t + 1, :], ACT.Copy)
                            nc.scalar.activation(t_hi[:, :, bass.ds(n * CHUNK + t * P, P)],
                                                 turn_ps[t % 2][:].rearrange("p (k t) -> p k t", k=KC),
                                                 ACT.Copy).then_inc(turned_high, 1)
                    act.wait_ge(gated, n + 1)
                    act.wait_ge(logit_back, n + 1)
                    nc.scalar.activation(logit_t[:], logit_ps[:], ACT.Copy).then_inc(logit_kept, 1)

        @block.vector
        def _(dve):
            prime(dve, logit_done)
            prime(dve, turned_low, by=2)
            dve.wait_ge(den_in, DMA)
            nc.vector.reciprocal(den[:], den[:]).then_inc(inverted, 1)
            nc.vector.memset(eps[:], 1e-5).then_inc(eps_made, 1)
            dve.wait_ge(w_high, 1)
            nc.vector.tensor_tensor(wo_lo[:], wo[:], wo_hi[:], ALU.subtract).then_inc(w_split, 1)
            dve.wait_ge(w_high, 2)
            nc.vector.tensor_tensor(wg_lo[:], wg[:], wg_hi[:], ALU.subtract).then_inc(w_split, 1)
            with dve.Fori(0, CHUNKS // 2) as i:
                for p in range(2):
                    n = i * 2 + p
                    dve.wait_ge(a_high, n + 1)
                    nc.vector.tensor_tensor(a_lo[p][:], o_c[p][:], a_hi[p][:], ALU.subtract).then_inc(a_split, 1)
                    for step in range(TILES + 3):
                        if step < TILES:
                            t = step
                            if t == 0:
                                dve.wait_ge(x_in[p], (i + 1) * DMA)
                            dve.wait_ge(projected, n * TILES + t + 2 + TILES)
                            row = rows[:, bass.ds(n * TILES + t, 1), :].rearrange("p a d -> p (a d)")
                            nc.vector.tensor_tensor(fresh[:, t, :], wo_ps[t][:], row, ALU.add).then_inc(added, 1)
                            dve.wait_ge(added, n * TILES + t + 2 + TILES)
                            if t >= 1:
                                dve.wait_ge(counted, n * TILES + t)
                            nc.vector.bn_stats(stats[:, t, :], fresh[:, t, :]).then_inc(counted, 1)
                        if 2 <= step < TILES + 2:
                            t = step - 2
                            dve.wait_ge(rooted, n * TILES + t + 1)
                            if step == TILES:
                                dve.wait_ge(counted, n * TILES + TILES)
                            nc.vector.reciprocal(scale[:, t:t + 1], spread[:, t:t + 1]).then_inc(scaled, 1)
                        if 1 <= step <= TILES:
                            t = step - 1
                            nc.vector.bn_aggr(moments[:, t, :], stats[:, t, :]).then_inc(averaged, 1)
                        if 2 <= step < TILES + 2:
                            t = step - 2
                            dve.wait_ge(scaled, n * TILES + t + 1)
                            nc.vector.tensor_scalar(fresh[:, t, :], fresh[:, t, :], moments[:, t, 0:1], scale[:, t:t + 1],
                                                    ALU.subtract, ALU.mult).then_inc(normed, 1)
                        if step >= 3:
                            t = step - 3
                            cols = bass.ds(n * CHUNK + t * P, P)
                            dve.wait_ge(turned_high, n * TILES + t + 1)
                            nc.vector.tensor_tensor(t_lo[:, :, cols], turn_ps[t % 2][:].rearrange("p (k t) -> p k t", k=KC),
                                                    t_hi[:, :, cols], ALU.subtract).then_inc(turned_low, 1)
                    dve.wait_ge(logit_back, n + 2)
                    nc.vector.tensor_copy(logits[:, bass.ds(n * TILES, TILES), :],
                                          back_ps[:].rearrange("p (t e) -> p t e", e=P)[:, :, 0:EXPERTS]
                                          ).then_inc(logit_done, 1)

        @block.tensor
        def _(pe):
            prime(pe, logit_back)
            prime(pe, projected, by=TILES + 1)
            pe.wait_ge(w_split, 2)
            with pe.Fori(0, CHUNKS // 2) as i:
                for p in range(2):
                    n = i * 2 + p

                    def turn(t):
                        pe.wait_ge(turned_low, n * TILES + t + 1)
                        pe.wait_ge(normed, n * TILES + t + 1)
                        for k in range(KC):
                            last = nc.tensor.transpose(turn_ps[t % 2][:, k * P:(k + 1) * P],
                                                       fresh[:, t, k * P:(k + 1) * P], ident[:])
                        last.then_inc(turned, 1)

                    for t in range(TILES):
                        if t == 0:
                            pe.wait_ge(a_split, n + 3)
                        pe.wait_ge(added, n * TILES + t + 2)
                        terms = [(k, a, b) for k in range(KC) for a, b in
                                 ((a_hi[p], wo_hi), (a_hi[p], wo_lo), (a_lo[p], wo_hi))]
                        for j, (k, a, b) in enumerate(terms):
                            last = nc.tensor.matmul(wo_ps[t][:], a[:, k, t * P:(t + 1) * P], b[:, k, :], start=j == 0,
                                                    stop=j == len(terms) - 1)
                        last.then_inc(projected, 1)
                        if t >= 2:
                            turn(t - 2)
                    turn(TILES - 2)
                    turn(TILES - 1)
                    pe.wait_ge(turned_low, (n + 1) * TILES + 2)
                    pe.wait_ge(logit_kept, n + 1)
                    cols = bass.ds(n * CHUNK, CHUNK)
                    terms = [(k, a, b) for k in range(KC) for a, b in ((wg_hi, t_hi), (wg_hi, t_lo), (wg_lo, t_hi))]
                    for j, (k, a, b) in enumerate(terms):
                        last = nc.tensor.matmul(logit_ps[:], a[:, k, :], b[:, k, cols], start=j == 0,
                                                stop=j == len(terms) - 1)
                    last.then_inc(gated, 1)
                    pe.wait_ge(logit_kept, n + 2)
                    pe.wait_ge(logit_done, n + 1)
                    for t in range(TILES):
                        last = nc.tensor.transpose(back_ps[:, t * P:(t + 1) * P], logit_t[:, t * P:(t + 1) * P],
                                                   ident[:])
                    last.then_inc(logit_back, 1)
            pe.wait_ge(logit_done, CHUNKS + 1)


def shared_expert(nc, w_gate_up, w_down, rows, t_hi, t_lo):
    with ExitStack() as c:
        sb = lambda n, s, d=F32: c.enter_context(nc.sbuf_tensor(f"ff_{n}", s, d))
        sem = lambda n: c.enter_context(nc.semaphore(f"ff_{n}"))
        ps = lambda n: c.enter_context(nc.psum_tensor(f"ff_{n}", [P, CHUNK], F32))
        TILES = CHUNK // P
        GU = 2 * INTER
        w_gu = [sb(f"w_gu{p}", [P, KC, GU]) for p in range(2)]
        w_dn = [sb(f"w_dn{p}", [P, DIM]) for p in range(2)]
        gu_hi = [sb(f"gu_hi{p}", [P, KC, GU], F32R) for p in range(2)]
        gu_lo = [sb(f"gu_lo{p}", [P, KC, GU], F32R) for p in range(2)]
        dn_hi = [sb(f"dn_hi{p}", [P, DIM], F32R) for p in range(2)]
        dn_lo = [sb(f"dn_lo{p}", [P, DIM], F32R) for p in range(2)]
        gate = [sb(f"gate{j}", [P, CHUNK]) for j in range(2)]
        act_f = [sb(f"act_f{j}", [P, CHUNK]) for j in range(2)]
        act_hi = [sb(f"act_hi{j}", [P, CHUNK], F32R) for j in range(2)]
        act_lo = [sb(f"act_lo{j}", [P, CHUNK], F32R) for j in range(2)]
        gate_ps = [ps(f"gate_ps{j}") for j in range(2)]
        up_ps = [ps(f"up_ps{j}") for j in range(2)]
        y_ps = [ps(f"y_ps{t}") for t in range(TILES)]

        w_in = [sem(f"w_in{p}") for p in range(2)]
        w_high, w_split = sem("w_high"), sem("w_split")
        gated, upped, silued = sem("gated"), sem("upped"), sem("silued")
        acted, act_high, act_split = sem("acted"), sem("act_high"), sem("act_split")
        downed, added = sem("downed"), sem("added")
        LOADS = 2
        block = c.enter_context(nc.Block())

        @block.sync
        def _(sp):
            prime(sp, w_split, by=2)
            with sp.Fori(0, SHARED // 2) as i:
                for p in range(2):
                    e = i * 2 + p
                    sp.wait_ge(w_split, e + 1)
                    sp.dma_start(w_gu[p][:], w_gate_up[bass.ds(e, 1)].rearrange("e (k p) n -> p (e k) n", p=P)
                                 ).then_inc(w_in[p], DMA)
                    sp.dma_start(w_dn[p][:], w_down[bass.ds(e, 1)].rearrange("e p n -> p (e n)")).then_inc(w_in[p], DMA)

        @block.scalar
        def _(act):
            prime(act, silued, by=2)

            def high_weights(p, e, pair):
                act.wait_ge(w_in[p], (pair + 1) * (LOADS * DMA))
                act.wait_ge(downed, e * (CHUNKS * TILES) + 1)
                nc.scalar.activation(gu_hi[p][:], w_gu[p][:], ACT.Copy)
                nc.scalar.activation(dn_hi[p][:], w_dn[p][:], ACT.Copy).then_inc(w_high, 1)

            def pair_of_parts(i, final=False):
                for p in range(2):
                    e = i * 2 + p
                    for n in range(CHUNKS):
                        j = n % 2
                        u = e * CHUNKS + n
                        act.wait_ge(gated, u + 1)
                        act.wait_ge(acted, u + 1)
                        nc.scalar.activation(gate[j][:], gate_ps[j][:], ACT.Silu).then_inc(silued, 1)
                        act.wait_ge(acted, u + 3)
                        act.wait_ge(downed, u * TILES + (CHUNKS - 1) * TILES + 1)
                        nc.scalar.activation(act_hi[j][:], act_f[j][:], ACT.Copy).then_inc(act_high, 1)
                        if n == 1 and not (final and p == 1):
                            high_weights(1 - p, e + 1, i + p)

            high_weights(0, 0, 0)
            with act.Fori(0, SHARED // 2 - 1) as i:
                pair_of_parts(i)
            pair_of_parts(SHARED // 2 - 1, final=True)

        @block.gpsimd
        def _(pool):
            with pool.Fori(0, SHARED // 2) as i:
                for p in range(2):
                    pool.wait_ge(w_high, i * 2 + p + 1)
                    nc.gpsimd.tensor_tensor(gu_lo[p][:], w_gu[p][:], gu_hi[p][:], ALU.subtract)
                    nc.gpsimd.tensor_tensor(dn_lo[p][:], w_dn[p][:], dn_hi[p][:], ALU.subtract).then_inc(w_split, 1)

        @block.vector
        def _(dve):
            prime(dve, acted, by=2)
            prime(dve, added, by=TILES)
            with dve.Fori(0, SHARED // 2) as i:
                for p in range(2):
                    for n in range(CHUNKS):
                        j = n % 2
                        u = (i * 2 + p) * CHUNKS + n
                        dve.wait_ge(upped, u + 1)
                        dve.wait_ge(silued, u + 3)
                        nc.vector.tensor_tensor(act_f[j][:], up_ps[j][:], gate[j][:], ALU.mult).then_inc(acted, 1)
                        dve.wait_ge(act_high, u + 1)
                        nc.vector.tensor_tensor(act_lo[j][:], act_f[j][:], act_hi[j][:], ALU.subtract).then_inc(act_split, 1)
                        for t in range(TILES):
                            row = rows[:, n * TILES + t, :]
                            dve.wait_ge(downed, u * TILES + t + 2 + CHUNKS * TILES)
                            nc.vector.tensor_tensor(row, row, y_ps[t][:], ALU.add).then_inc(added, 1)
            dve.wait_ge(added, SHARED * CHUNKS * TILES + TILES)

        @block.tensor
        def _(pe):
            prime(pe, downed, by=CHUNKS * TILES + 1)

            def gate_and_up(p, e, n):
                j = n % 2
                u = e * CHUNKS + n
                if n == 0:
                    pe.wait_ge(w_split, e + 3)
                cols = slice(n * CHUNK, (n + 1) * CHUNK)
                for bank, first, done in ((gate_ps[j], 0, gated), (up_ps[j], INTER, upped)):
                    if done is gated:
                        pe.wait_ge(silued, u + 1)
                    else:
                        pe.wait_ge(acted, u + 1)
                    terms = [(k, a, b) for k in range(KC) for a, b in
                             ((gu_hi[p], t_hi), (gu_hi[p], t_lo), (gu_lo[p], t_hi))]
                    for m, (k, a, b) in enumerate(terms):
                        last = nc.tensor.matmul(bank[:], a[:, k, first:first + INTER], b[:, k, cols], start=m == 0,
                                                stop=m == len(terms) - 1)
                    last.then_inc(done, 1)

            def down(p, e, n):
                j = n % 2
                u = e * CHUNKS + n
                pe.wait_ge(act_split, u + 1)
                for t in range(TILES):
                    pe.wait_ge(added, u * TILES + t + 1)
                    terms = ((act_hi[j], dn_hi[p]), (act_hi[j], dn_lo[p]), (act_lo[j], dn_hi[p]))
                    for m, (a, b) in enumerate(terms):
                        last = nc.tensor.matmul(y_ps[t][:], a[:, t * P:(t + 1) * P], b[:], start=m == 0, stop=m == 2)
                    last.then_inc(downed, 1)

            def pair_of_parts(i, final=False):
                for p in range(2):
                    e = i * 2 + p
                    for n in range(CHUNKS):
                        if n + 1 < CHUNKS:
                            gate_and_up(p, e, n + 1)
                        elif not (final and p == 1):
                            gate_and_up(1 - p, e + 1, 0)
                        down(p, e, n)

            gate_and_up(0, 0, 0)
            with pe.Fori(0, SHARED // 2 - 1) as i:
                pair_of_parts(i)
            pair_of_parts(SHARED // 2 - 1, final=True)


def route(nc, logits, slots, weights, table, owner):
    with ExitStack() as c:
        T = TOKENS // P
        TE = [P, T, EXPERTS]
        sb = lambda n, s, d=F32: c.enter_context(nc.sbuf_tensor(f"ro_{n}", s, d))
        sem = lambda n: c.enter_context(nc.semaphore(f"ro_{n}"))
        order, eq, cand, first, second, place = [sb(n, TE) for n in ("order", "eq", "cand", "first", "second", "place")]
        mask = sb("mask", TE, BF16)
        top, pick, low_top, total, inv_total = [sb(n, [P, T]) for n in ("top", "pick", "low_top", "total", "inv_total")]
        earlier, every = sb("earlier", [P, P], BF16), sb("every", [P, P], BF16)
        limits = sb("limits", [P, EXPERTS, T])
        before = sb("before", [P, EXPERTS, EXPERTS])
        over, shift = sb("over", [P, EXPERTS, T]), sb("shift", [P, EXPERTS, EXPERTS])
        tiles, start, end, base = [sb(n, [P, EXPERTS]) for n in ("tiles", "start", "end", "base")]
        tile_no = sb("tile_no", [P, SLOT_TILES, EXPERTS])
        past = sb("past", [P, SLOT_TILES, EXPERTS])
        owner_f = sb("owner_f", [P, SLOT_TILES])
        slot_f, tile_f, lane_f = [sb(n, [P, 2 * T]) for n in ("slot_f", "tile_f", "lane_f")]
        tile_i = sb("tile_i", [P, 2 * T], I32)
        lane_no, slot_tile = sb("lane_no", [P, 1, P]), sb("slot_tile", [P, 1, SLOT_TILES])
        token, token_tile = sb("token", [P, 1]), sb("token_tile", [P, 2, T])
        in_lane = sb("in_lane", [P, 2 * T, P], BF16)
        in_tile = sb("in_tile", [P, 2 * T, SLOT_TILES])
        by_token = sb("by_token", [P, 2 * T, 2, SLOT_TILES], BF16)
        high_id = sb("high_id", [P, SLOT_TILES])
        rank_ps = c.enter_context(nc.psum_tensor("ro_rank_ps", [P, T, EXPERTS], F32))
        count_ps = c.enter_context(nc.psum_tensor("ro_count_ps", [P, EXPERTS], F32))
        table_ps = c.enter_context(nc.psum_tensor("ro_table_ps", [P, 2, SLOT_TILES], F32))
        made, lowered, exped, chosen = sem("made"), sem("lowered"), sem("exped"), sem("chosen")
        masked, ranked, spread, tabled = sem("masked"), sem("ranked"), sem("spread"), sem("tabled")
        block = c.enter_context(nc.Block())

        @block.gpsimd
        def _(pool):
            CONSTANTS = 0

            def make(made_by):
                nonlocal CONSTANTS
                CONSTANTS += 1
                made_by.then_inc(made, 1)
                pool.wait_ge(made, CONSTANTS)

            def count_up(tile, pattern, base=0, lanes=0):
                make(nc.gpsimd.iota(tile[:], pattern=pattern, base=base, channel_multiplier=lanes,
                                    allow_small_or_imprecise_dtypes=True))

            count_up(order, [[0, T], [-1, EXPERTS]], base=EXPERTS)
            for ones in (every, earlier, before):
                make(nc.gpsimd.memset(ones[:], 1.0))
            make(nc.gpsimd.affine_select(out=earlier[:], in_=earlier[:], compare_op=ALU.is_ge, fill=0.0, base=-1,
                                         pattern=[[1, P]], channel_multiplier=-1))
            make(nc.gpsimd.affine_select(out=before[:], in_=before[:], compare_op=ALU.is_ge, fill=0.0, base=-1,
                                         pattern=[[1, EXPERTS], [-1, EXPERTS]], channel_multiplier=0))
            count_up(limits, [[0, EXPERTS], [P, T]])
            count_up(tile_no, [[1, SLOT_TILES], [0, EXPERTS]])
            count_up(lane_no, [[0, 1], [1, P]])
            count_up(slot_tile, [[0, 1], [1, SLOT_TILES]])
            count_up(token, [[0, 1]], lanes=1)
            count_up(token_tile, [[0, 2], [1, T]])

        CONSTANTS = 12

        @block.scalar
        def _(act):
            act.wait_ge(lowered, 1)
            nc.scalar.activation(logits[:], logits[:], ACT.Exp).then_inc(exped, 1)

        @block.vector
        def _(dve):
            done = 0

            def step(made_by):
                nonlocal done
                done += 1
                made_by.then_inc(chosen, 1)
                dve.wait_ge(chosen, done)

            tt, reduce = nc.vector.tensor_tensor, nc.vector.tensor_reduce
            wide = lambda v, shape=TE: v.unsqueeze(2).to_broadcast(shape)
            tall = lambda v, shape=TE: v.unsqueeze(1).to_broadcast(shape)

            def pick_largest(value, best, hot):
                step(reduce(best[:], value[:], AX.X, ALU.max))
                step(tt(eq[:], value[:], wide(best[:]), ALU.is_equal))
                step(tt(cand[:], eq[:], order[:], ALU.mult))
                step(reduce(pick[:], cand[:], AX.X, ALU.max))
                step(tt(hot[:], cand[:], wide(pick[:]), ALU.is_equal))

            dve.wait_ge(made, CONSTANTS)
            step(reduce(top[:], logits[:], AX.X, ALU.max))
            tt(logits[:], logits[:], wide(top[:]), ALU.subtract).then_inc(lowered, 1)
            dve.wait_ge(exped, 1)
            pick_largest(logits, top, first)
            step(nc.vector.tensor_scalar(eq[:], first[:], 2.0, None, ALU.mult))
            step(tt(logits[:], logits[:], eq[:], ALU.subtract))
            pick_largest(logits, low_top, second)
            tt(mask[:], first[:], second[:], ALU.add).then_inc(masked, 1)
            step(tt(total[:], top[:], low_top[:], ALU.add))
            step(nc.vector.reciprocal(inv_total[:], total[:]))
            step(tt(weights[:, 0, :], top[:], inv_total[:], ALU.mult))
            step(tt(weights[:, 1, :], low_top[:], inv_total[:], ALU.mult))
            dve.wait_ge(ranked, 2)
            step(tt(over[:], wide(count_ps[:], over.shape), limits[:], ALU.is_gt))
            step(reduce(tiles[:], over[:], AX.X, ALU.add))
            step(tt(shift[:], tall(tiles[:], shift.shape), before[:], ALU.mult))
            step(reduce(start[:], shift[:], AX.X, ALU.add))
            step(nc.vector.tensor_scalar(base[:], start[:], float(P), None, ALU.mult))
            step(tt(place[:], rank_ps[:], tall(base[:]), ALU.add))
            for choice, hot in enumerate((first, second)):
                step(tt(cand[:], hot[:], place[:], ALU.mult))
                step(reduce(slot_f[:, choice * T:(choice + 1) * T], cand[:], AX.X, ALU.add))
            step(nc.vector.tensor_copy(slots[:], slot_f[:]))
            step(nc.vector.tensor_scalar(tile_i[:], slots[:], 7, None, ALU.arith_shift_right))
            step(nc.vector.tensor_copy(tile_f[:], tile_i[:]))
            step(nc.vector.tensor_scalar(lane_f[:], tile_f[:], float(-P), None, ALU.mult))
            step(tt(lane_f[:], lane_f[:], slot_f[:], ALU.add))
            step(tt(in_tile[:], tall(slot_tile[:, 0, :], in_tile.shape), wide(tile_f[:], in_tile.shape), ALU.is_equal))
            step(tt(in_lane[:], tall(lane_no[:, 0, :], in_lane.shape), wide(lane_f[:], in_lane.shape), ALU.is_equal))
            step(nc.vector.tensor_scalar(by_token[:, :, 0, :], in_tile[:], token[:, 0:1], None, ALU.mult))
            tt(by_token[:, :, 1, :], in_tile[:], wide(token_tile[:].rearrange("p c t -> p (c t)"), in_tile.shape), ALU.mult
               ).then_inc(spread, 1)
            step(tt(end[:], start[:], tiles[:], ALU.add))
            step(tt(past[:], tile_no[:], tall(end[:], past.shape), ALU.is_ge))
            step(reduce(owner_f[:], past[:], AX.X, ALU.add))
            step(nc.vector.tensor_scalar(owner_f[:], owner_f[:], float(EXPERTS - 1), None, ALU.min))
            step(nc.vector.tensor_copy(owner[:], owner_f[:]))
            dve.wait_ge(tabled, 1)
            step(nc.vector.tensor_scalar(high_id[:], table_ps[:, 1, :], float(P), None, ALU.mult))
            step(tt(high_id[:], high_id[:], table_ps[:, 0, :], ALU.add))
            step(nc.vector.tensor_copy(table[:], high_id[:]))

        @block.tensor
        def _(pe):
            pe.wait_ge(made, CONSTANTS)
            pe.wait_ge(masked, 1)
            nc.tensor.matmul(rank_ps[:].rearrange("p t e -> p (t e)"), earlier[:], mask[:].rearrange("p t e -> p (t e)"),
                             start=True, stop=False)
            for back in range(1, T):
                last = nc.tensor.matmul(rank_ps[:, back:, :].rearrange("p t e -> p (t e)"), every[:],
                                        mask[:, 0:T - back, :].rearrange("p t e -> p (t e)"), start=False,
                                        stop=back == T - 1)
            last.then_inc(ranked, 1)
            for t in range(T):
                last = nc.tensor.matmul(count_ps[:], every[:], mask[:, t, :], start=t == 0, stop=t == T - 1)
            last.then_inc(ranked, 1)
            pe.wait_ge(spread, 1)
            for t in range(2 * T):
                last = nc.tensor.matmul(table_ps[:].rearrange("p a n -> p (a n)"), in_lane[:, t, :],
                                        by_token[:, t].rearrange("p a n -> p (a n)"), start=t == 0, stop=t == 2 * T - 1)
            last.then_inc(tabled, 1)


def experts(nc, w_gate_up, w_down, ident, x_s, y_s, rows, slots, weights, table, owner, out):
    with ExitStack() as c:
        T = TOKENS // P
        DEPTH = 4
        sb = lambda n, s, d=F32: c.enter_context(nc.sbuf_tensor(f"ex_{n}", s, d))
        sem = lambda n: c.enter_context(nc.semaphore(f"ex_{n}"))
        ps = lambda n, w: c.enter_context(nc.psum_tensor(f"ex_{n}", [P, w], F32))
        w_gu = sb("w_gu", [P, EXPERTS, KC, 2 * INTER])
        w_dn = sb("w_dn", [P, EXPERTS, DIM])
        x_g = [sb(f"x_g{j}", [P, DIM]) for j in range(DEPTH)]
        x_t = [sb(f"x_t{j}", [P, KC, P]) for j in range(2)]
        gate = [sb(f"gate{j}", [P, INTER]) for j in range(2)]
        acts = [sb(f"acts{j}", [P, INTER]) for j in range(2)]
        acts_t = [sb(f"acts_t{j}", [P, P]) for j in range(2)]
        y = [sb(f"y{j}", [P, DIM]) for j in range(DEPTH)]
        y_g = [sb(f"y_g{j}", [P, DIM]) for j in range(2 * DEPTH)]
        eps = sb("eps", [P, 1])
        stats, moments = sb("stats", [P, T, 6]), sb("moments", [P, T, 2])
        spread, scale = sb("spread", [P, T]), sb("scale", [P, T])
        x_ps = [ps(f"x_ps{j}", DIM) for j in range(2)]
        gu_ps = [ps(f"gu_ps{j}", CHUNK) for j in range(2)]
        t_ps = [ps(f"t_ps{j}", CHUNK) for j in range(2)]
        y_ps = [ps(f"y_ps{j}", DIM) for j in range(2)]
        w_in = sem("w_in")
        gathered = [sem(f"gathered{j}") for j in range(DEPTH)]
        stored = [sem(f"stored{j}") for j in range(DEPTH)]
        turned, kept, gated, silued, acted = [sem(n) for n in ("turned", "kept", "gated", "silued", "acted")]
        act_turned, act_kept, downed, y_kept = [sem(n) for n in ("act_turned", "act_kept", "downed", "y_kept")]
        returned = [sem(f"returned{j}") for j in range(2 * DEPTH)]
        summed, eps_made, counted, averaged, rooted, scaled, normed = [
            sem(n) for n in ("summed", "eps_made", "counted", "averaged", "rooted", "scaled", "normed")]
        finished = sem("finished")
        block = c.enter_context(nc.Block())

        @block.sync
        def _(sp):
            prime(sp, *stored)
            for e in range(EXPERTS):
                sp.dma_start(w_gu[:, e], w_gate_up[SHARED + e].rearrange("(k p) n -> p k n", p=P)).then_inc(w_in, DMA)
                sp.dma_start(w_dn[:, e], w_down[SHARED + e]).then_inc(w_in, DMA)
            with sp.Fori(0, SLOT_TILES // DEPTH) as i:
                for j in range(DEPTH):
                    tile = i * DEPTH + j
                    sp.wait_ge(y_kept, tile + 3)
                    sp.dma_start(y_s[bass.ds(tile * P, P), :], y[j][:]).then_inc(stored[j], DMA)
            for t in range(T):
                sp.wait_ge(normed, t + 1)
                sp.dma_start(out[t * P:(t + 1) * P, :], rows[:, t, :]).then_inc(finished, DMA)
            sp.wait_ge(finished, T * DMA)

        @block.gpsimd
        def _(pool):
            nc.gpsimd.memset(eps[:], 1e-5).then_inc(eps_made, 1)
            for tile in range(SLOT_TILES):
                if tile >= DEPTH:
                    pool.wait_ge(turned, tile - DEPTH + 1)
                nc.gpsimd.indirect_dma_start(x_g[tile % DEPTH][:], None, x_s[:], bass.IndirectOffsetOnAxis(
                    ap=table[:, tile:tile + 1], axis=0)).then_inc(gathered[tile % DEPTH], DMA)
            for j in range(DEPTH):
                pool.wait_ge(stored[j], SLOT_TILES // DEPTH * DMA + 1)
            for t in range(T):
                for choice in range(2):
                    n = 2 * t + choice
                    if n >= 2 * DEPTH:
                        pool.wait_ge(summed, n - 2 * DEPTH + 1)
                    at = choice * T + t
                    nc.gpsimd.indirect_dma_start(y_g[n % (2 * DEPTH)][:], None, y_s[:], bass.IndirectOffsetOnAxis(
                        ap=slots[:, at:at + 1], axis=0)).then_inc(returned[n % (2 * DEPTH)], DMA)

        @block.scalar
        def _(act):
            prime(act, kept, by=2)
            with act.Fori(0, SLOT_TILES // DEPTH) as i:
                for j in range(DEPTH):
                    tile = i * DEPTH + j
                    b = j % 2
                    act.wait_ge(turned, tile + 1)
                    act.wait_ge(gated, tile + 1)
                    nc.scalar.activation(x_t[b][:], x_ps[b][:].rearrange("p (k t) -> p k t", k=KC), ACT.Copy).then_inc(kept, 1)
                    act.wait_ge(gated, tile + 3)
                    act.wait_ge(acted, tile + 1)
                    nc.scalar.activation(gate[b][:], gu_ps[b][:, 0:INTER], ACT.Silu).then_inc(silued, 1)
            act.wait_ge(eps_made, 1)
            act.wait_ge(averaged, T)
            nc.scalar.activation(spread[:], moments[:, :, 1], ACT.Sqrt, bias=eps[:, 0:1]).then_inc(rooted, 1)

        @block.vector
        def _(dve):
            prime(dve, acted, y_kept, act_kept, by=2)
            with dve.Fori(0, SLOT_TILES // DEPTH) as i:
                for j in range(DEPTH):
                    tile = i * DEPTH + j
                    b = j % 2
                    dve.wait_ge(silued, tile + 1)
                    dve.wait_ge(act_turned, tile + 1)
                    nc.vector.tensor_tensor(acts[b][:], gu_ps[b][:, INTER:2 * INTER], gate[b][:], ALU.mult).then_inc(acted, 1)
                    dve.wait_ge(act_turned, tile + 3)
                    dve.wait_ge(downed, tile + 1)
                    nc.vector.tensor_copy(acts_t[b][:], t_ps[b][:, 0:P]).then_inc(act_kept, 1)
                    dve.wait_ge(downed, tile + 3)
                    dve.wait_ge(stored[j], i * DMA + 1)
                    nc.vector.tensor_copy(y[j][:], y_ps[b][:]).then_inc(y_kept, 1)
            for t in range(T):
                for choice in range(2):
                    n = 2 * t + choice
                    dve.wait_ge(returned[n % (2 * DEPTH)], (n // (2 * DEPTH) + 1) * DMA)
                    if choice:
                        dve.wait_ge(summed, n)
                    nc.vector.scalar_tensor_tensor(rows[:, t, :], y_g[n % (2 * DEPTH)][:], weights[:, choice, t:t + 1],
                                                   rows[:, t, :], ALU.mult, ALU.add).then_inc(summed, 1)
                dve.wait_ge(summed, 2 * t + 2)
                nc.vector.bn_stats(stats[:, t, :], rows[:, t, :]).then_inc(counted, 1)
            for t in range(T):
                dve.wait_ge(counted, t + 1)
                nc.vector.bn_aggr(moments[:, t, :], stats[:, t, :]).then_inc(averaged, 1)
            dve.wait_ge(rooted, 1)
            nc.vector.reciprocal(scale[:], spread[:]).then_inc(scaled, 1)
            dve.wait_ge(scaled, 1)
            for t in range(T):
                nc.vector.tensor_scalar(rows[:, t, :], rows[:, t, :], moments[:, t, 0:1], scale[:, t:t + 1],
                                        ALU.subtract, ALU.mult).then_inc(normed, 1)

        @block.tensor
        def _(pe):
            prime(pe, gated, act_turned, downed, by=2)

            def turn(j, tile, i):
                pe.wait_ge(gathered[j], (i + 1) * DMA)
                pe.wait_ge(kept, tile + 1)
                for k in range(KC):
                    last = nc.tensor.transpose(x_ps[j % 2][:, k * P:(k + 1) * P], x_g[j][:, k * P:(k + 1) * P], ident[:])
                last.then_inc(turned, 1)

            def turn_acts(b, tile):
                pe.wait_ge(acted, tile + 3)
                pe.wait_ge(act_kept, tile + 1)
                nc.tensor.transpose(t_ps[b][:, 0:P], acts[b][:], ident[:]).then_inc(act_turned, 1)

            def gate_and_up(b, tile, e):
                pe.wait_ge(kept, tile + 3)
                pe.wait_ge(acted, tile + 1)
                for k in range(KC):
                    last = nc.tensor.matmul(gu_ps[b][:, 0:2 * INTER], x_t[b][:, k, :],
                                            w_gu[:, bass.ds(e, 1), k, :].rearrange("p e n -> p (e n)"), start=k == 0,
                                            stop=k == KC - 1)
                last.then_inc(gated, 1)

            def down(b, tile, e):
                pe.wait_ge(act_kept, tile + 3)
                pe.wait_ge(y_kept, tile + 1)
                nc.tensor.matmul(y_ps[b][:], acts_t[b][:], w_dn[:, bass.ds(e, 1), :].rearrange("p e n -> p (e n)"),
                                 start=True, stop=True).then_inc(downed, 1)

            def owner_of(tile):
                return pe.value_load(owner[0:1, bass.ds(tile, 1)], min_val=0, max_val=EXPERTS - 1)

            def group(i, final=False):
                for j in range(DEPTH):
                    tile = i * DEPTH + j
                    e = owner_of(tile)
                    gate_and_up(j % 2, tile, e)
                    if not (final and j == DEPTH - 1):
                        turn((j + 1) % DEPTH, tile + 1, i + (j + 1) // DEPTH)
                    turn_acts(j % 2, tile)
                    down(j % 2, tile, e)

            pe.wait_ge(w_in, 2 * EXPERTS * DMA)
            turn(0, 0, 0)
            with pe.Fori(0, SLOT_TILES // DEPTH - 1) as i:
                group(i)
            group(SLOT_TILES // DEPTH - 1, final=True)


def layer(nc, ins, out):
    with ExitStack() as c:
        dram = lambda n, *s: nc.dram_tensor(n, s, F32).ap()
        q_s, k_s = dram("q_scratch", HEADS, 2, HEAD, TOKENS), dram("k_scratch", KV_HEADS, 2, HEAD, TOKENS)
        m_s = dram("m_scratch", HEADS, 2, TOKENS)
        o_s, d_s, r_s = dram("o_scratch", HEADS, HEAD, TOKENS), dram("d_scratch", HEADS, TOKENS), dram("r_scratch", HEADS, TOKENS)
        x_s, y_s = dram("x_scratch", TOKENS, DIM), dram("y_scratch", SLOT_TILES * P, DIM)
        sb = lambda n, s, d=F32: c.enter_context(nc.sbuf_tensor(n, s, d))
        ident = sb("ident", [P, P])
        bound = sb("bound", [P, 1])
        with nc.sbuf_tensor("values", [P, TOKENS // P, P], F32) as values:
            project_qkv(nc, ins["x_t"], ins["w_qkv"], ins["cos"], ins["sin"], ins["ident"], q_s, k_s, m_s, values, ident,
                        bound)
            attend(nc, q_s, k_s, m_s, values, bound, o_s, d_s)
        rows = sb("rows", [P, TOKENS // P, DIM])
        logits = sb("logits", [P, TOKENS // P, EXPERTS])
        slots = sb("slots", [P, 2 * TOKENS // P], I32)
        weights = sb("weights", [P, 2, TOKENS // P])
        table = sb("table", [P, SLOT_TILES], I32)
        owner = sb("owner", [P, SLOT_TILES], I32)
        with nc.sbuf_tensor("t_hi", [P, KC, TOKENS], F32R) as t_hi, nc.sbuf_tensor("t_lo", [P, KC, TOKENS], F32R) as t_lo:
            project_out(nc, ins["x"], ins["w_o"], ins["w_gate"], ident, o_s, d_s, r_s, x_s, rows, t_hi, t_lo, logits)
            route(nc, logits, slots, weights, table, owner)
            shared_expert(nc, ins["w_gate_up"], ins["w_down"], rows, t_hi, t_lo)
        experts(nc, ins["w_gate_up"], ins["w_down"], ident, x_s, y_s, rows, slots, weights, table, owner, out)


def arrange(a):
    import numpy as np
    f = lambda n: np.asarray(a[n])
    x = f("L0_attn_x").reshape(TOKENS, DIM)
    w_q = f("L0_attn_Wq").reshape(DIM, SETS, SET_HEADS * PAIRS, 2)
    w_k = f("L0_attn_Wk").reshape(DIM, KV_HEADS * PAIRS, 2)
    cols = [w_k[:, :, 0], w_k[:, :, 0], w_k[:, :, 1], w_k[:, :, 1]]
    for s in range(SETS):
        cols += [w_q[:, s, :, 0], w_q[:, s, :, 1]]
    cols.append(f("L0_attn_Wv"))
    inv_freq = (1.0 / np.float32(10000.0) ** (np.arange(0, HEAD, 2, dtype=np.float32) / np.float32(HEAD))).astype(np.float32)
    ang = np.arange(SEQ, dtype=np.float32)[None, :] * np.tile(inv_freq, SET_HEADS)[:, None]
    gate = np.zeros((DIM, P), np.float32)
    gate[:, :EXPERTS] = f("L0_ffn_gate_w").T
    shared = f("L0_ffn_shared_w_gate_up").reshape(2, SHARED, INTER, DIM).transpose(1, 3, 0, 2).reshape(SHARED, DIM, 2 * INTER)
    shared_down = f("L0_ffn_shared_w_down").reshape(DIM, SHARED, INTER).transpose(1, 2, 0)
    t = np.ascontiguousarray
    return {
        "x": t(x), "x_t": t(x.T), "w_qkv": np.concatenate(cols, axis=1),
        "cos": np.cos(ang).astype(np.float32), "sin": np.sin(ang).astype(np.float32),
        "ident": np.eye(P, dtype=np.float32),
        "w_o": t(f("L0_attn_Wo")), "w_gate": gate,
        "w_gate_up": np.concatenate([shared, f("L0_ffn_w_gate_up").transpose(0, 2, 1)]),
        "w_down": np.concatenate([shared_down, f("L0_ffn_w_down").transpose(0, 2, 1)]),
    }


def kernel(**inputs):
    import concourse.bacc as bacc
    from concourse.bass_utils import run_bass_kernel_spmd as run

    nc = bacc.Bacc("TRN2", target_bir_lowering=False, num_devices=1)
    arrays = arrange(inputs)
    ins = {n: nc.dram_tensor(f"in_{n}", v.shape, mybir.dt.from_np(v.dtype), kind="ExternalInput").ap() for n, v in arrays.items()}
    out = nc.dram_tensor("out", (TOKENS, DIM), F32, kind="ExternalOutput").ap()
    layer(nc, ins, out)
    r = run(nc, [{f"in_{n}": v for n, v in arrays.items()}], core_ids=[0])
    return r.results[0]["out"].reshape(BATCH, SEQ, DIM)
```

```python
from contextlib import ExitStack

import concourse.bass as bass
from concourse import mybir

F32 = mybir.dt.float32
F32R = mybir.dt.float32r
BF16 = mybir.dt.bfloat16
I32 = mybir.dt.int32
ALU = mybir.AluOpType
ACT = mybir.ActivationFunctionType
AX = mybir.AxisListType

P = 128
BATCH, SEQ, DIM = 2, 1024, 512
TOKENS = BATCH * SEQ
HEADS, KV_HEADS, HEAD = 32, 8, 16
REP = HEADS // KV_HEADS
PAIRS = HEAD // 2
KC = DIM // P
CHUNK = 512
CHUNKS = TOKENS // CHUNK
KT = SEQ // P
GROUPS = BATCH * KV_HEADS
SETS = HEADS * PAIRS // P
SET_HEADS = P // PAIRS
COLS = 7
SCALE = HEAD ** -0.5
VW = 32
EXPERTS, INTER = 16, 128
SHARED = 512 // INTER
SLOT_TILES = 2 * TOKENS // P + EXPERTS
SAFE_NORM = 160.0
BOUND_ROW = 4 * HEAD + 2
AHEAD_K = 2
LARGEST = 3.4028234663852886e38
DMA = 16


def prime(eng, *sems, by=1):
    for s in sems:
        eng.sem_inc(s, by)


def project_qkv(nc, x_t, w_qkv, cos, sin, ident_dram, q_s, k_s, m_s, values, ident, bound, loose):
    with ExitStack() as c:
        sb = lambda n, s, d=F32: c.enter_context(nc.sbuf_tensor(n, s, d))
        sem = lambda n: c.enter_context(nc.semaphore(n))
        w = sb("w", [P, KC, COLS * P])
        w_hi = sb("w_hi", [P, KC, COLS * P], F32R)
        w_lo = sb("w_lo", [P, KC, COLS * P], F32R)
        xs = [sb(f"x{n}", [P, KC, CHUNK]) for n in range(2)]
        x_hi = sb("x_hi", [P, KC, TOKENS], F32R)
        x_lo = sb("x_lo", [P, KC, TOKENS], F32R)
        cos_s = sb("cos_s", [P, SEQ])
        sin_s = sb("sin_s", [P, SEQ])
        prod = sb("prod", [P, 4, CHUNK])
        rot = sb("rot", [P, 2, CHUNK])
        parts = sb("parts", [P, SETS + 1, 2, 2, CHUNK], F32R)
        v_t = sb("v_t", [P, TOKENS])
        sq = sb("sq", [P, 2, CHUNK], BF16)
        sum_heads = sb("sum_heads", [P, 32], BF16)
        norm = sb("norm", [P, CHUNK])
        norm_hi = sb("norm_hi", [P, CHUNK], F32R)
        norm_lo = sb("norm_lo", [P, CHUNK], F32R)
        least = sb("least", [P, CHUNKS])
        least_row = sb("least_row", [P, 1])
        k_one, all_one = sb("k_one", [1, 1]), sb("all_one", [1, 1])
        ones_row = sb("ones_row", [1, P])
        less_one = sb("less_one", [P, 1])
        acc = [c.enter_context(nc.psum_tensor(f"acc{j}", [P, CHUNK], F32)) for j in range(COLS)]
        small = c.enter_context(nc.psum_tensor("small", [P, CHUNK], F32))

        w_in, x_in, table_in, ident_in = [sem(f"w_in{j}") for j in range(SETS + 2)], [sem("x_in0"), sem("x_in1")], sem("table_in"), sem("ident_in")
        w_high, w_split, x_high, x_split = sem("w_high"), sem("w_split"), sem("x_high"), sem("x_split")
        projected = sem("projected")
        products, turned = sem("products"), sem("turned")
        high, low, stored = sem("high"), sem("low"), sem("stored")
        squared, summed, normed = sem("squared"), sem("summed"), sem("normed")
        norm_high, norm_low, norm_stored = sem("norm_high"), sem("norm_low"), sem("norm_stored")
        v_copied, v_turned, v_kept = sem("v_copied"), sem("v_turned"), sem("v_kept")
        made = sem("made")
        top_ready, top_turned, top_one, top_spread, top_done = [sem(f"top{j}") for j in range(5)]
        block = c.enter_context(nc.Block())
        N_SETS = SETS + 1
        W_PARTS = [(2 * P * s, min(2 * P * (s + 1), COLS * P)) for s in range(N_SETS + 1)]

        @block.sync
        def _(sp):
            prime(sp, stored, norm_stored)

            def load_w(i):
                a, b = W_PARTS[i]
                sp.dma_start(w[:, :, a:b], w_qkv.rearrange("(c p) n -> p c n", p=P)[:, :, a:b]).then_inc(w_in[i], DMA)

            load_w(0)
            for n in range(CHUNKS):
                if n >= 2:
                    sp.wait_ge(x_split, n - 1)
                sp.dma_start(xs[n % 2][:], x_t[:, n * CHUNK:(n + 1) * CHUNK].rearrange("(c p) n -> p c n", p=P)
                             ).then_inc(x_in[n % 2], DMA)
                if n == 0:
                    for i in range(1, len(W_PARTS)):
                        load_w(i)
                    sp.dma_start(cos_s[:], cos).then_inc(table_in, DMA)
                    sp.dma_start(sin_s[:], sin).then_inc(table_in, DMA)
                    sp.dma_start(ident[:], ident_dram).then_inc(ident_in, DMA)
            with sp.Fori(0, CHUNKS) as n:
                col = n * CHUNK
                for s in range(N_SETS):
                    rows = P // 2 if s == 0 else P
                    dst = k_s if s == 0 else q_s[(s - 1) * SET_HEADS:s * SET_HEADS]
                    for half in range(2):
                        for part in range(2):
                            if half == 0 and part == 0:
                                sp.wait_ge(low, (n * N_SETS + s + 1) * 2 + 1)
                            sp.dma_start(dst[:, part, half * PAIRS:(half + 1) * PAIRS, bass.ds(col, CHUNK)],
                                         parts[0:rows, s, half, part, :].bitcast(F32)).then_inc(stored, DMA)
                sp.wait_ge(norm_low, n + 2)
                for s in range(SETS):
                    for part, src in enumerate((norm_hi, norm_lo)):
                        at = 32 * (s + 1)
                        sp.dma_start(m_s[s * SET_HEADS:(s + 1) * SET_HEADS, part, bass.ds(col, CHUNK)],
                                     src[at:at + SET_HEADS, :].bitcast(F32)).then_inc(norm_stored, DMA)
            sp.wait_ge(stored, CHUNKS * N_SETS * 4 * DMA + 1)
            sp.wait_ge(norm_stored, CHUNKS * SETS * 2 * DMA + 1)

        @block.scalar
        def _(act):
            prime(act, squared, high, v_copied, normed, norm_high)

            def w_part(i):
                a, b = W_PARTS[i]
                act.wait_ge(w_in[i], DMA)
                nc.scalar.activation(w_hi[:, :, a:b], w[:, :, a:b], ACT.Copy).then_inc(w_high, 1)

            w_part(0)
            for n in range(CHUNKS):
                act.wait_ge(x_in[n % 2], DMA * (n // 2 + 1))
                nc.scalar.activation(x_hi[:, :, n * CHUNK:(n + 1) * CHUNK], xs[n % 2][:], ACT.Copy).then_inc(x_high, 1)
                if n == 0:
                    for i in range(1, len(W_PARTS)):
                        w_part(i)
            with act.Fori(0, CHUNKS) as n:
                for s in range(N_SETS):
                    act.wait_ge(projected, n * COLS + 2 * s + 3)
                    act.wait_ge(summed, n * N_SETS + s + 1)
                    for half in range(2):
                        last = nc.scalar.activation(sq[:, half, :], acc[2 * s + half][:], ACT.Square)
                    last.then_inc(squared, 1)
                    if s == N_SETS - 1:
                        act.wait_ge(projected, n * COLS + COLS + 1)
                        nc.scalar.activation(v_t[:, bass.ds(n * CHUNK, CHUNK)], acc[COLS - 1][:], ACT.Copy).then_inc(v_copied, 1)
                    act.wait_ge(turned, n * N_SETS + s + 2)
                    if s == 0:
                        act.wait_ge(stored, n * (N_SETS * 4 * DMA) + 1)
                    nc.scalar.activation(parts[:, s, :, 0, :], rot[:], ACT.Copy).then_inc(high, 1)
                act.wait_ge(summed, n * N_SETS + N_SETS + 1)
                act.wait_ge(norm_low, n + 1)
                nc.scalar.activation(norm[0:96], small[0:96], ACT.Copy, scale=-0.5).then_inc(normed, 1)
                act.wait_ge(normed, n + 2)
                act.wait_ge(norm_stored, n * (SETS * 2 * DMA) + 1)
                nc.scalar.activation(norm_hi[0:96], norm[0:96], ACT.Copy).then_inc(norm_high, 1)
            for n in range(CHUNKS):
                act.wait_ge(v_turned, n + 1)
                nc.scalar.activation(values[:, n * (CHUNK // P):(n + 1) * (CHUNK // P), :],
                                     acc[n][:].rearrange("p (t d) -> p t d", d=P), ACT.Copy).then_inc(v_kept, 1)
            act.wait_ge(v_kept, CHUNKS)

        @block.vector
        def _(dve):
            nc.vector.memset(ones_row[:], 1.0)
            nc.vector.memset(least_row[:], 0.0).then_inc(made, 1)
            for _ in range(N_SETS - 1):
                prime(dve, products)
            prime(dve, products, turned, low, norm_low)

            def w_part(i):
                a, b = W_PARTS[i]
                dve.wait_ge(w_high, i + 1)
                nc.vector.tensor_tensor(w_lo[:, :, a:b], w[:, :, a:b], w_hi[:, :, a:b], ALU.subtract).then_inc(w_split, 1)

            w_part(0)
            dve.wait_ge(x_high, 1)
            nc.vector.tensor_tensor(x_lo[:, :, 0:CHUNK], xs[0][:], x_hi[:, :, 0:CHUNK], ALU.subtract).then_inc(x_split, 1)
            for i in range(1, len(W_PARTS)):
                w_part(i)
            dve.wait_ge(table_in, 2 * DMA)
            with dve.Fori(0, BATCH) as b:
                for half_seq in range(SEQ // CHUNK):
                    n = b * (SEQ // CHUNK) + half_seq
                    co = cos_s[:, half_seq * CHUNK:(half_seq + 1) * CHUNK]
                    si = sin_s[:, half_seq * CHUNK:(half_seq + 1) * CHUNK]
                    for s in range(N_SETS):
                        even, odd = acc[2 * s], acc[2 * s + 1]
                        dve.wait_ge(squared, n * N_SETS + s + 2)
                        dve.wait_ge(turned, n * N_SETS + s + 1)
                        nc.vector.tensor_tensor(prod[:, 0, :], even[:], co, ALU.mult)
                        nc.vector.tensor_tensor(prod[:, 1, :], odd[:], si, ALU.mult)
                        nc.vector.tensor_tensor(prod[:, 2, :], even[:], si, ALU.mult)
                        nc.vector.tensor_tensor(prod[:, 3, :], odd[:], co, ALU.mult).then_inc(products, 1)
                        dve.wait_ge(products, (n + 1) * N_SETS + s + 1)
                        dve.wait_ge(high, n * N_SETS + s + 1)
                        dve.wait_ge(low, (n * N_SETS + s) * 2 + 1)
                        nc.vector.tensor_tensor(rot[:, 0, :], prod[:, 0, :], prod[:, 1, :], ALU.subtract)
                        nc.vector.tensor_tensor(rot[:, 1, :], prod[:, 2, :], prod[:, 3, :], ALU.add).then_inc(turned, 1)
                        dve.wait_ge(high, n * N_SETS + s + 2)
                        for half in range(2):
                            nc.vector.tensor_tensor(parts[:, s, half, 1, :], rot[:, half, :], parts[:, s, half, 0, :],
                                                    ALU.subtract).then_inc(low, 1)
                    dve.wait_ge(norm_high, n + 2)
                    nc.vector.tensor_tensor(norm_lo[0:96], norm[0:96], norm_hi[0:96], ALU.subtract)
                    nc.vector.tensor_reduce(least[0:96, bass.ds(n, 1)], norm[0:96, :], AX.X, ALU.min).then_inc(norm_low, 1)
            dve.wait_ge(norm_low, CHUNKS + 1)
            nc.vector.tensor_reduce(least_row[0:96, :], least[0:96, :], AX.X, ALU.min).then_inc(top_ready, 1)
            dve.wait_ge(top_turned, 1)
            nc.vector.tensor_reduce(k_one[:], small[0:1, 0:KV_HEADS], AX.X, ALU.min).then_inc(top_one, 1)
            nc.vector.tensor_reduce(all_one[:], small[0:1, 0:96], AX.X, ALU.min).then_inc(top_one, 1)
            dve.wait_ge(top_one, 2)
            nc.vector.tensor_scalar(loose[:], all_one[:], -SAFE_NORM / 2, None, ALU.is_lt).then_inc(top_done, 1)
            dve.wait_ge(top_spread, 1)
            nc.vector.tensor_scalar(less_one[:], small[:, P:P + 1], 1.0, None, ALU.subtract).then_inc(top_done, 1)
            dve.wait_ge(top_done, 2)
            nc.vector.tensor_scalar(bound[:], less_one[:], ident[:, BOUND_ROW:BOUND_ROW + 1], 1.0, ALU.mult, ALU.add
                                    ).then_inc(top_done, 1)
            dve.wait_ge(top_done, 3)

        @block.gpsimd
        def _(pool):
            nc.gpsimd.memset(sum_heads[:], 1.0).then_inc(made, 1)
            pool.wait_ge(made, 2)
            nc.gpsimd.affine_select(out=sum_heads[:], in_=sum_heads[:], compare_op=ALU.is_ge, fill=0.0, base=0,
                                    pattern=[[-PAIRS, 32]], channel_multiplier=1).then_inc(made, 1)
            pool.wait_ge(made, 3)
            nc.gpsimd.affine_select(out=sum_heads[:], in_=sum_heads[:], compare_op=ALU.is_ge, fill=0.0, base=PAIRS - 1,
                                    pattern=[[PAIRS, 32]], channel_multiplier=-1).then_inc(made, 1)
            pool.wait_ge(made, 4)
            for n in range(1, CHUNKS):
                cols = slice(n * CHUNK, (n + 1) * CHUNK)
                pool.wait_ge(x_high, n + 1)
                pool.wait_ge(x_split, n)
                nc.gpsimd.tensor_tensor(x_lo[:, :, cols], xs[n % 2][:], x_hi[:, :, cols], ALU.subtract).then_inc(x_split, 1)

        @block.tensor
        def _(pe):
            prime(pe, projected, summed)
            pe.wait_ge(made, 4)
            pe.wait_ge(ident_in, DMA)

            with pe.Fori(0, CHUNKS) as n:
                pe.wait_ge(x_split, n + 1)
                xh = x_hi[:, :, bass.ds(n * CHUNK, CHUNK)]
                xl = x_lo[:, :, bass.ds(n * CHUNK, CHUNK)]

                def norms(s):
                    pe.wait_ge(squared, n * N_SETS + s + 2)
                    if s == 0:
                        pe.wait_ge(normed, n + 1)
                    for half in range(2):
                        last = nc.tensor.matmul(small[32 * s:32 * s + 32, :], sum_heads[:], sq[:, half, :],
                                                start=half == 0, stop=half == 1)
                    last.then_inc(summed, 1)

                for j in range(COLS):
                    if j < 2 * N_SETS:
                        if j % 2 == 0:
                            pe.wait_ge(products, n * N_SETS + j // 2 + 1)
                            pe.wait_ge(w_split, j // 2 + 1)
                    else:
                        pe.wait_ge(v_copied, n + 1)
                        pe.wait_ge(w_split, len(W_PARTS))
                    terms = [(k, a, b) for k in range(KC) for a, b in ((w_hi, xh), (w_hi, xl), (w_lo, xh))]
                    for i, (k, a, b) in enumerate(terms):
                        last = nc.tensor.matmul(acc[j][:], a[:, k, j * P:(j + 1) * P], b[:, k, :],
                                                start=i == 0, stop=i == len(terms) - 1)
                    last.then_inc(projected, 1)
                    if j in (3, 5):
                        norms((j - 3) // 2)
                norms(N_SETS - 1)
            pe.wait_ge(v_copied, CHUNKS + 1)
            pe.wait_ge(products, (CHUNKS + 1) * N_SETS)
            for n in range(CHUNKS):
                for t in range(CHUNK // P):
                    at = n * CHUNK + t * P
                    last = nc.tensor.transpose(acc[n][:, t * P:(t + 1) * P], v_t[:, at:at + P], ident[:])
                last.then_inc(v_turned, 1)
            pe.wait_ge(top_ready, 1)
            nc.tensor.transpose(small[0:1, 0:P], least_row[:], ident[:]).then_inc(top_turned, 1)
            pe.wait_ge(top_one, 2)
            nc.tensor.matmul(small[:, P:P + 1], ones_row[:], k_one[:], start=True, stop=True).then_inc(top_spread, 1)


def exact_maxima(nc, q_s, k_s, m_s, ident, bound, loose):
    with ExitStack() as c:
        sb = lambda n, s, d=F32: c.enter_context(nc.sbuf_tensor(f"em_{n}", s, d))
        sem = lambda n: c.enter_context(nc.semaphore(f"em_{n}"))
        q_st, k_st = sb("q_st", [4 * HEAD, SEQ], F32R), sb("k_st", [4 * HEAD, SEQ], F32R)
        allowed = sb("allowed", [P, P])
        top, minus = sb("top", [P, KT]), sb("minus", [P, KT])
        m_hi, m_lo = sb("m_hi", [KT, P], F32R), sb("m_lo", [KT, P], F32R)
        score_ps = c.enter_context(nc.psum_tensor("em_score_ps", [P, SEQ], F32))
        turn_ps = c.enter_context(nc.psum_tensor("em_turn_ps", [KT, P], F32))
        k_in, q_in, made = sem("k_in"), sem("q_in"), sem("made")
        scored, masked, topped = sem("scored"), sem("masked"), sem("topped")
        negated, turned, high, split, stored, cleared = [
            sem(n) for n in ("negated", "turned", "high", "split", "stored", "cleared")]
        block = c.enter_context(nc.Block())

        def where_loose(eng, body):
            with eng.If(eng.value_load(loose[0:1, 0:1], min_val=0, max_val=1) > 0):
                body()

        @block.sync
        def _(sp):
            def body():
                with sp.Fori(0, GROUPS) as g:
                    b, kv = g // KV_HEADS, g % KV_HEADS
                    cols = bass.ds(b * SEQ, SEQ)
                    for r in range(REP):
                        h = g * REP + r
                        sp.wait_ge(scored, h * KT + 1)
                        if r == 0:
                            for part in range(2):
                                for copy in range(2):
                                    at = (2 * part + copy) * HEAD
                                    sp.dma_start(k_st[at:at + HEAD, :].bitcast(F32), k_s[bass.ds(kv, 1), part, :, cols].rearrange(
                                        "k d t -> (k d) t")).then_inc(k_in, DMA)
                        for copy in range(2):
                            sp.dma_start(q_st[2 * HEAD * copy:2 * HEAD * (copy + 1), :].bitcast(F32),
                                         q_s[bass.ds(kv * REP + r, 1), :, :, cols].rearrange("h a d t -> (h a d) t")
                                         ).then_inc(q_in, DMA)
                        sp.wait_ge(split, h + 1)
                        for part, src in enumerate((m_hi, m_lo)):
                            sp.dma_start(m_s[bass.ds(kv * REP + r, 1), part, cols].rearrange("h (t p) -> (h t) p", p=P),
                                         src[:].bitcast(F32)).then_inc(stored, DMA)
                sp.wait_ge(stored, GROUPS * REP * 2 * DMA + 1)
            where_loose(sp, body)

        @block.gpsimd
        def _(pool):
            nc.gpsimd.memset(allowed[:], LARGEST).then_inc(made, 1)
            pool.wait_ge(made, 1)
            nc.gpsimd.affine_select(out=allowed[:], in_=allowed[:], compare_op=ALU.is_ge, fill=-LARGEST, base=0,
                                    pattern=[[-1, P]], channel_multiplier=1).then_inc(made, 1)
            pool.wait_ge(made, 2)

        @block.vector
        def _(dve):
            def body():
                prime(dve, topped, stored)
                dve.wait_ge(made, 2)
                nc.vector.tensor_scalar(bound[:], ident[:, BOUND_ROW:BOUND_ROW + 1], -1.0, 1.0, ALU.mult, ALU.add).then_inc(cleared, 1)
                with dve.Fori(0, GROUPS) as g:
                    for r in range(REP):
                        h = g * REP + r
                        for qt in range(KT):
                            diag = score_ps[:, qt * P:(qt + 1) * P]
                            dve.wait_ge(scored, h * KT + qt + 2)
                            nc.vector.tensor_tensor(diag, diag, allowed[:], ALU.min).then_inc(masked, 1)
                            dve.wait_ge(masked, h * KT + qt + 1)
                            nc.vector.tensor_reduce(top[:, qt:qt + 1], score_ps[:, 0:(qt + 1) * P], AX.X, ALU.max
                                                    ).then_inc(topped, 1)
                        dve.wait_ge(topped, (h + 1) * KT + 1)
                        nc.vector.tensor_scalar(minus[:], top[:], -1.0, None, ALU.mult).then_inc(negated, 1)
                        dve.wait_ge(stored, h * (2 * DMA) + 1)
                        dve.wait_ge(turned, h + 1)
                        nc.vector.tensor_copy(m_hi[:], turn_ps[:]).then_inc(high, 1)
                        dve.wait_ge(high, h + 1)
                        nc.vector.tensor_tensor(m_lo[:], turn_ps[:], m_hi[:], ALU.subtract).then_inc(split, 1)
                dve.wait_ge(cleared, 1)
            where_loose(dve, body)

        @block.tensor
        def _(pe):
            def body():
                prime(pe, scored)
                with pe.Fori(0, GROUPS) as g:
                    for r in range(REP):
                        h = g * REP + r
                        pe.wait_ge(k_in, (g + 1) * (4 * DMA))
                        pe.wait_ge(q_in, (h + 1) * (2 * DMA))
                        for qt in range(KT):
                            pe.wait_ge(topped, h * KT + qt + 1)
                            width = (qt + 1) * P
                            for a in range(0, width, CHUNK):
                                last = nc.tensor.matmul(score_ps[:, a:min(a + CHUNK, width)], q_st[:, qt * P:(qt + 1) * P],
                                                        k_st[:, a:min(a + CHUNK, width)], start=True, stop=True)
                            last.then_inc(scored, 1)
                        pe.wait_ge(negated, h + 1)
                        nc.tensor.transpose(turn_ps[:], minus[:], ident[:]).then_inc(turned, 1)
            where_loose(pe, body)


def attend(nc, q_s, k_s, m_s, values, bound, o_s, d_s):
    with ExitStack() as c:
        sb = lambda n, s, d=F32: c.enter_context(nc.sbuf_tensor(n, s, d))
        sem = lambda n: c.enter_context(nc.semaphore(n))
        ROWS = 4 * HEAD + 3
        SLOTS = 4
        q_st = [sb(f"q_st{p}", [P, REP, SEQ], F32R) for p in range(2)]
        k_st = [sb(f"k_st{p}", [P, SEQ], F32R) for p in range(2)]
        v_st = [sb(f"v_st{p}", [P, KT, VW]) for p in range(2)]
        prob = [sb(f"prob{j}", [P, REP, SEQ]) for j in range(SLOTS)]
        o_t = [sb(f"o_t{p}", [P, SEQ]) for p in range(2)]
        cap = sb("cap", [P, P])
        ring = [c.enter_context(nc.psum_tensor(f"ring{j}", [P, SEQ], F32)) for j in range(3)]
        out_ps = c.enter_context(nc.psum_tensor("out_ps", [P, SEQ], F32))
        loaded = [sem("loaded0"), sem("loaded1")]
        LOADS, STORES = 7, REP + 1
        cap_made, blank, ones_made, bounded, v_blank = [sem(n) for n in ("cap_made", "blank", "ones_made", "bounded", "v_blank")]
        scored, expd, masked = sem("scored"), sem("expd"), sem("masked")
        weighed = sem("weighed")
        v_staged, out_copied, out_stored = sem("v_staged"), sem("out_copied"), [sem("out_stored0"), sem("out_stored1")]
        UNIT = []
        for kt in range(KT):
            width = SEQ - kt * P
            heads = 1 if width > CHUNK else 2 if width > CHUNK // 2 else REP
            UNIT += [(kt, h, heads) for h in range(0, REP, heads)]
        UNITS = len(UNIT)
        LAST = [max(u for u in range(UNITS) if UNIT[u][0] == kt) for kt in range(KT)]
        AHEAD = 6
        HALF = [(0, CHUNK), (CHUNK, SEQ)]
        SLOT = [u % 3 for u in range(UNITS - 1)] + [1]
        LAST_IN_SLOT = [max(v for v in range(-UNITS, u) if SLOT[v % UNITS] == SLOT[u]) for u in range(UNITS)]

        def halves(kt):
            return [(max(a, kt * P), b, j) for j, (a, b) in enumerate(HALF) if kt * P < b]

        def unit_view(tile, kt, heads):
            width = SEQ - kt * P
            if heads == 1:
                return tile[:, kt * P:SEQ].unsqueeze(1)
            pitch = CHUNK if heads == 2 else width
            return tile[:, 0:heads * pitch].rearrange("p (h w) -> p h w", h=heads)[:, :, 0:width]

        WEIGH_AT = [6, 8, 10, 13, 15, 17, 18, 19, 21, 24, 26, 27]
        segments = [(kt, half) for kt in range(KT) for half in range(len(halves(kt)))]
        weigh_after = {v: [s for s, at in zip(segments, WEIGH_AT, strict=True) if at == v] for v in range(AHEAD, UNITS + AHEAD)}

        block = c.enter_context(nc.Block())

        @block.sync
        def _(sp):
            def load(parity, b, kv, first=False):
                q, k, st = q_st[parity], k_st[parity], loaded[parity]
                head = kv * REP
                cols = bass.ds(b * SEQ, SEQ)
                for r in range(2):
                    sp.dma_start(q[32 * r:32 * r + 32, :, :].bitcast(F32),
                                 q_s[bass.ds(head, REP), :, :, cols].rearrange("h a d t -> (a d) h t")).then_inc(st, DMA)
                    for s in range(2):
                        at = 32 * r + HEAD * s
                        sp.dma_start(k[at:at + HEAD, :].bitcast(F32), k_s[bass.ds(kv, 1), r, :, cols].rearrange(
                            "k d t -> (k d) t")).then_inc(st, DMA)
                if first:
                    sp.wait_ge(ones_made, parity + 2)
                sp.dma_start(q[4 * HEAD:ROWS - 1, :, :].bitcast(F32),
                             m_s[bass.ds(head, REP), :, cols].rearrange("h a t -> a h t")).then_inc(st, DMA)

            load(0, 0, 0, first=True)
            load(1, 0, 1, first=True)
            for b in range(BATCH):
                with sp.Fori(0, KV_HEADS // 2) as i:
                    for parity in range(2):
                        g = b * KV_HEADS + i * 2 + parity
                        sp.wait_ge(scored, (g + 1) * UNITS)
                        nxt = i * 2 + 2 + parity
                        if b + 1 < BATCH:
                            load(parity, b + nxt // KV_HEADS, nxt % KV_HEADS)
                        else:
                            load(parity, b, nxt % KV_HEADS)
                        sp.wait_ge(out_copied, 2 * g + 4)
                        heads = bass.ds((i * 2 + parity) * REP, REP)
                        for h in range(REP):
                            sp.dma_start(o_s[bass.ds((i * 2 + parity) * REP + h, 1), :, b * SEQ:(b + 1) * SEQ].rearrange(
                                "h d t -> (h d) t"), o_t[parity][VW * h:VW * h + HEAD, :]).then_inc(out_stored[parity], DMA)
                        sp.dma_start(d_s[heads, b * SEQ:(b + 1) * SEQ], o_t[parity][HEAD:P:VW, :]
                                     ).then_inc(out_stored[parity], DMA)
            for parity in range(2):
                sp.wait_ge(loaded[parity], (GROUPS // 2 + 1) * LOADS * DMA)
                sp.wait_ge(out_stored[parity], GROUPS // 2 * STORES * DMA + 1)

        @block.scalar
        def _(act):
            def exp_unit(g, u, first=False):
                kt, h, heads = UNIT[u]
                act.wait_ge(scored, g * UNITS + u + 1)
                if h == 0 and not (first and kt < SLOTS):
                    act.wait_ge(weighed, g * KT + kt - SLOTS + 2)
                nc.scalar.activation(prob[kt % SLOTS][:, h:h + heads, kt * P:SEQ], unit_view(ring[SLOT[u]], kt, heads),
                                     ACT.Exp, scale=SCALE).then_inc(expd, 1)

            for u in range(UNITS):
                exp_unit(0, u, first=True)
            with act.Fori(1, GROUPS) as g:
                for u in range(UNITS):
                    exp_unit(g, u)
            for u in range(AHEAD):
                exp_unit(GROUPS, u)

        @block.gpsimd
        def _(pool):
            def stage_v(parity, b, kv):
                nc.gpsimd.tensor_copy(v_st[parity][:, :, 0:HEAD],
                                      values[:, bass.ds(b * KT, KT), bass.ds(kv * HEAD, HEAD)]).then_inc(v_staged, 1)

            for p in range(2):
                nc.gpsimd.memset(k_st[p][4 * HEAD:P, :].bitcast(F32), 0.0).then_inc(blank, 1)
                pool.wait_ge(blank, p + 1)
                half = slice(REP // 2 if p == 0 else 0, REP)
                nc.gpsimd.memset(q_st[p][4 * HEAD:P, half, :].bitcast(F32), 1.0).then_inc(ones_made, 1)
                pool.wait_ge(ones_made, p + 2)
                nc.gpsimd.memset(v_st[p][:], 0.0).then_inc(v_blank, 1)
                pool.wait_ge(v_blank, 2 * p + 1)
                nc.gpsimd.memset(v_st[p][:, :, HEAD:HEAD + 1], 1.0).then_inc(v_blank, 1)
                pool.wait_ge(v_blank, 2 * p + 2)
            nc.gpsimd.memset(cap[:], LARGEST).then_inc(cap_made, 1)
            pool.wait_ge(cap_made, 1)
            nc.gpsimd.affine_select(out=cap[:], in_=cap[:], compare_op=ALU.is_ge, fill=0.0, base=0,
                                    pattern=[[1, P]], channel_multiplier=-1).then_inc(cap_made, 1)
            pool.wait_ge(cap_made, 2)
            pool.wait_ge(v_blank, 4)
            stage_v(0, 0, 0)
            with pool.Fori(0, GROUPS // 2) as i:
                for parity in range(2):
                    g = i * 2 + parity
                    pool.wait_ge(weighed, g * KT + 1)
                    pool.wait_ge(v_staged, g + 1)
                    nxt = (g + 1) % GROUPS
                    stage_v(1 - parity, nxt // KV_HEADS, nxt % KV_HEADS)

        @block.vector
        def _(dve):
            def mask_unit(g, u):
                kt, h, heads = UNIT[u]
                diag = prob[kt % SLOTS][:, h:h + heads, kt * P:(kt + 1) * P]
                dve.wait_ge(expd, g * UNITS + u + 1)
                nc.vector.tensor_tensor(diag, diag, cap[:].unsqueeze(1).to_broadcast([P, heads, P]),
                                        ALU.min).then_inc(masked, 1)

            prime(dve, *out_stored)
            prime(dve, out_copied, by=2)
            nc.vector.memset(q_st[0][4 * HEAD:P, 0:REP // 2, :].bitcast(F32), 1.0).then_inc(ones_made, 1)
            for p in range(2):
                dve.wait_ge(blank, p + 1)
                nc.vector.tensor_scalar(k_st[p][4 * HEAD:ROWS, :], k_st[p][4 * HEAD:ROWS, :], 0.0,
                                        bound[4 * HEAD:ROWS, 0:1], ALU.mult, ALU.add).then_inc(bounded, 1)
            dve.wait_ge(cap_made, 2)
            for u in range(AHEAD):
                mask_unit(0, u)
            with dve.Fori(0, GROUPS // 2) as i:
                for parity in range(2):
                    g = i * 2 + parity
                    for u in range(AHEAD, UNITS + AHEAD):
                        if u == UNITS:
                            dve.wait_ge(weighed, g * KT + CHUNK // P + 1)
                            dve.wait_ge(out_stored[parity], i * (STORES * DMA) + 1)
                            nc.vector.tensor_copy(o_t[parity][:, 0:CHUNK], out_ps[:, 0:CHUNK]).then_inc(out_copied, 1)
                        if u == UNITS + AHEAD - 1:
                            dve.wait_ge(weighed, (g + 1) * KT + 1)
                            nc.vector.tensor_copy(o_t[parity][:, CHUNK:SEQ], out_ps[:, CHUNK:SEQ]).then_inc(out_copied, 1)
                        mask_unit(g + u // UNITS, u % UNITS)

        @block.tensor
        def _(pe):
            def score(parity, u):
                kt, h0, heads = UNIT[u]
                view = unit_view(ring[SLOT[u]], kt, heads)
                for h in range(heads):
                    for a, b, _ in halves(kt):
                        last = nc.tensor.matmul(view[:, h, a - kt * P:b - kt * P],
                                                k_st[parity][:, kt * P:(kt + 1) * P],
                                                q_st[parity][:, h0 + h, a:b], start=True, stop=True)
                last.then_inc(scored, 1)

            def weigh(parity, g, kt, half):
                a, b, bank = halves(kt)[half]
                if half == 0:
                    pe.wait_ge(masked, g * UNITS + LAST[kt] + 1)
                if kt == 0:
                    if half == 0:
                        pe.wait_ge(v_staged, g + 1)
                    pe.wait_ge(out_copied, 2 * g + half + 1)
                last_of_bank = (kt + 1) * P == HALF[bank][1]
                for h in range(REP):
                    last = nc.tensor.matmul(out_ps[32 * h:32 * h + VW, a:b], v_st[parity][:, kt, :],
                                            prob[kt % SLOTS][:, h, a:b], start=kt == 0, stop=last_of_bank)
                if half == len(halves(kt)) - 1:
                    last.then_inc(weighed, 1)

            prime(pe, weighed)
            pe.wait_ge(bounded, 2)
            pe.wait_ge(loaded[0], LOADS * DMA)
            for u in range(AHEAD):
                if u >= 3:
                    pe.wait_ge(expd, u - 2)
                score(0, u)
            with pe.Fori(0, GROUPS // 2) as i:
                for parity in range(2):
                    g = i * 2 + parity
                    for u in range(AHEAD, UNITS + AHEAD):
                        nxt, v = divmod(u, UNITS)
                        pe.wait_ge(expd, (g + nxt) * UNITS + LAST_IN_SLOT[v] + 1)
                        if u == UNITS:
                            pe.wait_ge(loaded[1 - parity], (i + 1 + parity) * (LOADS * DMA))
                        score(parity ^ nxt, v)
                        for kt, half in weigh_after[u]:
                            weigh(parity, g, kt, half)


def project_out(nc, x, w_o, w_gate, ident, o_s, d_s, r_s, x_s, rows, t_hi, t_lo, logits):
    with ExitStack() as c:
        sb = lambda n, s, d=F32: c.enter_context(nc.sbuf_tensor(f"po_{n}", s, d))
        sem = lambda n: c.enter_context(nc.semaphore(f"po_{n}"))
        ps = lambda n: c.enter_context(nc.psum_tensor(f"po_{n}", [P, CHUNK], F32))
        TILES = CHUNK // P
        wo, wo_hi, wo_lo = sb("wo", [P, KC, DIM]), sb("wo_hi", [P, KC, DIM], F32R), sb("wo_lo", [P, KC, DIM], F32R)
        wg, wg_hi, wg_lo = sb("wg", [P, KC, P]), sb("wg_hi", [P, KC, P], F32R), sb("wg_lo", [P, KC, P], F32R)
        den = sb("den", [P, HEADS * TOKENS // P])
        o_c = [sb(f"o_c{p}", [P, KC, CHUNK]) for p in range(2)]
        r_c = [sb(f"r_c{p}", [P, KC, CHUNK]) for p in range(2)]
        a_hi = [sb(f"a_hi{p}", [P, KC, CHUNK], F32R) for p in range(2)]
        a_lo = [sb(f"a_lo{p}", [P, KC, CHUNK], F32R) for p in range(2)]
        fresh = sb("fresh", [P, TILES, DIM])
        eps = sb("eps", [P, 1])
        stats = sb("stats", [P, TILES, 6])
        moments = sb("moments", [P, TILES, 2])
        spread = sb("spread", [P, TILES])
        scale = sb("scale", [P, TILES])
        logit_t = r_c[0][:].rearrange("p c n -> p (c n)")
        wo_ps = [ps(f"wo_ps{j}") for j in range(2)]
        turn_ps = [ps(f"turn_ps{t}") for t in range(TILES)]
        back_ps = [ps(f"back_ps{j}") for j in range(2)]

        wo_in, wg_in, den_in, inv_out = sem("wo_in"), sem("wg_in"), sem("den_in"), sem("inv_out")
        o_in = [sem(f"o_in{p}") for p in range(2)]
        r_in = [[sem(f"r_in{p}{k}") for k in range(KC)] for p in range(2)]
        x_in = [sem(f"x_in{p}") for p in range(2)]
        inverted, eps_made = sem("inverted"), sem("eps_made")
        w_high, w_split = sem("w_high"), sem("w_split")
        divided, a_high, a_split = sem("divided"), sem("a_high"), sem("a_split")
        projected, added, counted, averaged, rooted, scaled, normed = [
            sem(n) for n in ("projected", "added", "counted", "averaged", "rooted", "scaled", "normed")]
        turned, turned_high, turned_low = sem("turned"), sem("turned_high"), sem("turned_low")
        gated, logit_kept, logit_back, logit_done = sem("gated"), sem("logit_kept"), sem("logit_back"), sem("logit_done")
        rows_kept, rows_out = sem("rows_kept"), sem("rows_out")
        block = c.enter_context(nc.Block())

        @block.sync
        def _(sp):
            prime(sp, a_split, by=2 * KC)
            prime(sp, added, by=TILES + 1)
            sp.dma_start(den[:], d_s.rearrange("h (a b) -> (h a) b", b=den.shape[1])).then_inc(den_in, DMA)

            def load_sums(n):
                sp.dma_start(o_c[n % 2][:], o_s.rearrange("(c h) d t -> (h d) c t", c=KC)[:, :, n * CHUNK:(n + 1) * CHUNK]
                             ).then_inc(o_in[n % 2], DMA)

            load_sums(0)
            sp.wait_ge(inverted, 1)
            sp.dma_start(r_s.rearrange("h (a b) -> (h a) b", b=den.shape[1]), den[:]).then_inc(inv_out, DMA)
            sp.dma_start(wo[:], w_o.rearrange("(c p) n -> p c n", p=P)).then_inc(wo_in, DMA)
            sp.wait_ge(inv_out, DMA)
            for n in range(CHUNKS):
                p = n % 2
                cols = slice(n * CHUNK, (n + 1) * CHUNK)
                if n >= 2:
                    sp.wait_ge(a_split, (n + 1) * KC)
                if n >= 1:
                    load_sums(n)
                for k in range(KC):
                    heads = P // HEAD
                    sp.dma_start(r_c[p][:, k, :], r_s[k * heads:(k + 1) * heads, cols].unsqueeze(1).to_broadcast(
                        [heads, HEAD, CHUNK])).then_inc(r_in[p][k], DMA)
                if n >= 2:
                    sp.wait_ge(added, n * TILES + 1)
                sp.dma_start(rows[:, n * TILES:(n + 1) * TILES, :], x[cols, :].rearrange("(t p) d -> p t d", p=P)
                             ).then_inc(x_in[p], DMA)
                if n == 0:
                    sp.dma_start(wg[:], w_gate.rearrange("(c p) n -> p c n", p=P)).then_inc(wg_in, DMA)
            for n in range(CHUNKS):
                sp.wait_ge(rows_kept, (n + 1) * TILES + TILES)
                sp.dma_start(x_s[n * CHUNK:(n + 1) * CHUNK, :].rearrange("(t p) d -> p t d", p=P),
                             rows[:, n * TILES:(n + 1) * TILES, :]).then_inc(rows_out, DMA)
            sp.wait_ge(rows_out, CHUNKS * DMA)

        @block.gpsimd
        def _(pool):
            with pool.Fori(0, CHUNKS // 2) as i:
                for p in range(2):
                    n = i * 2 + p
                    pool.wait_ge(o_in[p], (i + 1) * DMA)
                    pool.wait_ge(projected, n * TILES + 1)
                    for k in range(KC):
                        pool.wait_ge(r_in[p][k], (i + 1) * DMA)
                        nc.gpsimd.tensor_tensor(a_hi[p][:, k, :], o_c[p][:, k, :], r_c[p][:, k, :], ALU.mult).then_inc(a_high, 1)
                        pool.wait_ge(a_high, n * KC + k + 1)
                        nc.gpsimd.tensor_tensor(o_c[p][:, k, :], o_c[p][:, k, :], r_c[p][:, k, :], ALU.mult).then_inc(divided, 1)
                        pool.wait_ge(divided, n * KC + k + 1)
                        nc.gpsimd.tensor_tensor(a_lo[p][:, k, :], o_c[p][:, k, :], a_hi[p][:, k, :], ALU.subtract).then_inc(a_split, 1)

        @block.scalar
        def _(act):
            prime(act, rows_kept, by=TILES)
            act.wait_ge(wo_in, DMA)
            nc.scalar.activation(wo_hi[:], wo[:], ACT.Copy).then_inc(w_high, 1)
            act.wait_ge(wg_in, DMA)
            nc.scalar.activation(wg_hi[:], wg[:], ACT.Copy).then_inc(w_high, 1)
            act.wait_ge(eps_made, 1)
            with act.Fori(0, CHUNKS // 2) as i:
                for p in range(2):
                    n = i * 2 + p
                    for step in range(TILES + 2):
                        if step < TILES:
                            act.wait_ge(averaged, n * TILES + step + 1)
                            nc.scalar.activation(spread[:, step:step + 1], moments[:, step, 1:2], ACT.Sqrt,
                                                 bias=eps[:, 0:1]).then_inc(rooted, 1)
                        if step >= 2:
                            t = step - 2
                            act.wait_ge(turned, n * TILES + t + 1)
                            nc.scalar.activation(t_hi[:, :, bass.ds(n * CHUNK + t * P, P)],
                                                 turn_ps[t][:].rearrange("p (k t) -> p k t", k=KC),
                                                 ACT.Copy).then_inc(turned_high, 1)
                            nc.scalar.activation(rows[:, bass.ds(n * TILES + t, 1), :], fresh[:, t:t + 1, :], ACT.Copy
                                                 ).then_inc(rows_kept, 1)
            for n in range(CHUNKS):
                act.wait_ge(gated, n + 1)
                nc.scalar.activation(logit_t[:, n * CHUNK:(n + 1) * CHUNK], turn_ps[n][:], ACT.Copy).then_inc(logit_kept, 1)

        @block.vector
        def _(dve):
            prime(dve, turned_low, by=TILES)
            dve.wait_ge(den_in, DMA)
            nc.vector.reciprocal(den[:], den[:]).then_inc(inverted, 1)
            nc.vector.memset(eps[:], 1e-5).then_inc(eps_made, 1)
            dve.wait_ge(w_high, 1)
            nc.vector.tensor_tensor(wo_lo[:], wo[:], wo_hi[:], ALU.subtract).then_inc(w_split, 1)
            dve.wait_ge(w_high, 2)
            nc.vector.tensor_tensor(wg_lo[:], wg[:], wg_hi[:], ALU.subtract).then_inc(w_split, 1)
            with dve.Fori(0, CHUNKS // 2) as i:
                for p in range(2):
                    n = i * 2 + p
                    for step in range(TILES + 4):
                        if step < TILES:
                            t = step
                            if t == 0:
                                dve.wait_ge(x_in[p], (i + 1) * DMA)
                            dve.wait_ge(projected, n * TILES + t + 2 + TILES)
                            dve.wait_ge(rows_kept, n * TILES + t + 1)
                            row = rows[:, bass.ds(n * TILES + t, 1), :].rearrange("p a d -> p (a d)")
                            nc.vector.tensor_tensor(fresh[:, t, :], wo_ps[t % 2][:], row, ALU.add).then_inc(added, 1)
                            dve.wait_ge(added, n * TILES + t + 2 + TILES)
                            if t >= 1:
                                dve.wait_ge(counted, n * TILES + t)
                            nc.vector.bn_stats(stats[:, t, :], fresh[:, t, :]).then_inc(counted, 1)
                        if 2 <= step < TILES + 2:
                            t = step - 2
                            dve.wait_ge(rooted, n * TILES + t + 1)
                            if step == TILES:
                                dve.wait_ge(counted, n * TILES + TILES)
                            nc.vector.reciprocal(scale[:, t:t + 1], spread[:, t:t + 1]).then_inc(scaled, 1)
                        if 1 <= step <= TILES:
                            t = step - 1
                            nc.vector.bn_aggr(moments[:, t, :], stats[:, t, :]).then_inc(averaged, 1)
                        if 2 <= step < TILES + 2:
                            t = step - 2
                            dve.wait_ge(scaled, n * TILES + t + 1)
                            nc.vector.tensor_scalar(fresh[:, t, :], fresh[:, t, :], moments[:, t, 0:1], scale[:, t:t + 1],
                                                    ALU.subtract, ALU.mult).then_inc(normed, 1)
                        if step >= 4:
                            t = step - 4
                            cols = bass.ds(n * CHUNK + t * P, P)
                            dve.wait_ge(turned_high, n * TILES + t + 1)
                            nc.vector.tensor_tensor(t_lo[:, :, cols], turn_ps[t][:].rearrange("p (k t) -> p k t", k=KC),
                                                    t_hi[:, :, cols], ALU.subtract).then_inc(turned_low, 1)
            for n in range(CHUNKS):
                dve.wait_ge(logit_back, n + 1)
                nc.vector.tensor_copy(logits[:, n * TILES:(n + 1) * TILES, :],
                                      back_ps[n % 2][:].rearrange("p (t e) -> p t e", e=P)[:, :, 0:EXPERTS]
                                      ).then_inc(logit_done, 1)
            dve.wait_ge(logit_done, CHUNKS)

        @block.tensor
        def _(pe):
            prime(pe, projected, by=TILES + 1)
            pe.wait_ge(w_split, 1)
            with pe.Fori(0, CHUNKS // 2) as i:
                for p in range(2):
                    n = i * 2 + p

                    def turn(t):
                        pe.wait_ge(turned_low, n * TILES + t + 1)
                        pe.wait_ge(normed, n * TILES + t + 1)
                        for k in range(KC):
                            last = nc.tensor.transpose(turn_ps[t][:, k * P:(k + 1) * P],
                                                       fresh[:, t, k * P:(k + 1) * P], ident[:])
                        last.then_inc(turned, 1)

                    for t in range(TILES):
                        pe.wait_ge(added, n * TILES + t - 1 + TILES + 1)
                        terms = [(k, a, b) for k in range(KC) for a, b in
                                 ((a_hi[p], wo_hi), (a_hi[p], wo_lo), (a_lo[p], wo_hi))]
                        for j, (k, a, b) in enumerate(terms):
                            if t == 0 and j % 3 == 0:
                                pe.wait_ge(a_split, (n + 2) * KC + k + 1)
                            last = nc.tensor.matmul(wo_ps[t % 2][:], a[:, k, t * P:(t + 1) * P], b[:, k, :], start=j == 0,
                                                    stop=j == len(terms) - 1)
                        last.then_inc(projected, 1)
                    for t in range(TILES):
                        turn(t)
            terms = [(k, a, b) for k in range(KC) for a, b in ((wg_hi, t_hi), (wg_hi, t_lo), (wg_lo, t_hi))]
            pe.wait_ge(w_split, 2)
            pe.wait_ge(turned_low, CHUNKS * TILES + TILES)
            for n in range(CHUNKS):
                for j, (k, a, b) in enumerate(terms):
                    last = nc.tensor.matmul(turn_ps[n][:], a[:, k, :], b[:, k, n * CHUNK:(n + 1) * CHUNK], start=j == 0,
                                            stop=j == len(terms) - 1)
                last.then_inc(gated, 1)
            for n in range(CHUNKS):
                pe.wait_ge(logit_kept, n + 1)
                if n >= 2:
                    pe.wait_ge(logit_done, n - 1)
                for t in range(TILES):
                    last = nc.tensor.transpose(back_ps[n % 2][:, t * P:(t + 1) * P],
                                               logit_t[:, n * CHUNK + t * P:n * CHUNK + (t + 1) * P], ident[:])
                last.then_inc(logit_back, 1)


def load_part(sp, e, w_gate_up, w_down, w_gu, w_dn, done):
    sp.dma_start(w_gu[:], w_gate_up[e].rearrange("(k p) n -> p k n", p=P)).then_inc(done, DMA)
    sp.dma_start(w_dn[:], w_down[e]).then_inc(done, DMA)


def shared_expert(nc, w_gate_up, w_down, part_weights, rows, t_hi, t_lo, w_first, w_dn_all):
    with ExitStack() as c:
        sb = lambda n, s, d=F32: c.enter_context(nc.sbuf_tensor(f"ff_{n}", s, d))
        sem = lambda n: c.enter_context(nc.semaphore(f"ff_{n}"))
        ps = lambda n: c.enter_context(nc.psum_tensor(f"ff_{n}", [P, CHUNK], F32))
        TILES = CHUNK // P
        w_gu, w_dn, gu_hi, gu_lo, dn_hi, dn_lo = part_weights
        gate = [sb(f"gate{j}", [P, CHUNK]) for j in range(2)]
        act_f = sb("act_f", [P, CHUNK])
        act_hi = [sb(f"act_hi{j}", [P, CHUNK], F32R) for j in range(2)]
        act_lo = [sb(f"act_lo{j}", [P, CHUNK], F32R) for j in range(2)]
        gate_ps = [ps(f"gate_ps{j}") for j in range(2)]
        up_ps = [ps(f"up_ps{j}") for j in range(2)]
        y_ps = [ps(f"y_ps{t}") for t in range(TILES)]

        w_in, ahead = [sem(f"w_in{p}") for p in range(2)], sem("ahead")
        w_high, w_split = sem("w_high"), sem("w_split")
        gated, upped, silued = sem("gated"), sem("upped"), sem("silued")
        acted, act_high, act_split = sem("acted"), sem("act_high"), sem("act_split")
        downed, added = sem("downed"), sem("added")
        LOADS = 2
        block = c.enter_context(nc.Block())

        @block.sync
        def _(sp):
            for e in range(1, SHARED):
                if e >= 2:
                    sp.wait_ge(w_split, e - 1)
                load_part(sp, e, w_gate_up, w_down, w_gu, w_dn, w_in[e % 2])
            for e in range(EXPERTS):
                sp.dma_start(w_first[:, e], w_gate_up[SHARED + e, 0:AHEAD_K * P, :].rearrange("(k p) n -> p k n", p=P)).then_inc(ahead, DMA)
                sp.dma_start(w_dn_all[:, e, :], w_down[SHARED + e]).then_inc(ahead, DMA)
            sp.wait_ge(ahead, 2 * EXPERTS * DMA)

        @block.scalar
        def _(act):
            prime(act, silued, by=2)

            def high_weights(p, e, load):
                act.wait_ge(w_in[p], load * (LOADS * DMA))
                act.wait_ge(downed, e * (CHUNKS * TILES) + 1)
                nc.scalar.activation(gu_hi[p][:], w_gu[:], ACT.Copy)
                nc.scalar.activation(dn_hi[p][:], w_dn[:], ACT.Copy).then_inc(w_high, 1)

            def pair_of_parts(i, final=False):
                for p in range(2):
                    e = i * 2 + p
                    for n in range(CHUNKS):
                        j = n % 2
                        u = e * CHUNKS + n
                        act.wait_ge(gated, u + 1)
                        act.wait_ge(acted, u + 1)
                        nc.scalar.activation(gate[j][:], gate_ps[j][:], ACT.Silu).then_inc(silued, 1)
                        act.wait_ge(acted, u + 3)
                        act.wait_ge(downed, u * TILES + (CHUNKS - 1) * TILES + 1)
                        nc.scalar.activation(act_hi[j][:], act_f[:], ACT.Copy).then_inc(act_high, 1)
                        if n == 1 and not (final and p == 1):
                            high_weights(1 - p, e + 1, i + 1)

            with act.Fori(0, SHARED // 2 - 1) as i:
                pair_of_parts(i)
            pair_of_parts(SHARED // 2 - 1, final=True)

        @block.gpsimd
        def _(pool):
            for e in range(1, SHARED):
                pool.wait_ge(w_high, e)
                nc.gpsimd.tensor_tensor(gu_lo[e % 2][:], w_gu[:], gu_hi[e % 2][:], ALU.subtract)
                nc.gpsimd.tensor_tensor(dn_lo[e % 2][:], w_dn[:], dn_hi[e % 2][:], ALU.subtract).then_inc(w_split, 1)

        @block.vector
        def _(dve):
            prime(dve, acted, by=2)
            prime(dve, added, by=TILES)
            with dve.Fori(0, SHARED // 2) as i:
                for p in range(2):
                    for n in range(CHUNKS):
                        j = n % 2
                        u = (i * 2 + p) * CHUNKS + n
                        dve.wait_ge(upped, u + 1)
                        dve.wait_ge(silued, u + 3)
                        nc.vector.tensor_tensor(act_f[:], up_ps[j][:], gate[j][:], ALU.mult).then_inc(acted, 1)
                        dve.wait_ge(act_high, u + 1)
                        nc.vector.tensor_tensor(act_lo[j][:], act_f[:], act_hi[j][:], ALU.subtract).then_inc(act_split, 1)
                        for t in range(TILES):
                            row = rows[:, n * TILES + t, :]
                            dve.wait_ge(downed, u * TILES + t + 2 + CHUNKS * TILES)
                            nc.vector.tensor_tensor(row, row, y_ps[t][:], ALU.add).then_inc(added, 1)
            dve.wait_ge(added, SHARED * CHUNKS * TILES + TILES)

        @block.tensor
        def _(pe):
            prime(pe, downed, by=CHUNKS * TILES + 1)

            def gate_and_up(p, e, n, split=None):
                j = n % 2
                u = e * CHUNKS + n
                if n == 0 and split is not None:
                    pe.wait_ge(w_split, split)
                cols = slice(n * CHUNK, (n + 1) * CHUNK)
                for bank, first, done in ((gate_ps[j], 0, gated), (up_ps[j], INTER, upped)):
                    if done is gated:
                        pe.wait_ge(silued, u + 1)
                    else:
                        pe.wait_ge(acted, u + 1)
                    terms = [(k, a, b) for k in range(KC) for a, b in
                             ((gu_hi[p], t_hi), (gu_hi[p], t_lo), (gu_lo[p], t_hi))]
                    for m, (k, a, b) in enumerate(terms):
                        last = nc.tensor.matmul(bank[:], a[:, k, first:first + INTER], b[:, k, cols], start=m == 0,
                                                stop=m == len(terms) - 1)
                    last.then_inc(done, 1)

            def down(p, e, n):
                j = n % 2
                u = e * CHUNKS + n
                pe.wait_ge(act_split, u + 1)
                for t in range(TILES):
                    pe.wait_ge(added, u * TILES + t + 1)
                    terms = ((act_hi[j], dn_hi[p]), (act_hi[j], dn_lo[p]), (act_lo[j], dn_hi[p]))
                    for m, (a, b) in enumerate(terms):
                        last = nc.tensor.matmul(y_ps[t][:], a[:, t * P:(t + 1) * P], b[:], start=m == 0, stop=m == 2)
                    last.then_inc(downed, 1)

            def pair_of_parts(i, final=False):
                for p in range(2):
                    e = i * 2 + p
                    for n in range(CHUNKS):
                        if n + 1 < CHUNKS:
                            gate_and_up(p, e, n + 1)
                        elif not (final and p == 1):
                            gate_and_up(1 - p, e + 1, 0, split=e + 1)
                        down(p, e, n)

            gate_and_up(0, 0, 0)
            with pe.Fori(0, SHARED // 2 - 1) as i:
                pair_of_parts(i)
            pair_of_parts(SHARED // 2 - 1, final=True)


def route(nc, logits, slots, weights, table, owner, w_gate_up, w_down, part_weights):
    with ExitStack() as c:
        T = TOKENS // P
        TE = [P, T, EXPERTS]
        sb = lambda n, s, d=F32: c.enter_context(nc.sbuf_tensor(f"ro_{n}", s, d))
        sem = lambda n: c.enter_context(nc.semaphore(f"ro_{n}"))
        order, eq, cand, first, second, place = [sb(n, TE) for n in ("order", "eq", "cand", "first", "second", "place")]
        mask = sb("mask", TE, BF16)
        top, pick, low_top, total, inv_total = [sb(n, [P, T]) for n in ("top", "pick", "low_top", "total", "inv_total")]
        earlier, every = sb("earlier", [P, P], BF16), sb("every", [P, P], BF16)
        limits = sb("limits", [P, EXPERTS, T])
        before = sb("before", [P, EXPERTS, EXPERTS])
        over, shift = sb("over", [P, EXPERTS, T]), sb("shift", [P, EXPERTS, EXPERTS])
        tiles, start, end, base = [sb(n, [P, EXPERTS]) for n in ("tiles", "start", "end", "base")]
        tile_no = sb("tile_no", [P, SLOT_TILES, EXPERTS])
        past = sb("past", [P, SLOT_TILES, EXPERTS])
        owner_f = sb("owner_f", [P, SLOT_TILES])
        slot_f, tile_f, lane_f = [sb(n, [P, 2 * T]) for n in ("slot_f", "tile_f", "lane_f")]
        tile_i = sb("tile_i", [P, 2 * T], I32)
        lane_no, slot_tile = sb("lane_no", [P, 1, P]), sb("slot_tile", [P, 1, SLOT_TILES])
        token, token_tile = sb("token", [P, 1]), sb("token_tile", [P, 2, T])
        in_lane = sb("in_lane", [P, 2 * T, P], BF16)
        in_tile = sb("in_tile", [P, 2 * T, SLOT_TILES])
        by_token = sb("by_token", [P, 2 * T, 2, SLOT_TILES], BF16)
        high_id = sb("high_id", [P, SLOT_TILES])
        rank_ps = c.enter_context(nc.psum_tensor("ro_rank_ps", [P, T, EXPERTS], F32))
        count_ps = c.enter_context(nc.psum_tensor("ro_count_ps", [P, EXPERTS], F32))
        table_ps = c.enter_context(nc.psum_tensor("ro_table_ps", [P, 2, SLOT_TILES], F32))
        w_gu, w_dn, gu_hi, gu_lo, dn_hi, dn_lo = part_weights
        w_in, w_high, w_split = sem("w_in"), sem("w_high"), sem("w_split")
        CONSTANTS = 12
        made, lowered, exped, chosen = sem("made"), sem("lowered"), sem("exped"), sem("chosen")
        masked, ranked, spread, tabled = sem("masked"), sem("ranked"), sem("spread"), sem("tabled")
        block = c.enter_context(nc.Block())

        @block.sync
        def _(sp):
            load_part(sp, 0, w_gate_up, w_down, w_gu, w_dn, w_in)

        @block.gpsimd
        def _(pool):
            count = 0

            def make(made_by):
                nonlocal count
                count += 1
                made_by.then_inc(made, 1)
                pool.wait_ge(made, count)

            def count_up(tile, pattern, base=0, lanes=0):
                make(nc.gpsimd.iota(tile[:], pattern=pattern, base=base, channel_multiplier=lanes,
                                    allow_small_or_imprecise_dtypes=True))

            count_up(order, [[0, T], [-1, EXPERTS]], base=EXPERTS)
            for ones in (every, earlier, before):
                make(nc.gpsimd.memset(ones[:], 1.0))
            make(nc.gpsimd.affine_select(out=earlier[:], in_=earlier[:], compare_op=ALU.is_ge, fill=0.0, base=-1,
                                         pattern=[[1, P]], channel_multiplier=-1))
            make(nc.gpsimd.affine_select(out=before[:], in_=before[:], compare_op=ALU.is_ge, fill=0.0, base=-1,
                                         pattern=[[1, EXPERTS], [-1, EXPERTS]], channel_multiplier=0))
            count_up(limits, [[0, EXPERTS], [P, T]])
            count_up(tile_no, [[1, SLOT_TILES], [0, EXPERTS]])
            count_up(lane_no, [[0, 1], [1, P]])
            count_up(slot_tile, [[0, 1], [1, SLOT_TILES]])
            count_up(token, [[0, 1]], lanes=1)
            count_up(token_tile, [[0, 2], [1, T]])
            pool.wait_ge(w_high, 1)
            nc.gpsimd.tensor_tensor(gu_lo[0][:], w_gu[:], gu_hi[0][:], ALU.subtract).then_inc(w_split, 1)
            nc.gpsimd.tensor_tensor(dn_lo[0][:], w_dn[:], dn_hi[0][:], ALU.subtract).then_inc(w_split, 1)
            pool.wait_ge(w_split, 2)

        @block.scalar
        def _(act):
            act.wait_ge(lowered, 1)
            nc.scalar.activation(logits[:], logits[:], ACT.Exp).then_inc(exped, 1)
            act.wait_ge(w_in, 2 * DMA)
            nc.scalar.activation(gu_hi[0][:], w_gu[:], ACT.Copy)
            nc.scalar.activation(dn_hi[0][:], w_dn[:], ACT.Copy).then_inc(w_high, 1)

        @block.vector
        def _(dve):
            done = 0

            def step(made_by):
                nonlocal done
                done += 1
                made_by.then_inc(chosen, 1)
                dve.wait_ge(chosen, done)

            tt, reduce = nc.vector.tensor_tensor, nc.vector.tensor_reduce
            wide = lambda v, shape=TE: v.unsqueeze(2).to_broadcast(shape)
            tall = lambda v, shape=TE: v.unsqueeze(1).to_broadcast(shape)

            def pick_largest(value, best, hot):
                step(reduce(best[:], value[:], AX.X, ALU.max))
                step(tt(eq[:], value[:], wide(best[:]), ALU.is_equal))
                step(tt(cand[:], eq[:], order[:], ALU.mult))
                step(reduce(pick[:], cand[:], AX.X, ALU.max))
                step(tt(hot[:], cand[:], wide(pick[:]), ALU.is_equal))

            dve.wait_ge(made, 1)
            step(reduce(top[:], logits[:], AX.X, ALU.max))
            tt(logits[:], logits[:], wide(top[:]), ALU.subtract).then_inc(lowered, 1)
            dve.wait_ge(exped, 1)
            pick_largest(logits, top, first)
            step(nc.vector.tensor_scalar(eq[:], first[:], 2.0, None, ALU.mult))
            step(tt(logits[:], logits[:], eq[:], ALU.subtract))
            pick_largest(logits, low_top, second)
            tt(mask[:], first[:], second[:], ALU.add).then_inc(masked, 1)
            step(tt(total[:], top[:], low_top[:], ALU.add))
            step(nc.vector.reciprocal(inv_total[:], total[:]))
            step(tt(weights[:, 0, :], top[:], inv_total[:], ALU.mult))
            step(tt(weights[:, 1, :], low_top[:], inv_total[:], ALU.mult))
            dve.wait_ge(ranked, 2)
            dve.wait_ge(made, CONSTANTS)
            step(tt(over[:], wide(count_ps[:], over.shape), limits[:], ALU.is_gt))
            step(reduce(tiles[:], over[:], AX.X, ALU.add))
            step(tt(shift[:], tall(tiles[:], shift.shape), before[:], ALU.mult))
            step(reduce(start[:], shift[:], AX.X, ALU.add))
            step(nc.vector.tensor_scalar(base[:], start[:], float(P), None, ALU.mult))
            step(tt(place[:], rank_ps[:], tall(base[:]), ALU.add))
            for choice, hot in enumerate((first, second)):
                step(tt(cand[:], hot[:], place[:], ALU.mult))
                step(reduce(slot_f[:, choice * T:(choice + 1) * T], cand[:], AX.X, ALU.add))
            step(nc.vector.tensor_copy(slots[:], slot_f[:]))
            step(nc.vector.tensor_scalar(tile_i[:], slots[:], 7, None, ALU.arith_shift_right))
            step(nc.vector.tensor_copy(tile_f[:], tile_i[:]))
            step(nc.vector.tensor_scalar(lane_f[:], tile_f[:], float(-P), None, ALU.mult))
            step(tt(lane_f[:], lane_f[:], slot_f[:], ALU.add))
            step(tt(in_tile[:], tall(slot_tile[:, 0, :], in_tile.shape), wide(tile_f[:], in_tile.shape), ALU.is_equal))
            step(tt(in_lane[:], tall(lane_no[:, 0, :], in_lane.shape), wide(lane_f[:], in_lane.shape), ALU.is_equal))
            step(nc.vector.tensor_scalar(by_token[:, :, 0, :], in_tile[:], token[:, 0:1], None, ALU.mult))
            tt(by_token[:, :, 1, :], in_tile[:], wide(token_tile[:].rearrange("p c t -> p (c t)"), in_tile.shape), ALU.mult
               ).then_inc(spread, 1)
            step(tt(end[:], start[:], tiles[:], ALU.add))
            step(tt(past[:], tile_no[:], tall(end[:], past.shape), ALU.is_ge))
            step(reduce(owner_f[:], past[:], AX.X, ALU.add))
            step(nc.vector.tensor_scalar(owner_f[:], owner_f[:], float(EXPERTS - 1), None, ALU.min))
            step(nc.vector.tensor_copy(owner[:], owner_f[:]))
            dve.wait_ge(tabled, 1)
            step(nc.vector.tensor_scalar(high_id[:], table_ps[:, 1, :], float(P), None, ALU.mult))
            step(tt(high_id[:], high_id[:], table_ps[:, 0, :], ALU.add))
            step(nc.vector.tensor_copy(table[:], high_id[:]))

        @block.tensor
        def _(pe):
            pe.wait_ge(made, 5)
            pe.wait_ge(masked, 1)
            nc.tensor.matmul(rank_ps[:].rearrange("p t e -> p (t e)"), earlier[:], mask[:].rearrange("p t e -> p (t e)"),
                             start=True, stop=False)
            for back in range(1, T):
                last = nc.tensor.matmul(rank_ps[:, back:, :].rearrange("p t e -> p (t e)"), every[:],
                                        mask[:, 0:T - back, :].rearrange("p t e -> p (t e)"), start=False,
                                        stop=back == T - 1)
            last.then_inc(ranked, 1)
            for t in range(T):
                last = nc.tensor.matmul(count_ps[:], every[:], mask[:, t, :], start=t == 0, stop=t == T - 1)
            last.then_inc(ranked, 1)
            pe.wait_ge(spread, 1)
            for t in range(2 * T):
                last = nc.tensor.matmul(table_ps[:].rearrange("p a n -> p (a n)"), in_lane[:, t, :],
                                        by_token[:, t].rearrange("p a n -> p (a n)"), start=t == 0, stop=t == 2 * T - 1)
            last.then_inc(tabled, 1)


def experts(nc, w_gate_up, w_first, w_dn, ident, x_s, y_s, rows, slots, weights, table, owner, out):
    with ExitStack() as c:
        T = TOKENS // P
        DEPTH = 4
        BATCH_T = 4
        sb = lambda n, s, d=F32: c.enter_context(nc.sbuf_tensor(f"ex_{n}", s, d))
        sem = lambda n: c.enter_context(nc.semaphore(f"ex_{n}"))
        ps = lambda n, w: c.enter_context(nc.psum_tensor(f"ex_{n}", [P, w], F32))
        w_rest = sb("w_rest", [P, EXPERTS, KC - AHEAD_K, 2 * INTER])
        x_g = [sb(f"x_g{j}", [P, DIM]) for j in range(DEPTH)]
        x_t = [sb(f"x_t{j}", [P, KC, P]) for j in range(2)]
        gate = [sb(f"gate{j}", [P, INTER]) for j in range(2)]
        acts = [sb(f"acts{j}", [P, INTER]) for j in range(2)]
        acts_t = [sb(f"acts_t{j}", [P, P]) for j in range(2)]
        y = [sb(f"y{j}", [P, DIM]) for j in range(DEPTH)]
        y_g = [sb(f"y_g{j}", [P, DIM]) for j in range(2 * DEPTH)]
        eps = sb("eps", [P, 1])
        stats, moments = sb("stats", [P, T, 6]), sb("moments", [P, T, 2])
        spread, scale, offset = sb("spread", [P, T]), sb("scale", [P, T]), sb("offset", [P, T])
        x_ps = [ps(f"x_ps{j}", DIM) for j in range(2)]
        gu_ps = [ps(f"gu_ps{j}", CHUNK) for j in range(2)]
        t_ps = [ps(f"t_ps{j}", CHUNK) for j in range(2)]
        y_ps = [ps(f"y_ps{j}", DIM) for j in range(2)]
        w_in = sem("w_in")
        gathered = [sem(f"gathered{j}") for j in range(DEPTH)]
        stored = [sem(f"stored{j}") for j in range(DEPTH)]
        turned, kept, gated, silued, acted = [sem(n) for n in ("turned", "kept", "gated", "silued", "acted")]
        act_turned, act_kept, downed, y_kept = [sem(n) for n in ("act_turned", "act_kept", "downed", "y_kept")]
        returned = [sem(f"returned{j}") for j in range(2 * DEPTH)]
        summed, eps_made, counted, averaged, rooted, scaled, normed = [
            sem(n) for n in ("summed", "eps_made", "counted", "averaged", "rooted", "scaled", "normed")]
        finished = sem("finished")
        block = c.enter_context(nc.Block())

        @block.sync
        def _(sp):
            prime(sp, *stored)
            for e in range(EXPERTS):
                sp.dma_start(w_rest[:, e], w_gate_up[SHARED + e, AHEAD_K * P:DIM, :].rearrange("(k p) n -> p k n", p=P)).then_inc(w_in, DMA)
            with sp.Fori(0, SLOT_TILES // DEPTH) as i:
                for j in range(DEPTH):
                    tile = i * DEPTH + j
                    sp.wait_ge(y_kept, tile + 3)
                    sp.dma_start(y_s[bass.ds(tile * P, P), :], y[j][:]).then_inc(stored[j], DMA)
            for t in range(T):
                sp.wait_ge(normed, t + 1)
                sp.dma_start(out[t * P:(t + 1) * P, :], rows[:, t, :]).then_inc(finished, DMA)
            sp.wait_ge(finished, T * DMA)

        @block.gpsimd
        def _(pool):
            nc.gpsimd.memset(eps[:], 1e-5).then_inc(eps_made, 1)
            for tile in range(SLOT_TILES):
                if tile >= DEPTH:
                    pool.wait_ge(turned, tile - DEPTH + 1)
                nc.gpsimd.indirect_dma_start(x_g[tile % DEPTH][:], None, x_s[:], bass.IndirectOffsetOnAxis(
                    ap=table[:, tile:tile + 1], axis=0)).then_inc(gathered[tile % DEPTH], DMA)
            for j in range(DEPTH):
                pool.wait_ge(stored[j], SLOT_TILES // DEPTH * DMA + 1)
            for t in range(T):
                for choice in range(2):
                    n = 2 * t + choice
                    if n >= 2 * DEPTH:
                        pool.wait_ge(summed, n - 2 * DEPTH + 1)
                    at = choice * T + t
                    nc.gpsimd.indirect_dma_start(y_g[n % (2 * DEPTH)][:], None, y_s[:], bass.IndirectOffsetOnAxis(
                        ap=slots[:, at:at + 1], axis=0)).then_inc(returned[n % (2 * DEPTH)], DMA)

        @block.scalar
        def _(act):
            prime(act, kept, by=2)
            with act.Fori(0, SLOT_TILES // DEPTH) as i:
                for j in range(DEPTH):
                    tile = i * DEPTH + j
                    b = j % 2
                    act.wait_ge(turned, tile + 1)
                    act.wait_ge(gated, tile + 1)
                    nc.scalar.activation(x_t[b][:], x_ps[b][:].rearrange("p (k t) -> p k t", k=KC), ACT.Copy).then_inc(kept, 1)
                    act.wait_ge(gated, tile + 3)
                    act.wait_ge(acted, tile + 1)
                    nc.scalar.activation(gate[b][:], gu_ps[b][:, 0:INTER], ACT.Silu).then_inc(silued, 1)
            act.wait_ge(eps_made, 1)
            for t0 in range(0, T, BATCH_T):
                act.wait_ge(averaged, t0 + BATCH_T)
                nc.scalar.activation(spread[:, t0:t0 + BATCH_T], moments[:, t0:t0 + BATCH_T, 1], ACT.Sqrt,
                                     bias=eps[:, 0:1]).then_inc(rooted, 1)
                act.wait_ge(scaled, t0 // BATCH_T * 2 + 2)
                for t in range(t0, t0 + BATCH_T):
                    nc.scalar.activation(rows[:, t, :], rows[:, t, :], ACT.Identity, bias=offset[:, t:t + 1],
                                         scale=scale[:, t:t + 1]).then_inc(normed, 1)

        @block.vector
        def _(dve):
            prime(dve, acted, y_kept, act_kept, by=2)

            def keep_result(j, tile, i):
                dve.wait_ge(downed, tile + 3)
                dve.wait_ge(stored[j], i * DMA + 1)
                nc.vector.tensor_copy(y[j][:], y_ps[j % 2][:]).then_inc(y_kept, 1)

            def activate(j, tile, i=None):
                b = j % 2
                dve.wait_ge(silued, tile + 1)
                dve.wait_ge(act_turned, tile + 1)
                nc.vector.tensor_tensor(acts[b][:], gu_ps[b][:, INTER:2 * INTER], gate[b][:], ALU.mult).then_inc(acted, 1)
                if i is not None:
                    keep_result((j - 1) % DEPTH, tile - 1, i)
                dve.wait_ge(act_turned, tile + 3)
                dve.wait_ge(downed, tile + 1)
                nc.vector.tensor_copy(acts_t[b][:], t_ps[b][:, 0:P]).then_inc(act_kept, 1)

            activate(0, 0)
            with dve.Fori(0, SLOT_TILES // DEPTH - 1) as i:
                for j in range(1, DEPTH + 1):
                    activate(j % DEPTH, i * DEPTH + j, i)
            for j in range(1, DEPTH):
                activate(j, SLOT_TILES - DEPTH + j, SLOT_TILES // DEPTH - 1)
            keep_result(DEPTH - 1, SLOT_TILES - 1, SLOT_TILES // DEPTH - 1)

            def scale_and_offset(t0):
                dve.wait_ge(rooted, t0 // BATCH_T + 1)
                nc.vector.reciprocal(scale[:, t0:t0 + BATCH_T], spread[:, t0:t0 + BATCH_T]).then_inc(scaled, 1)
                dve.wait_ge(scaled, t0 // BATCH_T * 2 + 1)
                nc.vector.scalar_tensor_tensor(offset[:, t0:t0 + BATCH_T], moments[:, t0:t0 + BATCH_T, 0], -1.0,
                                               scale[:, t0:t0 + BATCH_T], ALU.mult, ALU.mult).then_inc(scaled, 1)

            for t0 in range(0, T, BATCH_T):
                for t in range(t0, t0 + BATCH_T):
                    for choice in range(2):
                        n = 2 * t + choice
                        dve.wait_ge(returned[n % (2 * DEPTH)], (n // (2 * DEPTH) + 1) * DMA)
                        if choice:
                            dve.wait_ge(summed, n)
                        nc.vector.scalar_tensor_tensor(rows[:, t, :], y_g[n % (2 * DEPTH)][:], weights[:, choice, t:t + 1],
                                                       rows[:, t, :], ALU.mult, ALU.add).then_inc(summed, 1)
                    dve.wait_ge(summed, 2 * t + 2)
                    nc.vector.bn_stats(stats[:, t, :], rows[:, t, :]).then_inc(counted, 1)
                for t in range(t0, t0 + BATCH_T):
                    dve.wait_ge(counted, t + 1)
                    nc.vector.bn_aggr(moments[:, t, :], stats[:, t, :]).then_inc(averaged, 1)
                scale_and_offset(t0)

        @block.tensor
        def _(pe):
            prime(pe, gated, act_turned, downed, by=2)

            def turn(j, tile, i):
                pe.wait_ge(gathered[j], (i + 1) * DMA)
                pe.wait_ge(kept, tile + 1)
                for k in range(KC):
                    last = nc.tensor.transpose(x_ps[j % 2][:, k * P:(k + 1) * P], x_g[j][:, k * P:(k + 1) * P], ident[:])
                last.then_inc(turned, 1)

            def turn_acts(b, tile):
                pe.wait_ge(acted, tile + 3)
                pe.wait_ge(act_kept, tile + 1)
                nc.tensor.transpose(t_ps[b][:, 0:P], acts[b][:], ident[:]).then_inc(act_turned, 1)

            def gate_and_up(b, tile, e):
                pe.wait_ge(kept, tile + 3)
                pe.wait_ge(acted, tile + 1)
                for k in range(KC):
                    w = (w_first[:, bass.ds(e, 1), k, :] if k < AHEAD_K else w_rest[:, bass.ds(e, 1), k - AHEAD_K, :])
                    last = nc.tensor.matmul(gu_ps[b][:, 0:2 * INTER], x_t[b][:, k, :], w.rearrange("p e n -> p (e n)"),
                                            start=k == 0, stop=k == KC - 1)
                last.then_inc(gated, 1)

            def down(b, tile, e):
                pe.wait_ge(act_kept, tile + 3)
                pe.wait_ge(y_kept, tile + 1)
                nc.tensor.matmul(y_ps[b][:], acts_t[b][:], w_dn[:, bass.ds(e, 1), :].rearrange("p e n -> p (e n)"),
                                 start=True, stop=True).then_inc(downed, 1)

            def owner_of(tile):
                return pe.value_load(owner[0:1, bass.ds(tile, 1)], min_val=0, max_val=EXPERTS - 1)

            def tile_after(j, tile, i):
                mine, last = owner_of(tile), owner_of(tile - 1)
                if i is not None:
                    turn((j + 1) % DEPTH, tile + 1, i)
                turn_acts(1 - j % 2, tile - 1)
                gate_and_up(j % 2, tile, mine)
                down(1 - j % 2, tile - 1, last)

            turn(0, 0, 0)
            turn(1, 1, 0)
            pe.wait_ge(w_in, EXPERTS * DMA)
            gate_and_up(0, 0, owner_of(0))
            with pe.Fori(0, SLOT_TILES // DEPTH - 1) as i:
                for j in range(1, DEPTH + 1):
                    tile_after(j % DEPTH, i * DEPTH + j, i + (j + 1) // DEPTH)
            last = SLOT_TILES - DEPTH
            for j in range(1, DEPTH):
                tile_after(j, last + j, last // DEPTH if j + 1 < DEPTH else None)
            turn_acts(1, SLOT_TILES - 1)
            down(1, SLOT_TILES - 1, owner_of(SLOT_TILES - 1))


def layer(nc, ins, out):
    with ExitStack() as c:
        dram = lambda n, *s: nc.dram_tensor(n, s, F32).ap()
        q_s, k_s = dram("q_scratch", HEADS, 2, HEAD, TOKENS), dram("k_scratch", KV_HEADS, 2, HEAD, TOKENS)
        m_s = dram("m_scratch", HEADS, 2, TOKENS)
        o_s, d_s, r_s = dram("o_scratch", HEADS, HEAD, TOKENS), dram("d_scratch", HEADS, TOKENS), dram("r_scratch", HEADS, TOKENS)
        x_s, y_s = dram("x_scratch", TOKENS, DIM), dram("y_scratch", SLOT_TILES * P, DIM)
        sb = lambda n, s, d=F32: c.enter_context(nc.sbuf_tensor(n, s, d))
        ident = sb("ident", [P, P])
        bound, loose = sb("bound", [P, 1]), sb("loose", [1, 1], I32)
        with nc.sbuf_tensor("values", [P, TOKENS // P, P], F32) as values:
            project_qkv(nc, ins["x_t"], ins["w_qkv"], ins["cos"], ins["sin"], ins["ident"], q_s, k_s, m_s, values, ident,
                        bound, loose)
            exact_maxima(nc, q_s, k_s, m_s, ident, bound, loose)
            attend(nc, q_s, k_s, m_s, values, bound, o_s, d_s)
        rows = sb("rows", [P, TOKENS // P, DIM])
        logits = sb("logits", [P, TOKENS // P, EXPERTS])
        slots = sb("slots", [P, 2 * TOKENS // P], I32)
        weights = sb("weights", [P, 2, TOKENS // P])
        table = sb("table", [P, SLOT_TILES], I32)
        owner = sb("owner", [P, SLOT_TILES], I32)
        with ExitStack() as until_shared:
            scoped = lambda n, s, d: until_shared.enter_context(nc.sbuf_tensor(n, s, d))
            t_hi, t_lo = scoped("t_hi", [P, KC, TOKENS], F32R), scoped("t_lo", [P, KC, TOKENS], F32R)
            project_out(nc, ins["x"], ins["w_o"], ins["w_gate"], ident, o_s, d_s, r_s, x_s, rows, t_hi, t_lo, logits)
            pair = lambda n, shape, d: [scoped(f"{n}{p}", shape, d) for p in range(2)]
            gu, dn = [P, KC, 2 * INTER], [P, DIM]
            part_weights = (scoped("part_gu", gu, F32), scoped("part_dn", dn, F32), pair("part_gu_hi", gu, F32R),
                            pair("part_gu_lo", gu, F32R), pair("part_dn_hi", dn, F32R), pair("part_dn_lo", dn, F32R))
            route(nc, logits, slots, weights, table, owner, ins["w_gate_up"], ins["w_down"], part_weights)
            w_first = c.enter_context(nc.sbuf_tensor("w_first", [P, EXPERTS, AHEAD_K, 2 * INTER], F32, side="right"))
            w_dn = c.enter_context(nc.sbuf_tensor("w_dn_all", [P, EXPERTS, DIM], F32, side="right"))
            shared_expert(nc, ins["w_gate_up"], ins["w_down"], part_weights, rows, t_hi, t_lo, w_first, w_dn)
        experts(nc, ins["w_gate_up"], w_first, w_dn, ident, x_s, y_s, rows, slots, weights, table, owner, out)


def arrange(a):
    import numpy as np
    f = lambda n: np.asarray(a[n])
    x = f("L0_attn_x").reshape(TOKENS, DIM)
    w_q = f("L0_attn_Wq").reshape(DIM, SETS, SET_HEADS * PAIRS, 2)
    w_k = f("L0_attn_Wk").reshape(DIM, KV_HEADS * PAIRS, 2)
    cols = [w_k[:, :, 0], w_k[:, :, 0], w_k[:, :, 1], w_k[:, :, 1]]
    for s in range(SETS):
        cols += [w_q[:, s, :, 0], w_q[:, s, :, 1]]
    cols.append(f("L0_attn_Wv"))
    inv_freq = (1.0 / np.float32(10000.0) ** (np.arange(0, HEAD, 2, dtype=np.float32) / np.float32(HEAD))).astype(np.float32)
    ang = np.arange(SEQ, dtype=np.float32)[None, :] * np.tile(inv_freq, SET_HEADS)[:, None]
    gate = np.zeros((DIM, P), np.float32)
    gate[:, :EXPERTS] = f("L0_ffn_gate_w").T
    shared = f("L0_ffn_shared_w_gate_up").reshape(2, SHARED, INTER, DIM).transpose(1, 3, 0, 2).reshape(SHARED, DIM, 2 * INTER)
    shared_down = f("L0_ffn_shared_w_down").reshape(DIM, SHARED, INTER).transpose(1, 2, 0)
    t = np.ascontiguousarray
    return {
        "x": t(x), "x_t": t(x.T), "w_qkv": np.concatenate(cols, axis=1),
        "cos": np.cos(ang).astype(np.float32), "sin": np.sin(ang).astype(np.float32),
        "ident": np.eye(P, dtype=np.float32),
        "w_o": t(f("L0_attn_Wo")), "w_gate": gate,
        "w_gate_up": np.concatenate([shared, f("L0_ffn_w_gate_up").transpose(0, 2, 1)]),
        "w_down": np.concatenate([shared_down, f("L0_ffn_w_down").transpose(0, 2, 1)]),
    }


def kernel(**inputs):
    import concourse.bacc as bacc
    from concourse.bass_utils import run_bass_kernel_spmd as run

    nc = bacc.Bacc("TRN2", target_bir_lowering=False, num_devices=1)
    arrays = arrange(inputs)
    ins = {n: nc.dram_tensor(f"in_{n}", v.shape, mybir.dt.from_np(v.dtype), kind="ExternalInput").ap() for n, v in arrays.items()}
    out = nc.dram_tensor("out", (TOKENS, DIM), F32, kind="ExternalOutput").ap()
    layer(nc, ins, out)
    r = run(nc, [{f"in_{n}": v for n, v in arrays.items()}], core_ids=[0])
    return r.results[0]["out"].reshape(BATCH, SEQ, DIM)
```
